# Optimizing a Trainium2 kernel written in Bass

```python
import numpy as np
import jax
import jax.numpy as jnp

def _softmax(x, axis=-1):
    return jax.nn.softmax(x, axis=axis)

def _gelu(x):
    return jax.nn.gelu(x, approximate=True)

def _silu(x):
    return jax.nn.silu(x)

def _sigmoid(x):
    return jax.nn.sigmoid(x)

def _layernorm(x, axis=-1, eps=1e-05):
    m = jnp.mean(x, axis=axis, keepdims=True)
    v = jnp.var(x, axis=axis, keepdims=True)
    return (x - m) / jnp.sqrt(v + eps)

def _scatter_add(tgt, idx, src, axis=0):
    return tgt.at[idx].add(src)

def _segment_sum(src, seg, n):
    return jax.ops.segment_sum(src, seg, n)
kernel_name = 'mk_sandwich_d1_jaxref_r8_ee9091'

def setup_inputs(seed: int=0):
    np.random.seed(seed)
    _w = jnp.asarray

    def _L0_attn_setup():
        import jax, jax.numpy as jnp
        import numpy as np
        B, S, HID = (2, 256, 256)
        NK, NV, DK, DV = (16, 32, 128, 128)
        KCONV, CHUNK, EPS = (4, 64, 1e-06)
        KEY_DIM = NK * DK
        VAL_DIM = NV * DV
        CONV_DIM = 2 * KEY_DIM + VAL_DIM

        def _forward(x, W_qkv, W_z, W_b, W_a, W_out, conv_w, dt_bias, A_log, norm_w):
            Bs, Ss, _ = x.shape
            mixed = jnp.einsum('bsh,ch->bsc', x, W_qkv)
            z = jnp.einsum('bsh,vh->bsv', x, W_z)
            b = jnp.einsum('bsh,nh->bsn', x, W_b)
            a = jnp.einsum('bsh,nh->bsn', x, W_a)
            xp = jnp.pad(mixed, ((0, 0), (KCONV - 1, 0), (0, 0)))
            conv = sum((xp[:, k:k + Ss, :] * conv_w[:, k] for k in range(KCONV)))
            mixed = jax.nn.silu(conv)
            q, k, v = jnp.split(mixed, [KEY_DIM, 2 * KEY_DIM], axis=-1)
            q = q.reshape(Bs, Ss, NK, DK)
            k = k.reshape(Bs, Ss, NK, DK)
            v = v.reshape(Bs, Ss, NV, DV)
            rep = NV // NK
            q = jnp.repeat(q, rep, axis=2)
            k = jnp.repeat(k, rep, axis=2)
            beta = jax.nn.sigmoid(b)
            g = -jnp.exp(A_log) * jax.nn.softplus(a + dt_bias)
            l2n = lambda t: t / jnp.maximum(jnp.linalg.norm(t, axis=-1, keepdims=True), 1e-12)
            q, k = (l2n(q), l2n(k))
            qT = jnp.swapaxes(q, 1, 2) * DK ** (-0.5)
            kT = jnp.swapaxes(k, 1, 2)
            vT = jnp.swapaxes(v, 1, 2)
            bT = jnp.swapaxes(beta, 1, 2)
            gT = jnp.swapaxes(g, 1, 2)
            N = Ss // CHUNK
            qc = qT.reshape(Bs, NV, N, CHUNK, DK)
            kc = kT.reshape(Bs, NV, N, CHUNK, DK)
            vc = vT.reshape(Bs, NV, N, CHUNK, DV)
            bc = bT.reshape(Bs, NV, N, CHUNK)
            gc = jnp.cumsum(gT.reshape(Bs, NV, N, CHUNK), axis=-1)
            v_beta = vc * bc[..., None]
            k_beta = kc * bc[..., None]
            tril = jnp.tril(jnp.ones((CHUNK, CHUNK), bool))
            strict = jnp.tril(jnp.ones((CHUNK, CHUNK), bool), -1)
            diff = gc[..., :, None] - gc[..., None, :]
            decay = jnp.exp(jnp.where(tril, diff, 0.0)) * tril
            A = -(jnp.einsum('bhnid,bhnjd->bhnij', k_beta, kc) * decay) * strict
            eye = jnp.eye(CHUNK, dtype=A.dtype)
            Tm = jax.scipy.linalg.solve_triangular(eye - A, jnp.broadcast_to(eye, A.shape), lower=True, unit_diagonal=True)
            u = jnp.einsum('bhnij,bhnjv->bhniv', Tm, v_beta)
            kcd = jnp.einsum('bhnij,bhnjd->bhnid', Tm, k_beta * jnp.exp(gc)[..., None])
            front = lambda t: jnp.moveaxis(t, 2, 0)
            xs = (front(qc), front(kc), front(u), front(kcd), front(decay), front(gc))
            S0 = jnp.zeros((Bs, NV, DK, DV), jnp.float32)

            def step(St, inp):
                q_i, k_i, u_i, kcd_i, dec_i, g_i = inp
                attn = jnp.einsum('bhid,bhjd->bhij', q_i, k_i) * dec_i
                v_new = u_i - jnp.einsum('bhid,bhdv->bhiv', kcd_i, St)
                inter = jnp.einsum('bhid,bhdv->bhiv', q_i * jnp.exp(g_i)[..., None], St)
                out_i = inter + jnp.einsum('bhij,bhjv->bhiv', attn, v_new)
                g_last = g_i[..., -1]
                St_new = St * jnp.exp(g_last)[..., None, None] + jnp.einsum('bhid,bhiv->bhdv', k_i * jnp.exp(g_last[..., None] - g_i)[..., None], v_new)
                return (St_new, out_i)
            _, outs = jax.lax.scan(step, S0, xs)
            core = jnp.moveaxis(outs, 0, 2).reshape(Bs, NV, Ss, DV)
            core = jnp.swapaxes(core, 1, 2)
            zr = z.reshape(Bs, Ss, NV, DV)
            var = jnp.mean(core * core, axis=-1, keepdims=True)
            normed = core * jax.lax.rsqrt(var + EPS) * norm_w * jax.nn.silu(zr)
            return jnp.einsum('bsv,hv->bsh', normed.reshape(Bs, Ss, VAL_DIM), W_out)
        key = jax.random.key(seed)
        ks = jax.random.split(key, 10)
        n = lambda k, shape, s: jax.random.normal(k, shape, jnp.float32) * s
        return {'x': n(ks[0], (B, S, HID), 1.0), 'W_qkv': n(ks[1], (CONV_DIM, HID), HID ** (-0.5)), 'W_z': n(ks[2], (VAL_DIM, HID), HID ** (-0.5)), 'W_b': n(ks[3], (NV, HID), HID ** (-0.5)), 'W_a': n(ks[4], (NV, HID), HID ** (-0.5)), 'W_out': n(ks[5], (HID, VAL_DIM), VAL_DIM ** (-0.5)), 'conv_w': n(ks[6], (CONV_DIM, KCONV), 0.5), 'dt_bias': n(ks[7], (NV,), 0.5), 'A_log': n(ks[8], (NV,), 0.5), 'norm_w': jnp.ones((DV,), jnp.float32)}
    _L0_attn_in = _L0_attn_setup()

    def _L0_ffn_setup():
        import jax, jax.numpy as jnp
        import numpy as np
        E, K, H, F = (64, 6, 256, 96)
        G, KG = (8, 4)
        SHARED_F = 96
        SCALE = 2.5
        T = 2 * 128
        CAP = 2 * (T * K // E)

        def _grouped_topk(logits, bias):
            scores = jax.nn.sigmoid(logits.astype(jnp.float32))
            scores_b = scores + bias[None, :]
            gs = scores_b.reshape(-1, G, E // G)
            group_scores = jnp.sum(jax.lax.top_k(gs, 2)[0], axis=-1)
            gidx = jax.lax.top_k(group_scores, KG)[1]
            rows = jnp.arange(group_scores.shape[0])[:, None]
            group_mask = jnp.zeros_like(group_scores).at[rows, gidx].set(1.0)
            score_mask = jnp.repeat(group_mask, E // G, axis=-1) > 0
            tmp = jnp.where(score_mask, scores_b, -jnp.inf)
            topk_ids = jax.lax.top_k(tmp, K)[1]
            topk_w = jnp.take_along_axis(scores, topk_ids, axis=-1)
            topk_w = topk_w / jnp.sum(topk_w, axis=-1, keepdims=True)
            return (topk_w * SCALE, topk_ids)

        def _routed_moe(x, topk_w, topk_ids, w_gate, w_up, w_down):
            Tn = x.shape[0]
            flat_e = topk_ids.reshape(-1)
            order = jnp.argsort(flat_e)
            se = flat_e[order]
            pos = jnp.arange(Tn * K) - jnp.searchsorted(se, se, side='left')
            tok = order // K
            valid = pos < CAP
            slot = jnp.where(valid, pos, CAP)
            buf = jnp.zeros((E, CAP + 1, H), x.dtype).at[se, slot].set(x[tok])[:, :CAP]
            h = jax.nn.silu(jnp.einsum('ech,ehf->ecf', buf, w_gate)) * jnp.einsum('ech,ehf->ecf', buf, w_up)
            out = jnp.einsum('ecf,efh->ech', h, w_down)
            gathered = out[se, jnp.minimum(pos, CAP - 1)] * valid.astype(x.dtype)[:, None]
            w = topk_w.reshape(-1)[order].astype(x.dtype)[:, None]
            return jax.ops.segment_sum(gathered * w, tok, num_segments=Tn)
        key = jax.random.key(seed)
        ks = jax.random.split(key, 9)
        s = 0.02
        return dict(hidden_states=jax.random.normal(ks[0], (2, 128, H), jnp.float32), gate_w=jax.random.normal(ks[1], (H, E), jnp.float32) * s, bias=jax.random.normal(ks[2], (E,), jnp.float32) * s, w_gate=jax.random.normal(ks[3], (E, H, F), jnp.float32) * s, w_up=jax.random.normal(ks[4], (E, H, F), jnp.float32) * s, w_down=jax.random.normal(ks[5], (E, F, H), jnp.float32) * s, ws_gate=jax.random.normal(ks[6], (H, SHARED_F), jnp.float32) * s, ws_up=jax.random.normal(ks[7], (H, SHARED_F), jnp.float32) * s, ws_down=jax.random.normal(ks[8], (SHARED_F, H), jnp.float32) * s)
    _L0_ffn_in = _L0_ffn_setup()
    _d = {'L0_attn_x': _L0_attn_in['x'], 'L0_attn_W_qkv': _L0_attn_in['W_qkv'], 'L0_attn_W_z': _L0_attn_in['W_z'], 'L0_attn_W_b': _L0_attn_in['W_b'], 'L0_attn_W_a': _L0_attn_in['W_a'], 'L0_attn_W_out': _L0_attn_in['W_out'], 'L0_attn_conv_w': _L0_attn_in['conv_w'], 'L0_attn_dt_bias': _L0_attn_in['dt_bias'], 'L0_attn_A_log': _L0_attn_in['A_log'], 'L0_attn_norm_w': _L0_attn_in['norm_w'], 'L0_ffn_gate_w': _L0_ffn_in['gate_w'], 'L0_ffn_bias': _L0_ffn_in['bias'], 'L0_ffn_w_gate': _L0_ffn_in['w_gate'], 'L0_ffn_w_up': _L0_ffn_in['w_up'], 'L0_ffn_w_down': _L0_ffn_in['w_down'], 'L0_ffn_ws_gate': _L0_ffn_in['ws_gate'], 'L0_ffn_ws_up': _L0_ffn_in['ws_up'], 'L0_ffn_ws_down': _L0_ffn_in['ws_down']}
    _x0 = _d['L0_attn_x']
    _d['L0_attn_x'] = jax.random.normal(jax.random.fold_in(jax.random.key(seed), 1), (2, 1024, 256), dtype=_x0.dtype)
    del _x0
    return _d

def reference(L0_attn_x, L0_attn_W_qkv, L0_attn_W_z, L0_attn_W_b, L0_attn_W_a, L0_attn_W_out, L0_attn_conv_w, L0_attn_dt_bias, L0_attn_A_log, L0_attn_norm_w, L0_ffn_gate_w, L0_ffn_bias, L0_ffn_w_gate, L0_ffn_w_up, L0_ffn_w_down, L0_ffn_ws_gate, L0_ffn_ws_up, L0_ffn_ws_down):

    def _L0_attn_ref(x, W_qkv, W_z, W_b, W_a, W_out, conv_w, dt_bias, A_log, norm_w):
        import jax, jax.numpy as jnp
        import numpy as np
        B, S, HID = (2, 256, 256)
        NK, NV, DK, DV = (16, 32, 128, 128)
        KCONV, CHUNK, EPS = (4, 64, 1e-06)
        KEY_DIM = NK * DK
        VAL_DIM = NV * DV
        CONV_DIM = 2 * KEY_DIM + VAL_DIM

        def _forward(x, W_qkv, W_z, W_b, W_a, W_out, conv_w, dt_bias, A_log, norm_w):
            Bs, Ss, _ = x.shape
            mixed = jnp.einsum('bsh,ch->bsc', x, W_qkv)
            z = jnp.einsum('bsh,vh->bsv', x, W_z)
            b = jnp.einsum('bsh,nh->bsn', x, W_b)
            a = jnp.einsum('bsh,nh->bsn', x, W_a)
            xp = jnp.pad(mixed, ((0, 0), (KCONV - 1, 0), (0, 0)))
            conv = sum((xp[:, k:k + Ss, :] * conv_w[:, k] for k in range(KCONV)))
            mixed = jax.nn.silu(conv)
            q, k, v = jnp.split(mixed, [KEY_DIM, 2 * KEY_DIM], axis=-1)
            q = q.reshape(Bs, Ss, NK, DK)
            k = k.reshape(Bs, Ss, NK, DK)
            v = v.reshape(Bs, Ss, NV, DV)
            rep = NV // NK
            q = jnp.repeat(q, rep, axis=2)
            k = jnp.repeat(k, rep, axis=2)
            beta = jax.nn.sigmoid(b)
            g = -jnp.exp(A_log) * jax.nn.softplus(a + dt_bias)
            l2n = lambda t: t / jnp.maximum(jnp.linalg.norm(t, axis=-1, keepdims=True), 1e-12)
            q, k = (l2n(q), l2n(k))
            qT = jnp.swapaxes(q, 1, 2) * DK ** (-0.5)
            kT = jnp.swapaxes(k, 1, 2)
            vT = jnp.swapaxes(v, 1, 2)
            bT = jnp.swapaxes(beta, 1, 2)
            gT = jnp.swapaxes(g, 1, 2)
            N = Ss // CHUNK
            qc = qT.reshape(Bs, NV, N, CHUNK, DK)
            kc = kT.reshape(Bs, NV, N, CHUNK, DK)
            vc = vT.reshape(Bs, NV, N, CHUNK, DV)
            bc = bT.reshape(Bs, NV, N, CHUNK)
            gc = jnp.cumsum(gT.reshape(Bs, NV, N, CHUNK), axis=-1)
            v_beta = vc * bc[..., None]
            k_beta = kc * bc[..., None]
            tril = jnp.tril(jnp.ones((CHUNK, CHUNK), bool))
            strict = jnp.tril(jnp.ones((CHUNK, CHUNK), bool), -1)
            diff = gc[..., :, None] - gc[..., None, :]
            decay = jnp.exp(jnp.where(tril, diff, 0.0)) * tril
            A = -(jnp.einsum('bhnid,bhnjd->bhnij', k_beta, kc) * decay) * strict
            eye = jnp.eye(CHUNK, dtype=A.dtype)
            Tm = jax.scipy.linalg.solve_triangular(eye - A, jnp.broadcast_to(eye, A.shape), lower=True, unit_diagonal=True)
            u = jnp.einsum('bhnij,bhnjv->bhniv', Tm, v_beta)
            kcd = jnp.einsum('bhnij,bhnjd->bhnid', Tm, k_beta * jnp.exp(gc)[..., None])
            front = lambda t: jnp.moveaxis(t, 2, 0)
            xs = (front(qc), front(kc), front(u), front(kcd), front(decay), front(gc))
            S0 = jnp.zeros((Bs, NV, DK, DV), jnp.float32)

            def step(St, inp):
                q_i, k_i, u_i, kcd_i, dec_i, g_i = inp
                attn = jnp.einsum('bhid,bhjd->bhij', q_i, k_i) * dec_i
                v_new = u_i - jnp.einsum('bhid,bhdv->bhiv', kcd_i, St)
                inter = jnp.einsum('bhid,bhdv->bhiv', q_i * jnp.exp(g_i)[..., None], St)
                out_i = inter + jnp.einsum('bhij,bhjv->bhiv', attn, v_new)
                g_last = g_i[..., -1]
                St_new = St * jnp.exp(g_last)[..., None, None] + jnp.einsum('bhid,bhiv->bhdv', k_i * jnp.exp(g_last[..., None] - g_i)[..., None], v_new)
                return (St_new, out_i)
            _, outs = jax.lax.scan(step, S0, xs)
            core = jnp.moveaxis(outs, 0, 2).reshape(Bs, NV, Ss, DV)
            core = jnp.swapaxes(core, 1, 2)
            zr = z.reshape(Bs, Ss, NV, DV)
            var = jnp.mean(core * core, axis=-1, keepdims=True)
            normed = core * jax.lax.rsqrt(var + EPS) * norm_w * jax.nn.silu(zr)
            return jnp.einsum('bsv,hv->bsh', normed.reshape(Bs, Ss, VAL_DIM), W_out)
        return _forward(x, W_qkv, W_z, W_b, W_a, W_out, conv_w, dt_bias, A_log, norm_w)

    def _L0_ffn_ref(hidden_states, gate_w, bias, w_gate, w_up, w_down, ws_gate, ws_up, ws_down):
        import jax, jax.numpy as jnp
        import numpy as np
        E, K, H, F = (64, 6, 256, 96)
        G, KG = (8, 4)
        SHARED_F = 96
        SCALE = 2.5
        T = 2 * 128
        CAP = 2 * (T * K // E)

        def _grouped_topk(logits, bias):
            scores = jax.nn.sigmoid(logits.astype(jnp.float32))
            scores_b = scores + bias[None, :]
            gs = scores_b.reshape(-1, G, E // G)
            group_scores = jnp.sum(jax.lax.top_k(gs, 2)[0], axis=-1)
            gidx = jax.lax.top_k(group_scores, KG)[1]
            rows = jnp.arange(group_scores.shape[0])[:, None]
            group_mask = jnp.zeros_like(group_scores).at[rows, gidx].set(1.0)
            score_mask = jnp.repeat(group_mask, E // G, axis=-1) > 0
            tmp = jnp.where(score_mask, scores_b, -jnp.inf)
            topk_ids = jax.lax.top_k(tmp, K)[1]
            topk_w = jnp.take_along_axis(scores, topk_ids, axis=-1)
            topk_w = topk_w / jnp.sum(topk_w, axis=-1, keepdims=True)
            return (topk_w * SCALE, topk_ids)

        def _routed_moe(x, topk_w, topk_ids, w_gate, w_up, w_down):
            Tn = x.shape[0]
            flat_e = topk_ids.reshape(-1)
            order = jnp.argsort(flat_e)
            se = flat_e[order]
            pos = jnp.arange(Tn * K) - jnp.searchsorted(se, se, side='left')
            tok = order // K
            valid = pos < CAP
            slot = jnp.where(valid, pos, CAP)
            buf = jnp.zeros((E, CAP + 1, H), x.dtype).at[se, slot].set(x[tok])[:, :CAP]
            h = jax.nn.silu(jnp.einsum('ech,ehf->ecf', buf, w_gate)) * jnp.einsum('ech,ehf->ecf', buf, w_up)
            out = jnp.einsum('ecf,efh->ech', h, w_down)
            gathered = out[se, jnp.minimum(pos, CAP - 1)] * valid.astype(x.dtype)[:, None]
            w = topk_w.reshape(-1)[order].astype(x.dtype)[:, None]
            return jax.ops.segment_sum(gathered * w, tok, num_segments=Tn)
        orig_shape = hidden_states.shape
        x = hidden_states.reshape(-1, H)
        router_logits = x @ gate_w
        topk_w, topk_ids = _grouped_topk(router_logits, bias)
        y = _routed_moe(x, topk_w, topk_ids, w_gate, w_up, w_down)
        shared = jax.nn.silu(x @ ws_gate) * (x @ ws_up) @ ws_down
        return (y + shared).reshape(orig_shape)
    x = L0_attn_x
    x = x + _layernorm(_L0_attn_ref(_layernorm(x, axis=-1), L0_attn_W_qkv, L0_attn_W_z, L0_attn_W_b, L0_attn_W_a, L0_attn_W_out, L0_attn_conv_w, L0_attn_dt_bias, L0_attn_A_log, L0_attn_norm_w), axis=-1)
    x = x + _layernorm(_L0_ffn_ref(_layernorm(x, axis=-1), L0_ffn_gate_w, L0_ffn_bias, L0_ffn_w_gate, L0_ffn_w_up, L0_ffn_w_down, L0_ffn_ws_gate, L0_ffn_ws_up, L0_ffn_ws_down), axis=-1)
    return x

_drawn_inputs = setup_inputs


def setup_inputs(seed=0):
    import zlib

    import numpy as np

    out = dict(_drawn_inputs(seed))
    spreads = {'L0_attn_norm_w': (1.0, 0.2)}
    factors = {}
    for name, (base, spread) in spreads.items():
        noise = np.random.default_rng([zlib.crc32(name.encode()), seed]).standard_normal(out[name].shape)
        drawn = base * np.exp(spread * noise) if base else spread * noise
        out[name] = jnp.asarray(drawn.astype(out[name].dtype))
    for name, factor in factors.items():
        out[name] = (out[name] * factor).astype(out[name].dtype)
    return out
```

```python
from contextlib import ExitStack

import concourse.bass as bass
from concourse import mybir

ALU = mybir.AluOpType
ACT = mybir.ActivationFunctionType
AX = mybir.AxisListType
F32 = mybir.dt.float32
F16 = mybir.dt.float16
U32 = mybir.dt.uint32

P = 128
B, S, H = 2, 1024, 256
KT = H // P
D = 128
NK = 16
NV = 2 * NK
C = 64
NC = S // C
BLK = 2 * C
NB = S // BLK
NSTEPS = NK * NC
TAPS = 4
K_, Q_, V_, Z_ = 0, 1, 2, 4
NT = 6
NEG = -1e30
EPS_LN, EPS_RMS = 1e-5, 1e-6
E = 64
TOP = 6
EG, KG = 8, 4
F = 96
CAP = 48
ROUTE_SCALE = 2.5
NTAB = 4
TOKENS = B * S
GROUPS = 4
GC = NC // GROUPS
ZPARTS = 8
ZCOLS = (TOKENS + CAP) // 16 * H // ZPARTS


def twice(ap):
    return ap.unsqueeze(1).broadcast_to([ap.shape[0], 2, ap.shape[1]])


def sems(ctx, nc, names):
    return {n: ctx.enter_context(nc.semaphore(n)) for n in names.split()}


def at_start(count):
    return isinstance(count, int) and count == 0


def in_register(eng, count):
    if not isinstance(count, int):
        eng.compute_val(count)
    return count


def u_half(u):
    return slice(u * C, (u + 1) * C)


class LayerNorm:

    def __init__(self, ctx, nc, name):
        self.nc = nc
        self.total = ctx.enter_context(nc.sbuf_tensor(name + "_total", [P, NC], F32))
        self.mean = ctx.enter_context(nc.sbuf_tensor(name + "_mean", [P, NC], F32))
        self.sumsq = ctx.enter_context(nc.sbuf_tensor(name + "_sumsq", [P, NC], F32))
        self.var = ctx.enter_context(nc.sbuf_tensor(name + "_var", [P, NC], F32))
        self.inv = ctx.enter_context(nc.sbuf_tensor(name + "_inv", [P, NC], F32))
        self.minus_half = ctx.enter_context(nc.sbuf_tensor(name + "_minus_half", [P, GC], F32))
        self.squares = ctx.enter_context(nc.sbuf_tensor(name + "_squares", [P, H], F32))
        self.s = sems(ctx, nc, " ".join(f"{name}_{x}" for x in "averaged centred squared inverted done".split()))
        self.name = name

    def sem(self, what):
        return self.s[f"{self.name}_{what}"]

    def vector(self, eng, src, dst, before_group=None):
        v = self.nc.vector
        for g in range(GROUPS):
            a = slice(g * GC, (g + 1) * GC)
            if before_group:
                before_group(g)
            v.tensor_reduce(self.total[:, a], src[:, a], AX.X, ALU.add).then_inc(self.sem("averaged"), 1)
            eng.wait_ge(self.sem("averaged"), 2 * g + 1)
            v.tensor_scalar(self.mean[:, a], self.total[:, a], -1.0 / H, None, ALU.mult).then_inc(self.sem("averaged"), 1)
            eng.wait_ge(self.sem("averaged"), 2 * g + 2)
            v.tensor_tensor(dst[:, a], src[:, a], self.mean[:, a].unsqueeze(2).broadcast_to([P, GC, H]),
                            ALU.add).then_inc(self.sem("centred"), 1)
        for g in range(GROUPS):
            a = slice(g * GC, (g + 1) * GC)
            eng.wait_ge(self.sem("inverted"), 2 * g + 3)
            v.tensor_tensor(dst[:, a], dst[:, a], self.inv[:, a].unsqueeze(2).broadcast_to([P, GC, H]),
                            ALU.mult).then_inc(self.sem("done"), 1)

    def scalar(self, eng, dst):
        a = self.nc.scalar
        for g in range(GROUPS):
            eng.wait_ge(self.sem("centred"), g + 1)
            for c in range(g * GC, (g + 1) * GC):
                if c:
                    eng.wait_ge(self.sem("squared"), c)
                a.activation(self.squares[:], dst[:, c], ACT.Square, accum_out=self.sumsq[:, c:c + 1]).then_inc(self.sem("squared"), 1)

    def gpsimd(self, eng):
        p = self.nc.gpsimd
        p.memset(self.minus_half[:], -0.5).then_inc(self.sem("inverted"), 1)
        for g in range(GROUPS):
            a = slice(g * GC, (g + 1) * GC)
            eng.wait_ge(self.sem("squared"), (g + 1) * GC)
            p.tensor_scalar(self.var[:, a], self.sumsq[:, a], 1.0 / H, EPS_LN, ALU.mult, ALU.add).then_inc(self.sem("inverted"), 1)
            eng.wait_ge(self.sem("inverted"), 2 * g + 2)
            p.tensor_tensor(self.inv[:, a], self.var[:, a], self.minus_half[:], ALU.pow).then_inc(self.sem("inverted"), 1)


def setup(nc, io, k):
    with ExitStack() as ctx:
        def sb(name, shape, dt=F32):
            return ctx.enter_context(nc.sbuf_tensor(name, shape, dt))

        ps = [ctx.enter_context(nc.psum_tensor(f"setup_bank{i}", [P, 512], F32)) for i in range(6)]
        xn = sb("xn", [P, NC, H])
        w_ba = sb("w_ba", [P, KT, 2 * NV])
        dt_row, a_row, neg_a = sb("dt_row", [P, NV]), sb("a_row", [P, NV]), sb("neg_a", [P, NV])
        tri, halves = sb("tri", [P, P]), sb("halves", [P, P])
        gate_shape = [P, NC, NV]
        beta, pre, soft, g, g_sum, g_last = (sb(n, gate_shape) for n in ("beta", "pre", "soft", "g", "g_sum", "g_last"))
        gT, eT = sb("gT", [NV, B, S]), sb("eT", [NV, B, S])
        zeros = sb("zeros", [2, NB * B * BLK])
        zeros_wide = sb("zeros_wide", [16, ZCOLS])
        beta_hc, g_hc, last_hc = (sb(n, [P, 2, NK, NC]) for n in ("beta_hc", "g_hc", "last_hc"))
        beta_col, g_col, last_col, eg_col = (sb(n, [P, B, NSTEPS]) for n in ("beta_col", "g_sum_col", "last_col", "eg_col"))
        ln = LayerNorm(ctx, nc, "ln_in")
        s = sems(ctx, nc, """x_in weights_in tables_zeroed masks_cleared masks_ready turned x_copied ba_done summed row_turned
            pre_ready gate_exp gate_log gate_step gates_done hc_done sums_out rows_copied rows_exp rows_out cols_in col_exp col_step
            cols_done""")
        flat = lambda ap: ap.rearrange("p c h -> p (c h)")

        block = ctx.enter_context(nc.Block())

        @block.sync
        def _(sp):
            for b in range(B):
                sp.dma_start(k.x_tok[b * C:(b + 1) * C], io["x"][b].rearrange("(c i) h -> i c h", i=C)).then_inc(s["x_in"], 16)
            for dst, src in ((w_ba[:], io["w_ba"]), (dt_row[:], io["dt_bias"].partition_broadcast(P)),
                             (a_row[:], io["A_log"].partition_broadcast(P)), (k.half_norm_w[:], io["norm_w"])):
                sp.dma_start(dst, src).then_inc(s["weights_in"], 16)
            sp.wait_ge(s["masks_cleared"], 1)
            for t in range(NTAB):
                rows = k.tables[t].rearrange("(p q) h -> p (q h)", q=(TOKENS + CAP) // 16)
                for part in range(ZPARTS):
                    sp.dma_start(rows[:, part * ZCOLS:(part + 1) * ZCOLS], zeros_wide[0:16]).then_inc(s["tables_zeroed"], 16)
            sp.wait_ge(s["hc_done"], 3)
            for src, dst in ((g_hc, g_col), (beta_hc, beta_col), (last_hc, last_col)):
                for u in range(2):
                    for b in range(B):
                        sp.dma_start(dst[u_half(u), b], src[u_half(b), u].rearrange("p j c -> p (j c)")).then_inc(s["cols_in"], 16)
            sp.wait_ge(s["rows_exp"], 1)
            sp.wait_ge(s["rows_copied"], 4)
            for src, dst in ((gT, k.g_rows), (eT, k.e_rows)):
                for b in range(B):
                    sp.dma_start(dst[0:NK].rearrange("j u r b t -> (j u) r b t")[:, :, b],
                                 src[:, b].rearrange("h (r t) -> h r t", r=NB)).then_inc(s["rows_out"], 16)
                sp.dma_start(dst[NK].rearrange("u r b t -> u (r b t)"), zeros[:]).then_inc(s["rows_out"], 16)
            sp.wait_ge(s["rows_out"], 16 * 6)
            sp.wait_ge(s["tables_zeroed"], 16 * NTAB * ZPARTS)

        @block.gpsimd
        def _(pool):
            g_ = nc.gpsimd
            g_.memset(k.ident[:], 0.0)
            g_.memset(k.ident_half[:], 0.0)
            g_.memset(tri[:], 1.0)
            g_.memset(halves[:], 0.0)
            g_.memset(k.mask_l[:], 0.0)
            g_.memset(k.mask_u[:], 0.0)
            g_.memset(k.ones_col[:], 1.0)
            g_.memset(k.pow_half[:], -0.5)
            for t in (k.g_col, k.tail_col, k.half_beta, k.minus_beta, k.minus_beta_eg):
                g_.memset(t[:, NSTEPS:], 0.0)
            g_.memset(zeros_wide[:], 0.0)
            g_.memset(zeros[:], 0.0).then_inc(s["masks_cleared"], 1)
            pool.wait_ge(s["masks_cleared"], 1)
            g_.affine_select(out=k.ident[:], in_=k.ident[:], compare_op=ALU.not_equal, fill=1.0, base=0,
                             pattern=[[-1, P]], channel_multiplier=1)
            g_.affine_select(out=tri[:], in_=tri[:], compare_op=ALU.is_ge, fill=0.0, base=0,
                             pattern=[[1, P]], channel_multiplier=-1).then_inc(s["masks_cleared"], 1)
            steps = 2
            for u in range(2):
                h = u_half(u)
                for make in (lambda: g_.memset(halves[h, h], 1.0),
                             lambda: g_.affine_select(out=k.ident_half[h], in_=k.ident_half[h], compare_op=ALU.not_equal, fill=1.0,
                                                      base=0, pattern=[[-1, C]], channel_multiplier=1),
                             lambda: g_.affine_select(out=k.mask_l[h], in_=k.mask_l[h], compare_op=ALU.is_gt, fill=NEG, base=0,
                                                      pattern=[[-1, C]], channel_multiplier=1),
                             lambda: g_.affine_select(out=k.mask_u[h], in_=k.mask_u[h], compare_op=ALU.is_ge, fill=NEG, base=0,
                                                      pattern=[[1, C]], channel_multiplier=-1)):
                    pool.wait_ge(s["masks_cleared"], steps)
                    make().then_inc(s["masks_cleared"], 1)
                    steps += 1
            pool.wait_ge(s["masks_cleared"], steps)
            g_.memset(tri[0:C, C:P], 0.0).then_inc(s["masks_ready"], 1)
            pool.wait_ge(s["masks_ready"], 1)
            ln.gpsimd(pool)

        @block.vector
        def _(dve):
            v = nc.vector
            dve.wait_ge(s["x_in"], 32)
            ln.vector(dve, k.x_tok, xn)
            dve.wait_ge(s["weights_in"], 64)
            dve.wait_ge(s["ba_done"], 1)
            for i in range(2):
                a8 = slice(i * 8, (i + 1) * 8)
                v.tensor_tensor(pre[:, a8], ps[2 + i][:].rearrange("p (c h) -> p c h", c=8)[:, :, NV:],
                                dt_row[:].unsqueeze(1).broadcast_to([P, 8, NV]), ALU.add).then_inc(s["gate_step"], 1)
            v.tensor_scalar(k.half_norm_w[:], k.half_norm_w[:], 0.5, None, ALU.mult)
            dve.wait_ge(s["gate_step"], 2)
            v.tensor_scalar(soft[:], pre[:], -1.0, None, ALU.mult).then_inc(s["gate_step"], 1)
            dve.wait_ge(s["gate_step"], 3)
            v.tensor_tensor(soft[:], soft[:], pre[:], ALU.min).then_inc(s["pre_ready"], 1)
            dve.wait_ge(s["gate_log"], 1)
            v.tensor_scalar(pre[:], pre[:], 0.0, None, ALU.max).then_inc(s["gate_step"], 1)
            v.tensor_scalar(neg_a[:], neg_a[:], -1.0, None, ALU.mult).then_inc(s["gate_step"], 1)
            dve.wait_ge(s["gate_step"], 5)
            v.tensor_tensor(soft[:], soft[:], pre[:], ALU.add).then_inc(s["gate_step"], 1)
            dve.wait_ge(s["gate_step"], 6)
            v.tensor_tensor(g[:], soft[:], neg_a[:].unsqueeze(1).broadcast_to([P, NC, NV]), ALU.mult).then_inc(s["gates_done"], 1)
            dve.wait_ge(s["summed"], 1)
            v.tensor_copy(flat(g_sum[:]), ps[4][:]).then_inc(s["sums_out"], 1)
            v.tensor_copy(flat(g_last[:]), ps[5][:]).then_inc(s["sums_out"], 1)
            dve.wait_ge(s["sums_out"], 2)
            dve.wait_ge(s["gate_exp"], 2)
            for src, dst in ((g_sum, g_hc), (g_last, last_hc), (beta, beta_hc)):
                for u in range(2):
                    mm = v.tensor_copy(dst[:, u], src[:].rearrange("p c (j u) -> p u j c", u=2)[:, u])
                mm.then_inc(s["hc_done"], 1)
            dve.wait_ge(s["row_turned"], 1)
            for i in range(4):
                v.tensor_copy(gT[:, :, i * 4 * C:(i + 1) * 4 * C].rearrange("h b (c i) -> h c b i", i=C),
                              ps[i][0:NV].rearrange("h (c b i) -> h c b i", c=4, b=B)).then_inc(s["rows_copied"], 1)
            dve.wait_ge(s["cols_in"], 16 * 12)
            to = lambda t: t[:, 0:NSTEPS].rearrange("p s b -> p b s")
            v.tensor_scalar(to(k.half_beta), beta_col[:], 0.5, None, ALU.mult)
            v.tensor_scalar(to(k.minus_beta), beta_col[:], -1.0, None, ALU.mult).then_inc(s["col_step"], 1)
            v.tensor_copy(to(k.g_col), g_col[:])
            v.tensor_tensor(last_col[:], last_col[:], g_col[:], ALU.subtract).then_inc(s["col_step"], 1)
            dve.wait_ge(s["col_step"], 2)
            dve.wait_ge(s["col_exp"], 1)
            v.tensor_tensor(to(k.minus_beta_eg), to(k.minus_beta), eg_col[:], ALU.mult)

        @block.scalar
        def _(act):
            a = nc.scalar
            ln.scalar(act, xn)
            for c in range(NC):
                act.wait_ge(s["turned"], c + 1)
                a.copy(k.xT[:, :, c], ps[c % 2][:, 0:KT * P].rearrange("p (k b i) -> p k b i", k=KT, b=B)).then_inc(s["x_copied"], 1)
            act.wait_ge(s["weights_in"], 64)
            a.activation(neg_a[:], a_row[:], ACT.Exp)
            act.wait_ge(s["pre_ready"], 1)
            a.activation(g[:], soft[:], ACT.Exp).then_inc(s["gate_exp"], 1)
            act.wait_ge(s["gate_exp"], 1)
            a.activation(soft[:], g[:], ACT.Ln, bias=k.ones_col[:]).then_inc(s["gate_log"], 1)
            for i in range(2):
                a8 = slice(i * 8, (i + 1) * 8)
                last = a.activation(beta[:, a8], ps[2 + i][:].rearrange("p (c h) -> p c h", c=8)[:, :, 0:NV], ACT.Sigmoid)
            last.then_inc(s["gate_exp"], 1)
            act.wait_ge(s["rows_copied"], 4)
            a.activation(eT[:], gT[:], ACT.Exp).then_inc(s["rows_exp"], 1)
            act.wait_ge(s["cols_in"], 16 * 12)
            a.activation(eg_col[:], g_col[:], ACT.Exp).then_inc(s["col_exp"], 1)
            act.wait_ge(s["col_step"], 2)
            a.activation(k.tail_col[:, 0:NSTEPS].rearrange("p s b -> p b s"), last_col[:], ACT.Exp).then_inc(s["cols_done"], 1)

        @block.tensor
        def _(pe):
            pe.wait_ge(s["masks_ready"], 1)
            for c in range(NC):
                if c >= 2:
                    pe.wait_ge(s["x_copied"], c - 1)
                pe.wait_ge(ln.sem("done"), c // GC + 1)
                for kt in range(KT):
                    mm = nc.tensor.transpose(ps[c % 2][:, kt * P:(kt + 1) * P], xn[:, c, kt * P:(kt + 1) * P], k.ident[:])
                mm.then_inc(s["turned"], 1)
            pe.wait_ge(s["x_copied"], NC)
            pe.wait_ge(s["weights_in"], 64)
            for c in range(NC):
                for kt in range(KT):
                    mm = nc.tensor.matmul(ps[2 + c // 8][:, (c % 8) * 2 * NV:(c % 8 + 1) * 2 * NV], k.xT[:, kt, c].rearrange("p b i -> p (b i)"),
                                          w_ba[:, kt], start=(kt == 0), stop=(kt == KT - 1))
            mm.then_inc(s["ba_done"], 1)
            pe.wait_ge(s["gates_done"], 1)
            nc.tensor.matmul(ps[4][:], tri[:], flat(g[:]), start=True, stop=True)
            nc.tensor.matmul(ps[5][:], halves[:], flat(g[:]), start=True, stop=True).then_inc(s["summed"], 1)
            pe.wait_ge(s["sums_out"], 2)
            pe.wait_ge(s["gate_exp"], 2)
            for c in range(NC):
                mm = nc.tensor.transpose(ps[c // 4][0:NV, (c % 4) * P:(c % 4 + 1) * P], g_sum[:, c], k.ident[:])
            mm.then_inc(s["row_turned"], 1)


def delta_rule(nc, io, k, pairs):
    with ExitStack() as ctx:
        def sb(name, shape, dt=F32):
            return ctx.enter_context(nc.sbuf_tensor(name, shape, dt))

        bank = [ctx.enter_context(nc.psum_tensor(f"bank{i}", [P, 512], F32)) for i in range(8)]
        w_proj = sb("w_proj", [P, KT, NT, P])
        w_out = sb("w_out", [P, 2, H])
        conv_w = sb("conv_w", [P, 4, TAPS])
        raw = sb("raw", [P, 4, B, TAPS - 1 + BLK])
        conv = sb("conv", [P, 4, B, BLK])
        th = sb("th", [P, 4, B, BLK])
        kqv = sb("kqv", [P, 4, B, BLK])
        thz = sb("thz", [P, 2, B, BLK])
        zs = sb("zs", [P, 2, B, BLK])
        sq = sb("sq", [P, 2, B, BLK])
        g_blk = sb("g_blk", [P, B, BLK])
        e_blk = sb("e_blk", [P, 2, B, BLK])
        g_diff = sb("g_diff", [P, 2, B, C])
        dec_arg = sb("dec_arg", [P, 2, 2, B, C])
        dec = sb("dec", [P, 2, 2, B, C])
        ssq = sb("ssq", [P, 2, 2, B])
        rn = sb("rn", [P, 2, 2, B])
        rn2 = sb("rn2", [P, 2, B])
        kc = sb("kc", [P, 2, B, 2, C])
        vc = sb("vc", [P, B, 2, C])
        qg = sb("qg", [P, 2, B, 2, C])
        s_dec = sb("s_dec", [P, 2, B, 2])
        l_scale = sb("l_scale", [P, 2, B])
        v_scale = sb("v_scale", [P, 2, B])
        ks_scale = sb("ks_scale", [P, 2, B])
        k_tail = sb("k_tail", [P, 2, B])
        q_scale = sb("q_scale", [P, 2, B])
        q_scale2 = sb("q_scale2", [P, 2, B])
        attnT = sb("attnT", [P, 2, B, C])
        vb = sb("vb", [P, 2, B, D])
        kdec = sb("kdec", [P, 2, B, D])
        inv = sb("inv", [P, 2, B, C])
        UL = sb("UL", [P, 2, B, 2, C])
        prod = sb("prod", [P, 2, B, C])
        r = sb("r", [P, B, D])
        vt = sb("vt", [P, B, D])
        state = sb("state", [P, B, 2, D])
        state_d = sb("state_d", [P, B, 2, D])
        squares = sb("squares", [P, B, D])
        core_ss, core_ms, core_var, core_rs, core_f = (sb(n, [P, B]) for n in ("core_ss", "core_ms", "core_var", "core_rs", "core_f"))
        core_n = sb("core_n", [P, B, D])
        gated = sb("gated", [P, 2, B, C])
        credits = sb("credits", [P, 6])

        s = sems(ctx, nc, """w_in grown_0 conv_w_in w_out_in g_in e_in started
            projected_kq projected_v projected_z ssq_summed grammed turned u_turned squared powered
            ks_done vt_done core_done grown_1 core_turned y_projected
            raw_in tap_in conv_tanhed z_tanhed decayed vb_out u_out ul_out vt_out squares_out core_out
            conv_steps kqv_ready z_ready ssq_out l_ready attn_ready p_out r_ready s_updated gated_out y_added
            hist_done kq_squared rn_ready diffed dec_args kc_ready vc_ready qg_ready cols_ready rn2_ready q_steps p1_ready
            s_decayed f_steps f_ready""")

        def per_pair(eng, body):
            with eng.Fori(0, pairs) as pair:
                with eng.Fori(0, NB - 1) as rr:
                    body(pair, rr, pair * NB + rr, False)
                body(pair, NB - 1, pair * NB + (NB - 1), True)

        block = ctx.enter_context(nc.Block())

        @block.sync
        def _(sp):
            def load_projection(pair):
                sp.dma_start(w_proj[:], io["w_proj"][bass.ds(pair, 1)].rearrange("o p k t c -> (o p) k t c")).then_inc(s["w_in"], 16)
                sp.dma_start(conv_w[:], io["conv_w"][bass.ds(pair, 1)].rearrange("o p t w -> (o p) t w")).then_inc(s["conv_w_in"], 16)

            def load_w_out(pair):
                sp.dma_start(w_out[:], io["w_out"][bass.ds(pair, 1)].rearrange("o p u h -> (o p) u h")).then_inc(s["w_out_in"], 16)

            def load_rows(pair, rr):
                for u in range(2):
                    src = k.g_rows[bass.ds(pair, 1), u, bass.ds(rr, 1)].rearrange("o q b t -> (o q) (b t)")
                    sp.dma_start(g_blk[u_half(u)], src.broadcast_to([C, B * BLK])).then_inc(s["g_in"], 16)
                for u in range(2):
                    src = k.e_rows[bass.ds(pair, 1), u, bass.ds(rr, 1)].rearrange("o q b t -> (o q) (b t)")
                    sp.dma_start(e_blk[:, u], src.broadcast_to([P, B * BLK])).then_inc(s["e_in"], 16)

            load_projection(0)
            load_rows(0, 0)
            load_w_out(0)

            def body(pair, rr, n, last):
                if last:
                    sp.wait_ge(s["projected_z"], n + 1)
                    sp.wait_ge(s["conv_steps"], 12 * n + 12)
                    load_projection(pair + 1)
                sp.wait_ge(s["diffed"], n + 1)
                sp.wait_ge(s["qg_ready"], 2 * n + 2)
                sp.wait_ge(s["cols_ready"], 2 * n + 2)
                load_rows(pair + 1 if last else pair, 0 if last else rr + 1)
                if last:
                    sp.wait_ge(s["y_projected"], 2 * n + 2)
                    load_w_out(pair + 1)

            per_pair(sp, body)
            sp.wait_ge(s["w_in"], 16 * (pairs + 1))
            sp.wait_ge(s["conv_w_in"], 16 * (pairs + 1))
            sp.wait_ge(s["w_out_in"], 16 * (pairs + 1))
            sp.wait_ge(s["g_in"], 32 * (pairs * NB + 1))
            sp.wait_ge(s["e_in"], 32 * (pairs * NB + 1))

        @block.tensor
        def _(pe):
            te = nc.tensor

            def project(rr, tiles, bk, done):
                for q, t in enumerate(tiles):
                    for kt in range(KT):
                        mm = te.matmul(bank[bk][:, q * 2 * BLK:(q + 1) * 2 * BLK], w_proj[:, kt, t],
                                       k.xT[:, kt, bass.ds(rr * 2, 2)].rearrange("p c b i -> p b c i"), start=(kt == 0), stop=(kt == KT - 1))
                mm.then_inc(s[done], 1)

            def sum_squares(m):
                pe.wait_ge(s["kq_squared"], m + 1)
                pe.wait_ge(s["raw_in"], 2 * m + 2)
                for kq in range(2):
                    for p in range(2):
                        for b in range(B):
                            i = (kq * 2 + p) * B + b
                            for u in range(2):
                                mm = te.matmul(bank[1][u_half(u), i:i + 1], sq[:, kq, b, p * C:(p + 1) * C], k.ones_col[:],
                                               start=True, stop=True)
                mm.then_inc(s["ssq_summed"], 1)

            def gram(st, p):
                pe.wait_ge(s["kc_ready"], st + 1)
                for b in range(B):
                    mm = te.matmul(bank[3][:, b * P:(b + 1) * P], kc[:, p, b].rearrange("p u i -> p (u i)"),
                                   kqv[:, K_:Q_ + 1, b, p * C:(p + 1) * C], start=True, stop=True)
                mm.then_inc(s["grammed"], 1)

            def turn(st, p):
                pe.wait_ge(s["vc_ready"], st + 1)
                for b in range(B):
                    te.transpose(bank[2][:, b * P:(b + 1) * P], kc[:, p, b].rearrange("p u i -> p (u i)"), k.ident[:])
                    mm = te.transpose(bank[2][:, (2 + b) * P:(3 + b) * P], vc[:, b].rearrange("p u i -> p (u i)"), k.ident[:])
                mm.then_inc(s["turned"], 1)

            def tiles(fn):
                for b in range(B):
                    for u in range(2):
                        mm = fn(b, u_half(u))
                return mm

            def turn_u(st):
                rounds, this = in_register(pe, 5 * st + 1), in_register(pe, st + 1)
                ready()
                pe.wait_ge(s["ul_out"], rounds)
                pe.wait_ge(s["l_ready"], this)
                tiles(lambda b, h: te.matmul(bank[4][h, b * P:b * P + C], UL[h, 0, b, 1], k.ident[h, h],
                                             start=True, stop=True)).then_inc(s["u_turned"], 1)

            def ready():
                pe.wait_ge(s["started"], 1)

            def square(st, i):
                w = (i - 1) % 2
                rounds = in_register(pe, st + 1 if i == 1 else 5 * st + i)
                ready()
                if i == 1:
                    pe.wait_ge(s["u_out"], rounds)
                else:
                    pe.wait_ge(s["ul_out"], rounds)
                if i < 5:
                    tiles(lambda b, h: te.matmul(bank[4][h, b * P:b * P + C], UL[h, w, b, 1], UL[h, w, b, 0],
                                                 start=True, stop=True))
                tiles(lambda b, h: te.matmul(bank[4][h, b * P + C:(b + 1) * P], UL[h, w, b, 0], UL[h, w, b, 1],
                                             start=True, stop=True)).then_inc(s["squared"], 1)

            def power(st, i):
                w = (i - 1) % 2
                this, rounds, powers = (in_register(pe, x) for x in (st + 1, 5 * st + i, 5 * st + i - 1))
                ready()
                pe.wait_ge(s["ul_out"], rounds)
                if i == 2:
                    pe.wait_ge(s["p1_ready"], this)
                pe.wait_ge(s["p_out"], powers)
                tiles(lambda b, h: te.matmul(bank[5][h, b * C:(b + 1) * C], UL[h, w, b, 1], prod[h, i % 2, b],
                                             start=True, stop=True)).then_inc(s["powered"], 1)

            def keys_state(st, p):
                pe.wait_ge(s["s_updated"], st + 1)
                pe.wait_ge(s["kc_ready"], st + 1)
                pe.wait_ge(s["y_added"], st + 1)
                for b in range(B):
                    for u in range(2):
                        mm = te.matmul(bank[6][u_half(u), b * D:(b + 1) * D], kc[:, p, b, 0], state[:, b, u], start=True, stop=True)
                mm.then_inc(s["ks_done"], 1)

            def values(st, p):
                this, powers = in_register(pe, st + 1), in_register(pe, 5 * st + 6)
                ready()
                pe.wait_ge(s["r_ready"], this)
                pe.wait_ge(s["p_out"], powers)
                pe.wait_ge(s["core_out"], this)
                tiles(lambda b, h: te.matmul(bank[7][h, b * D:(b + 1) * D], inv[h, p, b], r[h, b],
                                             start=True, stop=True)).then_inc(s["vt_done"], 1)

            def core(st, p):
                pe.wait_ge(s["vt_out"], st + 1)
                pe.wait_ge(s["qg_ready"], st + 1)
                pe.wait_ge(s["attn_ready"], st + 1)
                for b in range(B):
                    for u in range(2):
                        h = u_half(u)
                        te.matmul(bank[7][h, b * D:(b + 1) * D], qg[:, p, b, u], state[:, b, u],
                                  start=True, stop=False, skip_group_check=True)
                        mm = te.matmul(bank[7][h, b * D:(b + 1) * D], attnT[h, p, b], vt[h, b],
                                       start=False, stop=True, skip_group_check=True)
                mm.then_inc(s["core_done"], 1)

            def grow(st, p):
                pe.wait_ge(s["vb_out"], 2 * st + 2)
                for u, bk in ((0, 3), (1, 6)):
                    for b in range(B):
                        mm = te.matmul(bank[bk][:, b * D:(b + 1) * D], kdec[u_half(u), p, b], vt[u_half(u), b], start=True, stop=True)
                    mm.then_inc(s[f"grown_{u}"], 1)

            def turn_core(st):
                pe.wait_ge(s["core_out"], st + 2)
                pe.wait_ge(s["s_updated"], st + 2)
                for b in range(B):
                    o = bank[6][:, 0:2 * P].rearrange("p (u b i) -> p u b i", u=2, b=B)[:, :, b]
                    mm = te.transpose(o, core_n[:, b], k.ident[:])
                mm.then_inc(s["core_turned"], 1)

            def project_out(st, pair):
                pe.wait_ge(s["w_out_in"], 16 * (pair + 1))
                pe.wait_ge(s["gated_out"], st + 1)
                for u in range(2):
                    mm = te.matmul(bank[6][:, 0:H], gated[:, u].rearrange("p b i -> p (b i)"), w_out[:, u],
                                   start=(u == 0), stop=(u == 1))
                mm.then_inc(s["y_projected"], 1)

            pe.wait_ge(s["started"], 1)
            pe.wait_ge(s["w_in"], 16)
            project(0, (K_, Q_), 0, "projected_kq")
            project(0, (V_, V_ + 1), 1, "projected_v")
            pe.wait_ge(s["raw_in"], 1)
            project(0, (Z_, Z_ + 1), 0, "projected_z")
            sum_squares(0)
            gram(0, 0)
            turn(0, 0)
            turn_u(0)
            for i in range(1, 7):
                if i <= 5:
                    square(0, i)
                if i >= 2:
                    power(0, i)

            def body(pair, rr, n, last):
                next_rr = 0 if last else rr + 1
                for half in range(2):
                    st, fs, p, fp = 2 * n + half, 2 * n + half + 1, half, 1 - half
                    pe.wait_ge(s["s_updated"], st + 1)
                    gram(fs, fp)
                    pe.wait_ge(s["vb_out"], 2 * st + 2)
                    turn(fs, fp)
                    keys_state(st, p)
                    if half == 0:
                        if last:
                            pe.wait_ge(s["w_in"], 16 * (pair + 2))
                        pe.wait_ge(s["z_ready"], n + 1)
                        project(next_rr, (K_, Q_), 0, "projected_kq")
                    turn_u(fs)
                    values(st, p)
                    square(fs, 1)
                    if half == 0:
                        pe.wait_ge(s["ssq_out"], n + 1)
                        project(next_rr, (V_, V_ + 1), 1, "projected_v")
                    core(st, p)
                    square(fs, 2)
                    power(fs, 2)
                    pe.wait_ge(s["attn_ready"], fs + 1)
                    grow(st, p)
                    square(fs, 3)
                    power(fs, 3)
                    if half == 1:
                        pe.wait_ge(s["raw_in"], 2 * n + 3)
                        project(next_rr, (Z_, Z_ + 1), 0, "projected_z")
                    turn_core(st)
                    square(fs, 4)
                    power(fs, 4)
                    project_out(st, pair)
                    square(fs, 5)
                    power(fs, 5)
                    power(fs, 6)
                    if half == 0:
                        sum_squares(n + 1)

            per_pair(pe, body)

        @block.scalar
        def _(act):
            a = nc.scalar

            def take_raw(m, i):
                pe_done = ("projected_kq", "projected_v")[i]
                act.wait_ge(s[pe_done], m + 1)
                act.wait_ge(s["hist_done"], m + 1)
                a.copy(raw[:, 2 * i:2 * i + 2, :, TAPS - 1:],
                       bank[i][:].rearrange("p (t b x) -> p t b x", t=2, b=B)).then_inc(s["raw_in"], 1)
                act.wait_ge(s["raw_in"], 2 * m + i + 1)
                for t in (2 * i, 2 * i + 1):
                    a.activation(conv[:, t], raw[:, t, :, 0:BLK], ACT.Copy, scale=conv_w[:, t, 0:1]).then_inc(s["tap_in"], 1)

            def tanh_conv(m, i):
                act.wait_ge(s["conv_steps"], 12 * m + 6 * i + 6)
                a.activation(th[:, 2 * i:2 * i + 2], conv[:, 2 * i:2 * i + 2], ACT.Tanh, scale=0.5).then_inc(s["conv_tanhed"], 1)

            def tanh_z(m):
                act.wait_ge(s["projected_z"], m + 1)
                a.activation(thz[:], bank[0][:], ACT.Tanh, scale=0.5).then_inc(s["z_tanhed"], 1)

            def decays(m):
                act.wait_ge(s["dec_args"], m + 1)
                a.activation(dec[:], dec_arg[:], ACT.Exp).then_inc(s["decayed"], 1)

            def token_major(st, p):
                act.wait_ge(s["turned"], st + 1)
                act.wait_ge(s["cols_ready"], st + 1)
                for b in range(B):
                    mm = a.activation(vb[:, p, b], bank[2][:, (2 + b) * P:(3 + b) * P], ACT.Copy, scale=v_scale[:, p, b:b + 1])
                mm.then_inc(s["vb_out"], 1)
                for b in range(B):
                    mm = a.activation(kdec[:, p, b], bank[2][:, b * P:(b + 1) * P], ACT.Copy, scale=k_tail[:, p, b:b + 1])
                mm.then_inc(s["vb_out"], 1)

            def take_u(st):
                act.wait_ge(s["u_turned"], st + 1)
                a.copy(UL[:, 0, :, 0], bank[4][:, 0:B * P].rearrange("p (b x) -> p b x", b=B)[:, :, 0:C]).then_inc(s["u_out"], 1)

            def take_ul(st, i):
                act.wait_ge(s["squared"], 5 * st + i)
                if i == 2:
                    act.wait_ge(s["p1_ready"], st + 1)
                both = bank[4][:, 0:B * P].rearrange("p (b w x) -> p b w x", b=B, w=2)
                if i < 5:
                    mm = a.copy(UL[:, i % 2], both)
                else:
                    mm = a.copy(UL[:, 1, :, 1], both[:, :, 1])
                mm.then_inc(s["ul_out"], 1)

            def take_values(st):
                act.wait_ge(s["vt_done"], st + 1)
                a.copy(vt[:].rearrange("p b d -> p (b d)"), bank[7][:, 0:B * D]).then_inc(s["vt_out"], 1)

            def core_squares(st):
                act.wait_ge(s["core_done"], st + 1)
                for b in range(B):
                    mm = a.activation(squares[:, b], bank[7][:, b * D:(b + 1) * D], ACT.Square, accum_out=core_ss[:, b:b + 1])
                    mm.then_inc(s["squares_out"], 1)

            def core_scaled(st):
                act.wait_ge(s["f_ready"], st + 2)
                for b in range(B):
                    mm = a.activation(core_n[:, b], bank[7][:, b * D:(b + 1) * D], ACT.Copy, scale=core_f[:, b:b + 1])
                mm.then_inc(s["core_out"], 1)

            act.wait_ge(s["conv_w_in"], 16)
            take_raw(0, 0)
            take_raw(0, 1)
            tanh_conv(0, 0)
            tanh_conv(0, 1)
            tanh_z(0)
            decays(0)
            take_u(0)
            take_ul(0, 1)
            token_major(0, 0)
            for i in range(2, 6):
                take_ul(0, i)

            def body(pair, rr, n, last):
                for half in range(2):
                    st, fs, fp = 2 * n + half, 2 * n + half + 1, 1 - half
                    if half == 0:
                        if last:
                            act.wait_ge(s["conv_w_in"], 16 * (pair + 2))
                        take_raw(n + 1, 0)
                    take_u(fs)
                    take_values(st)
                    take_ul(fs, 1)
                    core_squares(st)
                    core_scaled(st)
                    take_ul(fs, 2)
                    if half == 0:
                        take_raw(n + 1, 1)
                    take_ul(fs, 3)
                    token_major(fs, fp)
                    if half == 0:
                        tanh_conv(n + 1, 0)
                    take_ul(fs, 4)
                    if half == 1:
                        tanh_z(n + 1)
                    take_ul(fs, 5)
                    if half == 0:
                        tanh_conv(n + 1, 1)
                        decays(n + 1)

            per_pair(act, body)

        @block.vector
        def _(dve):
            v = nc.vector

            def convolve(m, i, t2):
                t = 2 * i + t2
                dve.wait_ge(s["tap_in"], 4 * m + t + 1)
                for w in range(1, TAPS):
                    if w > 1:
                        dve.wait_ge(s["conv_steps"], 12 * m + 3 * t + w - 1)
                    v.scalar_tensor_tensor(out=conv[:, t], in0=raw[:, t, :, w:w + BLK], scalar=conv_w[:, t, w:w + 1],
                                           in1=conv[:, t], op0=ALU.mult, op1=ALU.add).then_inc(s["conv_steps"], 1)

            def silu(m, i):
                dve.wait_ge(s["conv_tanhed"], 2 * m + i + 1)
                f = lambda t: t[:, 2 * i:2 * i + 2].rearrange("p t b x -> p (t b x)")
                v.scalar_tensor_tensor(out=f(kqv), in0=f(th), scalar=1.0, in1=f(conv), op0=ALU.add,
                                       op1=ALU.mult).then_inc(s["kqv_ready"], 1)

            def silu_z(m):
                dve.wait_ge(s["z_tanhed"], m + 1)
                if not at_start(m):
                    dve.wait_ge(s["gated_out"], 2 * m)
                v.scalar_tensor_tensor(out=zs[:].rearrange("p u b x -> p (u b x)"), in0=thz[:].rearrange("p u b x -> p (u b x)"),
                                       scalar=1.0, in1=bank[0][:], op0=ALU.add, op1=ALU.mult).then_inc(s["z_ready"], 1)

            def take_ssq(m):
                dve.wait_ge(s["ssq_summed"], m + 1)
                v.tensor_scalar(ssq[:].rearrange("p k s b -> p (k s b)"), bank[1][:, 0:4 * B], 4e-24, None,
                                ALU.max).then_inc(s["ssq_out"], 1)

            def make_l(st, p):
                dve.wait_ge(s["grammed"], st + 1)
                dve.wait_ge(s["cols_ready"], st + 1)
                for b in range(B):
                    mm = v.scalar_tensor_tensor(out=UL[:, 0, b, 1], in0=bank[3][:, b * P:b * P + C], scalar=l_scale[:, p, b:b + 1],
                                                in1=dec[:, 0, p, b], op0=ALU.mult, op1=ALU.mult)
                mm.then_inc(s["l_ready"], 1)
                v.tensor_tensor(attnT[:, p], bank[3][:, 0:B * P].rearrange("p (b x) -> p b x", b=B)[:, :, C:],
                                dec[:, 1, p], ALU.mult).then_inc(s["attn_ready"], 1)

            def take_p(st, i, p):
                dve.wait_ge(s["powered"], 5 * st + i - 1)
                out = inv[:, p] if i == 6 else prod[:, (i + 1) % 2]
                v.tensor_tensor(out, bank[5][:, 0:B * C].rearrange("p (b x) -> p b x", b=B), prod[:, i % 2],
                                ALU.add).then_inc(s["p_out"], 1)

            def make_r(st, p):
                dve.wait_ge(s["ks_done"], st + 1)
                dve.wait_ge(s["vb_out"], 2 * st + 1)
                for b in range(B):
                    mm = v.scalar_tensor_tensor(out=r[:, b], in0=bank[6][:, b * D:(b + 1) * D], scalar=ks_scale[:, p, b:b + 1],
                                                in1=vb[:, p, b], op0=ALU.mult, op1=ALU.add)
                mm.then_inc(s["r_ready"], 1)

            def update(st, reset):
                if reset:
                    dve.wait_ge(s["grown_1"], st + 1)
                    dve.wait_ge(s["s_decayed"], st + 1)
                    v.memset(state[:], 0.0).then_inc(s["s_updated"], 1)
                    return
                dve.wait_ge(s["s_decayed"], st + 1)
                for u, bk in ((0, 3), (1, 6)):
                    dve.wait_ge(s[f"grown_{u}"], st + 1)
                    mm = v.tensor_tensor(state[:, :, u], bank[bk][:, 0:B * D].rearrange("p (b d) -> p b d", b=B),
                                         state_d[:, :, u], ALU.add)
                mm.then_inc(s["s_updated"], 1)

            def gate(st, p):
                dve.wait_ge(s["core_turned"], st + 1)
                v.scalar_tensor_tensor(out=gated[:].rearrange("p u b i -> p (u b) i"),
                                       in0=bank[6][:, 0:2 * P].rearrange("p (q i) -> p q i", i=C), scalar=k.half_norm_w[:],
                                       in1=zs[:, :, :, p * C:(p + 1) * C].rearrange("p u b i -> p (u b) i"),
                                       op0=ALU.mult, op1=ALU.mult).then_inc(s["gated_out"], 1)

            def add_y(st, chunk):
                dve.wait_ge(s["y_projected"], st + 1)
                y = k.y_sum[:, bass.ds(chunk, 1)].rearrange("p o h -> p (o h)")
                v.tensor_tensor(y, bank[6][:, 0:H], y, ALU.add).then_inc(s["y_added"], 1)

            v.memset(k.y_sum[:], 0.0)
            v.memset(state[:], 0.0).then_inc(s["s_updated"], 1)
            v.memset(credits[:, 4:5], 0.0).then_inc(s["y_added"], 1)
            v.memset(credits[:, 5:6], 0.0).then_inc(s["p_out"], 1)
            dve.wait_ge(s["conv_w_in"], 16)
            for i in range(2):
                for t2 in range(2):
                    convolve(0, i, t2)
            silu(0, 0)
            silu(0, 1)
            silu_z(0)
            take_ssq(0)
            dve.wait_ge(s["decayed"], 1)
            make_l(0, 0)
            for i in range(2, 7):
                take_p(0, i, 0)

            def body(pair, rr, n, last):
                for half in range(2):
                    st, fs, p, fp = 2 * n + half, 2 * n + half + 1, half, 1 - half
                    if half == 1:
                        dve.wait_ge(s["decayed"], n + 2)
                    make_l(fs, fp)
                    make_r(st, p)
                    if half == 0:
                        convolve(n + 1, 0, 0)
                    take_p(fs, 2, fp)
                    update(st, last and half == 1)
                    if half == 0:
                        convolve(n + 1, 0, 1)
                    take_p(fs, 3, fp)
                    gate(st, p)
                    if half == 0:
                        convolve(n + 1, 1, 0)
                        dve.wait_ge(s["turned"], fs + 1)
                        dve.wait_ge(s["qg_ready"], fs + 1)
                        silu(n + 1, 0)
                    take_p(fs, 4, fp)
                    if half == 1:
                        silu_z(n + 1)
                    add_y(st, 2 * rr + half)
                    if half == 0:
                        convolve(n + 1, 1, 1)
                    take_p(fs, 5, fp)
                    take_p(fs, 6, fp)
                    if half == 0:
                        silu(n + 1, 1)
                        take_ssq(n + 1)

            per_pair(dve, body)

        @block.gpsimd
        def _(pool):
            g = nc.gpsimd

            def ready():
                pool.wait_ge(s["started"], 1)

            def history(m, reset):
                if reset:
                    mm = g.memset(raw[:, :, :, 0:TAPS - 1], 0.0)
                else:
                    mm = g.tensor_copy(raw[:, :, :, 0:TAPS - 1], raw[:, :, :, BLK:])
                mm.then_inc(s["hist_done"], 1)

            def gate_differences(m):
                pool.wait_ge(s["g_in"], 32 * m + 32)
                for p in range(2):
                    col = k.g_col[:, bass.ds(2 * m + p, 1)].rearrange("p o b -> p (o b)")
                    mm = g.tensor_tensor(g_diff[:, p], g_blk[:, :, p * C:(p + 1) * C],
                                         col.unsqueeze(2).broadcast_to([P, B, C]), ALU.subtract)
                mm.then_inc(s["diffed"], 1)
                pool.wait_ge(s["diffed"], m + 1)
                rows = g_diff[:].rearrange("p s b x -> p (s b) x")
                wide = [P, 2 * B, C]
                g.tensor_tensor(dec_arg[:, 0].rearrange("p s b x -> p (s b) x"), k.mask_l[:].unsqueeze(1).broadcast_to(wide), rows,
                                ALU.subtract)
                g.tensor_tensor(dec_arg[:, 1].rearrange("p s b x -> p (s b) x"), k.mask_u[:].unsqueeze(1).broadcast_to(wide), rows,
                                ALU.add).then_inc(s["dec_args"], 1)

            def square_kq(m):
                pool.wait_ge(s["kqv_ready"], 2 * m + 1)
                kq = kqv[:, K_:Q_ + 1]
                g.tensor_tensor(sq[:], kq, kq, ALU.mult).then_inc(s["kq_squared"], 1)

            def norms(m):
                pool.wait_ge(s["ssq_out"], m + 1)
                g.tensor_tensor(rn[:].rearrange("p k s b -> p (k s b)"), ssq[:].rearrange("p k s b -> p (k s b)"),
                                k.pow_half[:], ALU.pow).then_inc(s["rn_ready"], 1)
                pool.wait_ge(s["rn_ready"], m + 1)
                g.tensor_tensor(rn2[:], rn[:, 0], rn[:, 0], ALU.mult).then_inc(s["rn2_ready"], 1)

            def front(st, m, p):
                values, turns = in_register(pool, 2 * m + 2), in_register(pool, st)
                ready()
                pool.wait_ge(s["kqv_ready"], values)
                for b in range(B):
                    mm = g.tensor_copy(kc[:, p, b], twice(kqv[:, K_, b, p * C:(p + 1) * C]))
                mm.then_inc(s["kc_ready"], 1)
                if not at_start(st):
                    ready()
                    pool.wait_ge(s["turned"], turns)
                for b in range(B):
                    mm = g.tensor_copy(vc[:, b], kqv[:, V_:V_ + 2, b, p * C:(p + 1) * C])
                mm.then_inc(s["vc_ready"], 1)
                pool.wait_ge(s["rn2_ready"], m + 1)
                if not at_start(st):
                    pool.wait_ge(s["f_ready"], st)
                col = lambda t: t[:, bass.ds(st, 1)].rearrange("p o b -> p (o b)")
                g.tensor_tensor(l_scale[:, p], rn2[:, p], col(k.minus_beta), ALU.mult)
                g.tensor_tensor(ks_scale[:, p], rn2[:, p], col(k.minus_beta_eg), ALU.mult)
                g.tensor_tensor(v_scale[:, p], rn[:, 0, p], col(k.half_beta), ALU.mult)
                g.tensor_copy(k_tail[:, p], col(k.tail_col))
                g.tensor_scalar(q_scale[:, p], rn[:, 1, p], D ** -0.5, None, ALU.mult).then_inc(s["q_steps"], 1)
                scaled, loaded = in_register(pool, st + 1), in_register(pool, 32 * m + 32)
                ready()
                pool.wait_ge(s["q_steps"], scaled)
                pool.wait_ge(s["e_in"], loaded)
                g.tensor_copy(s_dec[:, p], e_blk[:, :, :, p * C + C - 1].rearrange("p u b -> p b u"))
                g.tensor_tensor(q_scale2[:, p], q_scale[:, p], q_scale[:, p], ALU.mult).then_inc(s["cols_ready"], 1)
                for b in range(B):
                    mm = g.tensor_tensor(qg[:, p, b], twice(kqv[:, Q_, b, p * C:(p + 1) * C]), e_blk[:, :, b, p * C:(p + 1) * C], ALU.mult)
                mm.then_inc(s["qg_ready"], 1)

            def first_product(st):
                pool.wait_ge(s["p_out"], 5 * st + 1)
                pool.wait_ge(s["u_out"], st + 1)
                mm = g.tensor_tensor(prod[:, 0], UL[:, 0, :, 0], k.ident_half[:].unsqueeze(1).broadcast_to([P, B, C]), ALU.add)
                mm.then_inc(s["p1_ready"], 1)

            def decay_state(st, p):
                pool.wait_ge(s["s_updated"], st + 1)
                pool.wait_ge(s["cols_ready"], st + 1)
                f = lambda t: t[:].rearrange("p b u d -> p (b u) d")
                g.tensor_tensor(f(state_d), f(state), s_dec[:, p].rearrange("p b u -> p (b u)").unsqueeze(2).broadcast_to([P, 2 * B, D]),
                                ALU.mult).then_inc(s["s_decayed"], 1)

            def rms_factor(st, p):
                pool.wait_ge(s["squares_out"], 2 * st + 2)
                g.tensor_tensor(core_ms[:], core_ss[:], q_scale2[:, p], ALU.mult).then_inc(s["f_steps"], 1)
                first = in_register(pool, 3 * st + 1)
                ready()
                pool.wait_ge(s["f_steps"], first)
                g.tensor_scalar(core_var[:], core_ms[:], 1.0 / D, EPS_RMS, ALU.mult, ALU.add).then_inc(s["f_steps"], 1)
                pool.wait_ge(s["f_steps"], 3 * st + 2)
                g.tensor_tensor(core_rs[:], core_var[:], k.pow_half[:, 0:B], ALU.pow).then_inc(s["f_steps"], 1)
                pool.wait_ge(s["f_steps"], 3 * st + 3)
                g.tensor_tensor(core_f[:], core_rs[:], q_scale[:, p], ALU.mult).then_inc(s["f_ready"], 1)

            g.memset(credits[:, 0:1], 0.0).then_inc(s["f_ready"], 1)
            g.memset(credits[:, 1:2], 0.0).then_inc(s["ul_out"], 1)
            g.memset(credits[:, 2:3], 0.0).then_inc(s["core_out"], 1)
            g.memset(credits[:, 3:4], 0.0).then_inc(s["started"], 1)
            history(0, True)
            gate_differences(0)
            square_kq(0)
            norms(0)
            front(0, 0, 0)
            first_product(0)

            def body(pair, rr, n, last):
                for half in range(2):
                    st, fs, p, fp = 2 * n + half, 2 * n + half + 1, half, 1 - half
                    decay_state(st, p)
                    if half == 0:
                        taps = in_register(pool, 12 * n + 12)
                        ready()
                        pool.wait_ge(s["conv_steps"], taps)
                        history(n + 1, last)
                    front(fs, n + half, fp)
                    first_product(fs)
                    rms_factor(st, p)
                    if half == 0:
                        pool.wait_ge(s["attn_ready"], fs + 1)
                        gate_differences(n + 1)
                        square_kq(n + 1)
                        norms(n + 1)

            per_pair(pool, body)


class Kept:

    def __init__(self, ctx, nc):
        def sb(name, shape):
            return ctx.enter_context(nc.sbuf_tensor(name, shape, F32))

        self.x_tok = sb("x_tok", [P, NC, H])
        self.y_sum = sb("y_sum", [P, NC, H])
        self.xT = sb("xT", [P, KT, NC, B, C])
        self.ident = sb("ident", [P, P])
        self.ident_half = sb("ident_half", [P, C])
        self.ones_col = sb("ones_col", [P, 1])
        self.pow_half = sb("pow_half", [P, 4 * B])
        self.mask_l = sb("mask_l", [P, C])
        self.mask_u = sb("mask_u", [P, C])
        self.half_norm_w = sb("half_norm_w", [P, 1])
        self.g_col = sb("g_col", [P, NSTEPS + 2, B])
        self.tail_col = sb("tail_col", [P, NSTEPS + 2, B])
        self.half_beta = sb("half_beta", [P, NSTEPS + 2, B])
        self.minus_beta = sb("minus_beta", [P, NSTEPS + 2, B])
        self.minus_beta_eg = sb("minus_beta_eg", [P, NSTEPS + 2, B])
        self.token_rows = nc.dram_tensor("token_rows", (TOKENS, H + E), F32, kind="Internal").ap()
        self.tables = [nc.dram_tensor(f"table{t}", (TOKENS + CAP, H), F32, kind="Internal").ap() for t in range(NTAB)]
        self.slots = ctx.enter_context(nc.sbuf_tensor("slots", [CAP, E, 2], U32))
        self.g_rows = nc.dram_tensor("g_rows", (NK + 1, 2, NB, B, BLK), F32, kind="Internal").ap()
        self.e_rows = nc.dram_tensor("e_rows", (NK + 1, 2, NB, B, BLK), F32, kind="Internal").ap()


def by_token(rows):
    return rows[0:TOKENS].rearrange("(b c i) h -> b i c h", b=B, i=C)


def route(nc, io, k):
    with ExitStack() as ctx:
        def sb(name, shape, dt=F32):
            return ctx.enter_context(nc.sbuf_tensor(name, shape, dt))

        ps = [ctx.enter_context(nc.psum_tensor(f"route_bank{i}", [P, 512], F32)) for i in range(8)]
        rows = sb("rows", [P, NC, H + E])
        hn, weights = rows[:, :, 0:H], rows[:, :, H:]
        gate_w = sb("gate_w", [P, KT, E])
        bias = sb("bias", [P, E])
        per_expert = [P, NC, E]
        scores, biased, a_, b_, c_, sel, pos = (sb(n, per_expert) for n in ("scores", "biased", "work_a", "work_b", "work_c", "sel", "pos"))
        sel16 = sb("sel16", per_expert, F16)
        per_group = [P, NC, EG]
        m1, m2, cnt, gscore, rank = (sb(n, per_group) for n in ("m1", "m2", "cnt", "gscore", "rank"))
        before = sb("before", [P, EG, EG])
        resets = sb("resets", per_expert)
        top8 = sb("top8", [P, NC, 8])
        above, wsum, winv = sb("above", [P, NC]), sb("wsum", [P, NC]), sb("winv", [P, NC])
        earlier = sb("earlier", [P, NC + 1, E])
        tri16, halves16, cross16 = (sb(n, [P, P], F16) for n in ("tri16", "halves16", "cross16"))
        slot_no = sb("slot_no", [P, CAP])
        onehot = sb("onehot", [P, 2, E, CAP], F16)
        token_no = sb("token_no", [P, NC])
        token16 = sb("token16", [P, NC], F16)
        found_row = sb("found_row", [1, E * CAP])
        found = sb("found", [CAP, E])
        empty, spare = sb("empty", [CAP, E]), sb("spare", [CAP, 1])
        ln1, ln2 = LayerNorm(ctx, nc, "ln_attn"), LayerNorm(ctx, nc, "ln_mid")
        s = sems(ctx, nc, """loaded added consts consts_ready turned copied logits scored step top_done sel_ready counted 
            ranks_ready onehot_ready matched row_out spread rows_ready rows_out """)
        rows_of = lambda ap: ap.rearrange("p c e -> p (c e)")
        by_group = lambda ap: ap.rearrange("p c (g e) -> p (c g) e", g=EG)
        wide = [P, NC * EG, E // EG]

        block = ctx.enter_context(nc.Block())

        @block.sync
        def _(sp):
            sp.dma_start(gate_w[:], io["gate_w"]).then_inc(s["loaded"], 16)
            sp.dma_start(bias[:], io["bias"].partition_broadcast(P)).then_inc(s["loaded"], 16)
            sp.wait_ge(s["rows_ready"], 1)
            sp.wait_ge(ln2.sem("done"), GROUPS)
            for b in range(B):
                sp.dma_start(by_token(k.token_rows)[b], rows[u_half(b)]).then_inc(s["rows_out"], 16)
            sp.wait_ge(s["rows_out"], 32)

        @block.gpsimd
        def _(pool):
            g = nc.gpsimd
            done = [0]

            def one(ins):
                ins.then_inc(s["consts"], 1)
                done[0] += 1
                pool.wait_ge(s["consts"], done[0])

            one(g.memset(tri16[:], 1.0))
            one(g.affine_select(out=tri16[:], in_=tri16[:], compare_op=ALU.is_gt, fill=0.0, base=0, pattern=[[1, P]],
                                channel_multiplier=-1))
            one(g.memset(tri16[0:C, C:P], 0.0))
            one(g.memset(halves16[:], 0.0))
            one(g.memset(halves16[0:C, 0:C], 1.0))
            one(g.memset(halves16[C:P, C:P], 1.0))
            one(g.memset(cross16[:], 0.0))
            one(g.memset(cross16[0:C, C:P], 1.0))
            one(g.memset(before[:], 1.0))
            one(g.affine_select(out=before[:], in_=before[:], compare_op=ALU.is_gt, fill=0.0, base=0, pattern=[[1, EG], [-1, EG]],
                                channel_multiplier=0))
            one(g.memset(resets[:], 1.0))
            one(g.memset(resets[:, :, 0:1], 0.0))
            one(g.iota(slot_no[:], pattern=[[1, CAP]], base=0, channel_multiplier=0, allow_small_or_imprecise_dtypes=True))
            for b in range(B):
                one(g.iota(token_no[u_half(b)], pattern=[[C, NC]], base=1 + b * S, channel_multiplier=1,
                           allow_small_or_imprecise_dtypes=True))
            one(g.tensor_copy(token16[:], token_no[:]))
            one(g.iota(spare[:], pattern=[[0, 1]], base=TOKENS, channel_multiplier=1, allow_small_or_imprecise_dtypes=True))
            g.memset(earlier[:, 0:1], 0.0).then_inc(s["consts_ready"], 1)
            ln1.gpsimd(pool)
            ln2.gpsimd(pool)

        @block.scalar
        def _(act):
            a = nc.scalar
            ln1.scalar(act, hn)
            ln2.scalar(act, hn)
            for c in range(NC):
                act.wait_ge(s["turned"], c + 1)
                a.copy(k.xT[:, :, c], ps[c % 2][:, 0:KT * P].rearrange("p (k b i) -> p k b i", k=KT, b=B)).then_inc(s["copied"], 1)
            act.wait_ge(s["logits"], 1)
            for i in range(2):
                mm = a.activation(scores[:, i * 8:(i + 1) * 8], ps[2 + i][:].rearrange("p (c e) -> p c e", e=E), ACT.Sigmoid)
            mm.then_inc(s["scored"], 1)

        @block.tensor
        def _(pe):
            te = nc.tensor
            for c in range(NC):
                if c >= 2:
                    pe.wait_ge(s["copied"], c - 1)
                pe.wait_ge(ln2.sem("done"), c // GC + 1)
                for kt in range(KT):
                    mm = te.transpose(ps[c % 2][:, kt * P:(kt + 1) * P], hn[:, c, kt * P:(kt + 1) * P], k.ident[:])
                mm.then_inc(s["turned"], 1)
            pe.wait_ge(s["copied"], NC)
            pe.wait_ge(s["loaded"], 32)
            for c in range(NC):
                for kt in range(KT):
                    mm = te.matmul(ps[2 + c // 8][:, (c % 8) * E:(c % 8 + 1) * E], k.xT[:, kt, c].rearrange("p b i -> p (b i)"),
                                   gate_w[:, kt], start=(kt == 0), stop=(kt == KT - 1))
            mm.then_inc(s["logits"], 1)
            pe.wait_ge(s["sel_ready"], 1)
            pe.wait_ge(s["consts_ready"], 1)
            for i in range(2):
                r16 = rows_of(sel16[:])[:, i * 512:(i + 1) * 512]
                te.matmul(ps[4 + i][:], tri16[:], r16, start=True, stop=True)
                te.matmul(ps[6 + i][:], halves16[:], r16, start=True, stop=True)
            for c in range(NC):
                mm = te.matmul(ps[0][:, 0:E], cross16[:], sel16[:, c], start=(c == 0), stop=(c == NC - 1))
            mm.then_inc(s["counted"], 1)
            pe.wait_ge(s["ranks_ready"], 1)
            for c in range(NC):
                pe.wait_ge(s["onehot_ready"], c + 1)
                flat = onehot[:, c % 2].rearrange("p e s -> p (e s)")
                for q in range(6):
                    mm = te.matmul(ps[q][0:1, :], token16[:, c:c + 1], flat[:, q * 512:(q + 1) * 512], start=(c == 0), stop=(c == NC - 1))
                mm.then_inc(s["matched"], 1)
            pe.wait_ge(s["row_out"], 6)
            for e in range(E):
                mm = te.matmul(ps[6][0:CAP, e:e + 1], found_row[:, e * CAP:(e + 1) * CAP], k.ones_col[0:1], start=True, stop=True)
            mm.then_inc(s["spread"], 1)

        @block.vector
        def _(dve):
            v = nc.vector
            done = [0]

            def one(ins):
                ins.then_inc(s["step"], 1)
                done[0] += 1
                dve.wait_ge(s["step"], done[0])

            ln1.vector(dve, k.y_sum, hn)
            for g in range(GROUPS):
                a = slice(g * GC, (g + 1) * GC)
                dve.wait_ge(ln1.sem("done"), g + 1)
                v.tensor_tensor(k.x_tok[:, a], k.x_tok[:, a], hn[:, a], ALU.add).then_inc(s["added"], 1)
            ln2.vector(dve, k.x_tok, hn, lambda g: dve.wait_ge(s["added"], g + 1))
            dve.wait_ge(s["loaded"], 32)
            dve.wait_ge(s["scored"], 1)
            dve.wait_ge(s["consts_ready"], 1)
            one(v.tensor_tensor(biased[:], scores[:], bias[:].unsqueeze(1).broadcast_to(per_expert), ALU.add))
            gflat = lambda ap: ap.rearrange("p c g -> p (c g)")
            over = lambda ap: gflat(ap).unsqueeze(2).broadcast_to(wide)
            one(v.tensor_reduce(gflat(m1[:]), by_group(biased[:]), AX.X, ALU.max))
            one(v.tensor_tensor(by_group(a_[:]), by_group(biased[:]), over(m1[:]), ALU.is_equal))
            one(v.tensor_reduce(gflat(cnt[:]), by_group(a_[:]), AX.X, ALU.add))
            one(v.scalar_tensor_tensor(out=rows_of(b_[:]), in0=rows_of(a_[:]), scalar=NEG, in1=rows_of(biased[:]), op0=ALU.mult, op1=ALU.add))
            one(v.tensor_reduce(gflat(m2[:]), by_group(b_[:]), AX.X, ALU.max))
            one(v.tensor_scalar(cnt[:], cnt[:], 2.0, -2.0 * NEG, ALU.is_ge, ALU.mult))
            one(v.tensor_scalar(cnt[:], cnt[:], NEG, None, ALU.add))
            one(v.tensor_tensor(cnt[:], cnt[:], m1[:], ALU.min))
            one(v.tensor_tensor(m2[:], m2[:], cnt[:], ALU.max))
            one(v.tensor_tensor(gscore[:], m1[:], m2[:], ALU.add))
            pairs = [P, NC, EG, EG]
            as_pairs = lambda ap: ap.rearrange("p c (g h) -> p c g h", g=EG)
            other, own = gscore[:].unsqueeze(2).broadcast_to(pairs), gscore[:].unsqueeze(3).broadcast_to(pairs)
            one(v.tensor_tensor(as_pairs(a_[:]), other, own, ALU.is_gt))
            one(v.tensor_tensor(as_pairs(b_[:]), other, own, ALU.is_equal))
            one(v.tensor_tensor(b_[:], b_[:], before[:].rearrange("p g h -> p (g h)").unsqueeze(1).broadcast_to(per_expert), ALU.mult))
            one(v.tensor_tensor(a_[:], a_[:], b_[:], ALU.add))
            one(v.tensor_reduce(gflat(rank[:]), a_[:].rearrange("p c (g h) -> p (c g) h", g=EG), AX.X, ALU.add))
            one(v.tensor_scalar(rank[:], rank[:], float(KG), NEG, ALU.is_ge, ALU.mult))
            one(v.tensor_tensor(by_group(c_[:]), by_group(biased[:]), over(rank[:]), ALU.add))
            for c in range(NC):
                v.max(out=top8[:, c], in_=c_[:, c]).then_inc(s["top_done"], 1)
            dve.wait_ge(s["top_done"], NC)
            least = top8[:, :, TOP - 1:TOP].broadcast_to(per_expert)
            one(v.tensor_tensor(a_[:], c_[:], least, ALU.is_gt))
            one(v.tensor_tensor(b_[:], c_[:], least, ALU.is_equal))
            one(v.tensor_reduce(above[:], a_[:], AX.X, ALU.add))
            one(v.tensor_tensor_scan(rows_of(c_[:]), rows_of(resets[:]), rows_of(b_[:]), 0.0, ALU.mult, ALU.add))
            one(v.tensor_tensor(c_[:], c_[:], above[:].unsqueeze(2).broadcast_to(per_expert), ALU.add))
            one(v.scalar_tensor_tensor(out=rows_of(b_[:]), in0=rows_of(c_[:]), scalar=float(TOP), in1=rows_of(b_[:]), op0=ALU.is_le, op1=ALU.mult))
            one(v.tensor_tensor(sel[:], a_[:], b_[:], ALU.add))
            v.tensor_copy(sel16[:], sel[:]).then_inc(s["sel_ready"], 1)
            one(v.tensor_tensor(c_[:], scores[:], sel[:], ALU.mult))
            one(v.tensor_reduce(wsum[:], c_[:], AX.X, ALU.add))
            one(v.reciprocal(winv[:], wsum[:]))
            one(v.tensor_tensor(c_[:], c_[:], winv[:].unsqueeze(2).broadcast_to(per_expert), ALU.mult))
            v.tensor_scalar(weights, c_[:], ROUTE_SCALE, None, ALU.mult).then_inc(s["rows_ready"], 1)
            dve.wait_ge(s["counted"], 1)
            one(v.tensor_copy(earlier[:, 0], ps[0][:, 0:E]))
            for c in range(NC):
                one(v.tensor_tensor(earlier[:, c + 1], ps[6 + c // 8][:, (c % 8) * E:(c % 8 + 1) * E], earlier[:, c], ALU.add))
            for i in range(2):
                a8 = slice(i * 8, (i + 1) * 8)
                mm = v.tensor_tensor(pos[:, a8], ps[4 + i][:].rearrange("p (c e) -> p c e", e=E), earlier[:, a8], ALU.add)
                one(mm)
            one(v.tensor_scalar(b_[:], sel[:], -2.0 * CAP, 2.0 * CAP, ALU.mult, ALU.add))
            v.tensor_tensor(a_[:], pos[:], b_[:], ALU.add).then_inc(s["ranks_ready"], 1)
            dve.wait_ge(s["ranks_ready"], 1)
            for c in range(NC):
                if c >= 2:
                    dve.wait_ge(s["matched"], c - 1)
                v.tensor_tensor(onehot[:, c % 2], a_[:, c].unsqueeze(2).broadcast_to([P, E, CAP]),
                                slot_no[:].unsqueeze(1).broadcast_to([P, E, CAP]), ALU.is_equal).then_inc(s["onehot_ready"], 1)
            dve.wait_ge(s["matched"], NC)
            for q in range(6):
                v.tensor_copy(found_row[:, q * 512:(q + 1) * 512], ps[q][0:1, :]).then_inc(s["row_out"], 1)
            dve.wait_ge(s["spread"], 1)
            one(v.tensor_copy(found[:], ps[6][0:CAP, 0:E]))
            one(v.tensor_scalar(k.slots[:, :, 0], found[:], -1.0, 0.0, ALU.add, ALU.max))
            one(v.tensor_scalar(spare[:], spare[:], 1.0, None, ALU.add))
            one(v.tensor_scalar(empty[:], found[:], 0.0, spare[:], ALU.is_equal, ALU.mult))
            one(v.scalar_tensor_tensor(out=k.slots[:, :, 1], in0=found[:], scalar=-1.0, in1=empty[:], op0=ALU.add, op1=ALU.add))


def experts(nc, io, k):
    with ExitStack() as ctx:
        def sb(name, shape, dt=F32):
            return ctx.enter_context(nc.sbuf_tensor(name, shape, dt))

        ps = [ctx.enter_context(nc.psum_tensor(f"moe_bank{i}", [P, 512], F32)) for i in range(8)]
        wsg, wsu, wsd = sb("wsg", [P, KT, F]), sb("wsu", [P, KT, F]), sb("wsd", [F, H])
        w_in = sb("w_gate_up", [P, NTAB, 2, KT, F])
        w_down = sb("w_down", [F, NTAB, H])
        at = sb("slot_rows", [CAP, NTAB, 2], U32)
        xg = sb("gathered", [CAP, NTAB, H + E])
        xgT = sb("gatheredT", [P, 2, KT, CAP])
        act_g = sb("act_g", [F, 2, CAP])
        hidden = sb("hidden", [F, 2, CAP])
        scaled = sb("scaled", [CAP, NTAB, H])
        credit = sb("credit", [1, 1])
        sh_g = sb("sh_g", [F, 2, 512])
        sh_h = sb("sh_h", [F, 2, 512])
        s = sems(ctx, nc, "sh_in pool_started sh_up sh_silu sh_hidden sh_down sh_out located " +
                 "turned turn_out upped silued multiplied downed weighted " +
                 " ".join(f"w_in_{t} gathered_{t} added_{t}" for t in range(NTAB)))
        NSH = 4

        block = ctx.enter_context(nc.Block())

        @block.sync
        def _(sp):
            for dst, src in ((wsg, "ws_gate"), (wsu, "ws_up"), (wsd, "ws_down")):
                sp.dma_start(dst[:], io[src]).then_inc(s["sh_in"], 16)

            def load(e, t):
                sp.dma_start(w_in[:, t], io["w_gate_up"][bass.ds(e, 1)].rearrange("o p g k f -> (o p) g k f")).then_inc(s[f"w_in_{t}"], 16)
                sp.dma_start(w_down[:, t], io["w_down"][bass.ds(e, 1)].rearrange("o f h -> (o f) h")).then_inc(s[f"w_in_{t}"], 16)

            for t in range(NTAB):
                load(t, t)
            with sp.Fori(0, E // NTAB - 1) as r:
                for t in range(NTAB):
                    sp.wait_ge(s["downed"], r * NTAB + t + 1)
                    load(r * NTAB + NTAB + t, t)
            for t in range(NTAB):
                sp.wait_ge(s[f"w_in_{t}"], 32 * (E // NTAB))

        @block.gpsimd
        def _(pool):
            g = nc.gpsimd

            def gather(e, r, t):
                g.tensor_copy(at[:, t], k.slots[:, bass.ds(e, 1)].rearrange("p o w -> p (o w)")).then_inc(s["located"], 1)
                made = in_register(pool, e + 1)
                pool.wait_ge(s["pool_started"], 1)
                pool.wait_ge(s["located"], made)
                g.indirect_dma_start(xg[:, t], None, k.token_rows, bass.IndirectOffsetOnAxis(ap=at[:, t, 0:1], axis=0),
                                     bounds_check=TOKENS - 1, oob_is_err=True).then_inc(s[f"gathered_{t}"], 16)

            def add(e, r, t):
                done = in_register(pool, e + 2)
                pool.wait_ge(s["pool_started"], 1)
                pool.wait_ge(s["weighted"], done)
                g.indirect_dma_start(k.tables[t], bass.IndirectOffsetOnAxis(ap=at[:, t, 1:2], axis=0), scaled[:, t], None,
                                     bounds_check=TOKENS + CAP - 1, oob_is_err=True, compute_op=ALU.add).then_inc(s[f"added_{t}"], 16)

            g.memset(credit[:], 0.0).then_inc(s["pool_started"], 1)
            for t in range(NTAB):
                gather(t, 0, t)
            with pool.Fori(0, E // NTAB - 1) as r:
                for t in range(NTAB):
                    add(r * NTAB + t, r, t)
                for t in range(NTAB):
                    landed = in_register(pool, 16 * (r + 1))
                    pool.wait_ge(s["pool_started"], 1)
                    pool.wait_ge(s[f"added_{t}"], landed)
                    gather(r * NTAB + NTAB + t, r + 1, t)
            for t in range(NTAB):
                add(E - NTAB + t, E // NTAB - 1, t)
            for t in range(NTAB):
                pool.wait_ge(s[f"added_{t}"], 16 * (E // NTAB))

        def per_expert(eng, body):
            with eng.Fori(0, E // NTAB) as r:
                for t in range(NTAB):
                    body(r * NTAB + t, r, t)

        @block.tensor
        def _(pe):
            te = nc.tensor
            pe.wait_ge(s["sh_in"], 48)
            for q in range(NSH):
                if q >= 2:
                    pe.wait_ge(s["sh_hidden"], q - 1)
                for g, w in enumerate((wsg, wsu)):
                    for kt in range(KT):
                        mm = te.matmul(ps[2 * (q % 2) + g][0:F, :], w[:, kt], k.xT[:, kt, 4 * q:4 * q + 4].rearrange("p c b i -> p (c b i)"),
                                       start=(kt == 0), stop=(kt == KT - 1))
                mm.then_inc(s["sh_up"], 1)
                pe.wait_ge(s["sh_hidden"], q + 1)
                for c in range(4):
                    n = 4 * q + c
                    if n >= 2:
                        pe.wait_ge(s["sh_out"], n - 1)
                    te.matmul(ps[4 + n % 2][:, 0:H], sh_h[:, q % 2, c * P:(c + 1) * P], wsd[:], start=True, stop=True).then_inc(s["sh_down"], 1)
            pe.wait_ge(s["sh_out"], NC)

            def body(e, r, t):
                w = t % 2
                landed, before = in_register(pe, 16 * (r + 1)), in_register(pe, e)
                pe.wait_ge(s["sh_in"], 48)
                pe.wait_ge(s[f"gathered_{t}"], landed)
                pe.wait_ge(s["weighted"], before)
                for kt in range(KT):
                    mm = te.transpose(ps[w][:, kt * CAP:(kt + 1) * CAP], xg[:, t, kt * P:(kt + 1) * P], k.ident[0:CAP, 0:CAP])
                mm.then_inc(s["turned"], 1)
                pe.wait_ge(s[f"w_in_{t}"], 32 * (r + 1))
                pe.wait_ge(s["turn_out"], e + 1)
                for g in range(2):
                    for kt in range(KT):
                        mm = te.matmul(ps[2 + w][0:F, g * CAP:(g + 1) * CAP], w_in[:, t, g, kt], xgT[:, w, kt],
                                       start=(kt == 0), stop=(kt == KT - 1))
                mm.then_inc(s["upped"], 1)
                pe.wait_ge(s["multiplied"], e + 1)
                te.matmul(ps[4 + w][0:CAP, 0:H], hidden[:, w], w_down[:, t], start=True, stop=True).then_inc(s["downed"], 1)

            per_expert(pe, body)

        @block.scalar
        def _(act):
            a = nc.scalar
            for q in range(NSH):
                act.wait_ge(s["sh_up"], q + 1)
                if q >= 2:
                    act.wait_ge(s["sh_hidden"], q - 1)
                a.activation(sh_g[:, q % 2], ps[2 * (q % 2)][0:F, :], ACT.Silu).then_inc(s["sh_silu"], 1)
                for c in range(4):
                    n = 4 * q + c
                    act.wait_ge(s["sh_down"], n + 1)
                    a.copy(k.y_sum[:, n], ps[4 + n % 2][:, 0:H]).then_inc(s["sh_out"], 1)

            def body(e, r, t):
                w = t % 2
                act.wait_ge(s["turned"], e + 1)
                a.copy(xgT[:, w].rearrange("p k s -> p (k s)"), ps[w][:, 0:KT * CAP]).then_inc(s["turn_out"], 1)
                act.wait_ge(s["upped"], e + 1)
                a.activation(act_g[:, w], ps[2 + w][0:F, 0:CAP], ACT.Silu).then_inc(s["silued"], 1)

            per_expert(act, body)

        @block.vector
        def _(dve):
            v = nc.vector
            for q in range(NSH):
                dve.wait_ge(s["sh_silu"], q + 1)
                if q >= 2:
                    dve.wait_ge(s["sh_down"], 4 * (q - 1))
                v.tensor_tensor(sh_h[:, q % 2], ps[2 * (q % 2) + 1][0:F, :], sh_g[:, q % 2], ALU.mult).then_inc(s["sh_hidden"], 1)
            v.memset(sh_g[0:1, 0, 0:1], 0.0).then_inc(s["weighted"], 1)

            def body(e, r, t):
                w = t % 2
                dve.wait_ge(s["silued"], e + 1)
                v.tensor_tensor(hidden[:, w], ps[2 + w][0:F, CAP:2 * CAP], act_g[:, w], ALU.mult).then_inc(s["multiplied"], 1)
                dve.wait_ge(s["downed"], e + 1)
                v.tensor_scalar(scaled[:, t], ps[4 + w][0:CAP, 0:H], xg[:, t, bass.ds(H + e, 1)], None, ALU.mult).then_inc(s["weighted"], 1)

            per_expert(dve, body)


def combine(nc, io, k, out):
    with ExitStack() as ctx:
        def sb(name, shape, dt=F32):
            return ctx.enter_context(nc.sbuf_tensor(name, shape, dt))

        part = [sb(f"part{t}", [P, NC, H]) for t in range(NTAB)]
        ln = LayerNorm(ctx, nc, "ln_out")
        s = sems(ctx, nc, "paired sums out_ready stored " + " ".join(f"parts_in_{g}" for g in range(GROUPS)))
        block = ctx.enter_context(nc.Block())
        groups = [slice(g * GC, (g + 1) * GC) for g in range(GROUPS)]

        @block.sync
        def _(sp):
            for g, a in enumerate(groups):
                for t in range(NTAB):
                    for b in range(B):
                        sp.dma_start(part[t][u_half(b), a], by_token(k.tables[t])[b][:, a]).then_inc(s[f"parts_in_{g}"], 16)
            for g, a in enumerate(groups):
                sp.wait_ge(s["out_ready"], g + 1)
                for b in range(B):
                    sp.dma_start(out[b].rearrange("(c i) h -> i c h", i=C)[:, a], part[0][u_half(b), a]).then_inc(s["stored"], 16)
            sp.wait_ge(s["stored"], 16 * B * GROUPS)

        @block.gpsimd
        def _(pool):
            for g, a in enumerate(groups):
                pool.wait_ge(s[f"parts_in_{g}"], 16 * B * NTAB)
                nc.gpsimd.tensor_tensor(part[2][:, a], part[2][:, a], part[3][:, a], ALU.add).then_inc(s["paired"], 1)
            ln.gpsimd(pool)

        @block.scalar
        def _(act):
            ln.scalar(act, part[0])

        @block.vector
        def _(dve):
            v = nc.vector

            def add_parts(g):
                a = groups[g]
                dve.wait_ge(s[f"parts_in_{g}"], 16 * B * NTAB)
                v.tensor_tensor(part[1][:, a], part[1][:, a], part[0][:, a], ALU.add).then_inc(s["sums"], 1)
                dve.wait_ge(s["paired"], g + 1)
                v.tensor_tensor(k.y_sum[:, a], k.y_sum[:, a], part[2][:, a], ALU.add).then_inc(s["sums"], 1)
                dve.wait_ge(s["sums"], 3 * g + 2)
                v.tensor_tensor(k.y_sum[:, a], k.y_sum[:, a], part[1][:, a], ALU.add).then_inc(s["sums"], 1)
                dve.wait_ge(s["sums"], 3 * g + 3)

            ln.vector(dve, k.y_sum, part[0], add_parts)
            for g, a in enumerate(groups):
                dve.wait_ge(ln.sem("done"), g + 1)
                v.tensor_tensor(part[0][:, a], part[0][:, a], k.x_tok[:, a], ALU.add).then_inc(s["out_ready"], 1)


def build(nc, io, out):
    with ExitStack() as ctx:
        k = Kept(ctx, nc)
        setup(nc, io, k)
        delta_rule(nc, io, k, NK)
        route(nc, io, k)
        experts(nc, io, k)
        combine(nc, io, k, out)


def laid_out(v):
    import numpy as np

    qkv, z = v["L0_attn_W_qkv"], v["L0_attn_W_z"]
    key_dim = NK * D

    def tiles_of(pair):
        rows = [qkv, qkv] + [qkv] * 2 + [z] * 2
        first = [key_dim + pair * D, pair * D] + [2 * key_dim + (2 * pair + u) * D for u in range(2)] + [(2 * pair + u) * D for u in range(2)]
        return rows, first

    w_proj, conv_w, w_out = [], [], []
    for pair in [*range(NK), NK - 1]:
        rows, first = tiles_of(pair)
        w_proj.append(np.stack([w[a:a + D] for w, a in zip(rows, first)]).reshape(NT, D, KT, P).transpose(3, 2, 0, 1))
        conv_w.append(np.stack([v["L0_attn_conv_w"][a:a + D] for a in first[:4]], axis=1))
        w_out.append(v["L0_attn_W_out"][:, 2 * pair * D:(2 * pair + 2) * D].reshape(H, 2, D).transpose(2, 1, 0))
    kfirst = lambda w: w.reshape(KT, P, w.shape[-1]).transpose(1, 0, 2)
    gate_up = np.stack([v["L0_ffn_w_gate"], v["L0_ffn_w_up"]], axis=1)
    return {
        "x": v["L0_attn_x"], "w_proj": np.stack(w_proj), "conv_w": np.stack(conv_w), "w_out": np.stack(w_out),
        "w_ba": np.concatenate([v["L0_attn_W_b"], v["L0_attn_W_a"]]).reshape(2 * NV, KT, P).transpose(2, 1, 0),
        "dt_bias": v["L0_attn_dt_bias"], "A_log": v["L0_attn_A_log"], "norm_w": v["L0_attn_norm_w"].reshape(D, 1),
        "gate_w": kfirst(v["L0_ffn_gate_w"]), "bias": v["L0_ffn_bias"],
        "w_gate_up": gate_up.reshape(E, 2, KT, P, F).transpose(0, 3, 1, 2, 4), "w_down": v["L0_ffn_w_down"],
        "ws_gate": kfirst(v["L0_ffn_ws_gate"]), "ws_up": kfirst(v["L0_ffn_ws_up"]), "ws_down": v["L0_ffn_ws_down"],
    }


def kernel(**inputs):
    import numpy as np
    import concourse.bacc as bacc
    from concourse.bass_utils import run_bass_kernel_spmd

    nc = bacc.Bacc("TRN2", target_bir_lowering=False, num_devices=1)
    arrays, io = {}, {}
    for name, a in laid_out({n: np.asarray(a) for n, a in inputs.items()}).items():
        arrays[f"in_{name}"] = np.ascontiguousarray(a)
        io[name] = nc.dram_tensor(f"in_{name}", a.shape, mybir.dt.from_np(a.dtype), kind="ExternalInput").ap()
    out = nc.dram_tensor("out", (B, S, H), F32, kind="ExternalOutput").ap()
    build(nc, io, out)
    got = run_bass_kernel_spmd(nc, [arrays], core_ids=[0])
    return got.results[0]["out"]
```

```python
from contextlib import ExitStack

import concourse.bass as bass
from concourse import mybir

ALU = mybir.AluOpType
ACT = mybir.ActivationFunctionType
AX = mybir.AxisListType
F32 = mybir.dt.float32
F16 = mybir.dt.float16
U32 = mybir.dt.uint32

P = 128
B, S, H = 2, 1024, 256
KT = H // P
D = 128
NK = 16
NV = 2 * NK
C = 64
NC = S // C
BLK = 2 * C
NB = S // BLK
NSTEPS = NK * NC
TAPS = 4
K_, Q_, V_, Z_ = 0, 1, 2, 4
NT = 6
NEG = -1e30
EPS_LN, EPS_RMS = 1e-5, 1e-6
E = 64
TOP = 6
EG, KG = 8, 4
F = 96
CAP = 48
ROUTE_SCALE = 2.5
NTAB = 4
TOKENS = B * S
GROUPS = 4
GC = NC // GROUPS
ZPARTS = 8
ZCOLS = (TOKENS + CAP) // 16 * H // ZPARTS


def twice(ap):
    return ap.unsqueeze(1).broadcast_to([ap.shape[0], 2, ap.shape[1]])


def sems(ctx, nc, names):
    return {n: ctx.enter_context(nc.semaphore(n)) for n in names.split()}


def at_start(count):
    return isinstance(count, int) and count == 0


def in_register(eng, count):
    if not isinstance(count, int):
        eng.compute_val(count)
    return count


def u_half(u):
    return slice(u * C, (u + 1) * C)


class LayerNorm:

    def __init__(self, ctx, nc, name):
        self.nc = nc
        self.total = ctx.enter_context(nc.sbuf_tensor(name + "_total", [P, NC], F32))
        self.mean = ctx.enter_context(nc.sbuf_tensor(name + "_mean", [P, NC], F32))
        self.sumsq = ctx.enter_context(nc.sbuf_tensor(name + "_sumsq", [P, NC], F32))
        self.var = ctx.enter_context(nc.sbuf_tensor(name + "_var", [P, NC], F32))
        self.inv = ctx.enter_context(nc.sbuf_tensor(name + "_inv", [P, NC], F32))
        self.minus_half = ctx.enter_context(nc.sbuf_tensor(name + "_minus_half", [P, GC], F32))
        self.squares = ctx.enter_context(nc.sbuf_tensor(name + "_squares", [P, H], F32))
        self.s = sems(ctx, nc, " ".join(f"{name}_{x}" for x in "averaged centred squared inverted done".split()))
        self.name = name

    def sem(self, what):
        return self.s[f"{self.name}_{what}"]

    def vector(self, eng, src, dst, before_group=None):
        v = self.nc.vector
        for g in range(GROUPS):
            a = slice(g * GC, (g + 1) * GC)
            if before_group:
                before_group(g)
            v.tensor_reduce(self.total[:, a], src[:, a], AX.X, ALU.add).then_inc(self.sem("averaged"), 1)
            eng.wait_ge(self.sem("averaged"), 2 * g + 1)
            v.tensor_scalar(self.mean[:, a], self.total[:, a], -1.0 / H, None, ALU.mult).then_inc(self.sem("averaged"), 1)
            eng.wait_ge(self.sem("averaged"), 2 * g + 2)
            v.tensor_tensor(dst[:, a], src[:, a], self.mean[:, a].unsqueeze(2).broadcast_to([P, GC, H]),
                            ALU.add).then_inc(self.sem("centred"), 1)
        for g in range(GROUPS):
            a = slice(g * GC, (g + 1) * GC)
            eng.wait_ge(self.sem("inverted"), 2 * g + 3)
            v.tensor_tensor(dst[:, a], dst[:, a], self.inv[:, a].unsqueeze(2).broadcast_to([P, GC, H]),
                            ALU.mult).then_inc(self.sem("done"), 1)

    def scalar(self, eng, dst):
        a = self.nc.scalar
        for g in range(GROUPS):
            eng.wait_ge(self.sem("centred"), g + 1)
            for c in range(g * GC, (g + 1) * GC):
                if c:
                    eng.wait_ge(self.sem("squared"), c)
                a.activation(self.squares[:], dst[:, c], ACT.Square, accum_out=self.sumsq[:, c:c + 1]).then_inc(self.sem("squared"), 1)

    def gpsimd(self, eng):
        p = self.nc.gpsimd
        p.memset(self.minus_half[:], -0.5).then_inc(self.sem("inverted"), 1)
        for g in range(GROUPS):
            a = slice(g * GC, (g + 1) * GC)
            eng.wait_ge(self.sem("squared"), (g + 1) * GC)
            p.tensor_scalar(self.var[:, a], self.sumsq[:, a], 1.0 / H, EPS_LN, ALU.mult, ALU.add).then_inc(self.sem("inverted"), 1)
            eng.wait_ge(self.sem("inverted"), 2 * g + 2)
            p.tensor_tensor(self.inv[:, a], self.var[:, a], self.minus_half[:], ALU.pow).then_inc(self.sem("inverted"), 1)


def setup(nc, io, k):
    with ExitStack() as ctx:
        def sb(name, shape, dt=F32):
            return ctx.enter_context(nc.sbuf_tensor(name, shape, dt))

        ps = [ctx.enter_context(nc.psum_tensor(f"setup_bank{i}", [P, 512], F32)) for i in range(6)]
        xn = sb("xn", [P, NC, H])
        w_ba = sb("w_ba", [P, KT, 2 * NV])
        dt_row, a_row, neg_a = sb("dt_row", [P, NV]), sb("a_row", [P, NV]), sb("neg_a", [P, NV])
        tri, halves = sb("tri", [P, P]), sb("halves", [P, P])
        gate_shape = [P, NC, NV]
        beta, pre, soft, g, g_sum, g_last = (sb(n, gate_shape) for n in ("beta", "pre", "soft", "g", "g_sum", "g_last"))
        gT, eT = sb("gT", [NV, B, S]), sb("eT", [NV, B, S])
        zeros = sb("zeros", [2, NB * B * BLK])
        zeros_wide = sb("zeros_wide", [16, ZCOLS])
        beta_hc, g_hc, last_hc = (sb(n, [P, 2, NK, NC]) for n in ("beta_hc", "g_hc", "last_hc"))
        beta_col, g_col, last_col, eg_col = (sb(n, [P, B, NSTEPS]) for n in ("beta_col", "g_sum_col", "last_col", "eg_col"))
        ln = LayerNorm(ctx, nc, "ln_in")
        s = sems(ctx, nc, """x_in weights_in tables_zeroed masks_cleared masks_ready turned x_copied ba_done summed row_turned
            pre_ready gate_exp gate_log gate_step gates_done hc_done sums_out rows_copied rows_exp rows_out cols_in col_exp col_step
            cols_done""")
        flat = lambda ap: ap.rearrange("p c h -> p (c h)")

        block = ctx.enter_context(nc.Block())

        @block.sync
        def _(sp):
            for b in range(B):
                sp.dma_start(k.x_tok[b * C:(b + 1) * C], io["x"][b].rearrange("(c i) h -> i c h", i=C)).then_inc(s["x_in"], 16)
            for dst, src in ((w_ba[:], io["w_ba"]), (dt_row[:], io["dt_bias"].partition_broadcast(P)),
                             (a_row[:], io["A_log"].partition_broadcast(P)), (k.half_norm_w[:], io["norm_w"])):
                sp.dma_start(dst, src).then_inc(s["weights_in"], 16)
            sp.wait_ge(s["masks_cleared"], 1)
            for t in range(NTAB):
                rows = k.tables[t].rearrange("(p q) h -> p (q h)", q=(TOKENS + CAP) // 16)
                for part in range(ZPARTS):
                    sp.dma_start(rows[:, part * ZCOLS:(part + 1) * ZCOLS], zeros_wide[0:16]).then_inc(s["tables_zeroed"], 16)
            sp.wait_ge(s["hc_done"], 3)
            for src, dst in ((g_hc, g_col), (beta_hc, beta_col), (last_hc, last_col)):
                for u in range(2):
                    for b in range(B):
                        sp.dma_start(dst[u_half(u), b], src[u_half(b), u].rearrange("p j c -> p (j c)")).then_inc(s["cols_in"], 16)
            sp.wait_ge(s["rows_exp"], 1)
            sp.wait_ge(s["rows_copied"], 4)
            for src, dst in ((gT, k.g_rows), (eT, k.e_rows)):
                for b in range(B):
                    sp.dma_start(dst[0:NK].rearrange("j u r b t -> (j u) r b t")[:, :, b],
                                 src[:, b].rearrange("h (r t) -> h r t", r=NB)).then_inc(s["rows_out"], 16)
                sp.dma_start(dst[NK].rearrange("u r b t -> u (r b t)"), zeros[:]).then_inc(s["rows_out"], 16)
            sp.wait_ge(s["rows_out"], 16 * 6)
            sp.wait_ge(s["tables_zeroed"], 16 * NTAB * ZPARTS)

        @block.gpsimd
        def _(pool):
            g_ = nc.gpsimd
            g_.memset(k.ident[:], 0.0)
            g_.memset(k.ident_half[:], 0.0)
            g_.memset(tri[:], 1.0)
            g_.memset(halves[:], 0.0)
            g_.memset(k.mask_l[:], 0.0)
            g_.memset(k.mask_u[:], 0.0)
            g_.memset(k.ones_col[:], 1.0)
            g_.memset(k.pow_half[:], -0.5)
            for t in (k.g_col, k.tail_col, k.half_beta, k.minus_beta, k.minus_beta_eg):
                g_.memset(t[:, NSTEPS:], 0.0)
            g_.memset(zeros_wide[:], 0.0)
            g_.memset(zeros[:], 0.0).then_inc(s["masks_cleared"], 1)
            pool.wait_ge(s["masks_cleared"], 1)
            g_.affine_select(out=k.ident[:], in_=k.ident[:], compare_op=ALU.not_equal, fill=1.0, base=0,
                             pattern=[[-1, P]], channel_multiplier=1)
            g_.affine_select(out=tri[:], in_=tri[:], compare_op=ALU.is_ge, fill=0.0, base=0,
                             pattern=[[1, P]], channel_multiplier=-1).then_inc(s["masks_cleared"], 1)
            steps = 2
            for u in range(2):
                h = u_half(u)
                for make in (lambda: g_.memset(halves[h, h], 1.0),
                             lambda: g_.affine_select(out=k.ident_half[h], in_=k.ident_half[h], compare_op=ALU.not_equal, fill=1.0,
                                                      base=0, pattern=[[-1, C]], channel_multiplier=1),
                             lambda: g_.affine_select(out=k.mask_l[h], in_=k.mask_l[h], compare_op=ALU.is_gt, fill=NEG, base=0,
                                                      pattern=[[-1, C]], channel_multiplier=1),
                             lambda: g_.affine_select(out=k.mask_u[h], in_=k.mask_u[h], compare_op=ALU.is_ge, fill=NEG, base=0,
                                                      pattern=[[1, C]], channel_multiplier=-1)):
                    pool.wait_ge(s["masks_cleared"], steps)
                    make().then_inc(s["masks_cleared"], 1)
                    steps += 1
            pool.wait_ge(s["masks_cleared"], steps)
            g_.memset(tri[0:C, C:P], 0.0).then_inc(s["masks_ready"], 1)
            pool.wait_ge(s["masks_ready"], 1)
            ln.gpsimd(pool)

        @block.vector
        def _(dve):
            v = nc.vector
            dve.wait_ge(s["x_in"], 32)
            ln.vector(dve, k.x_tok, xn)
            dve.wait_ge(s["weights_in"], 64)
            dve.wait_ge(s["ba_done"], 1)
            for i in range(2):
                a8 = slice(i * 8, (i + 1) * 8)
                v.tensor_tensor(pre[:, a8], ps[2 + i][:].rearrange("p (c h) -> p c h", c=8)[:, :, NV:],
                                dt_row[:].unsqueeze(1).broadcast_to([P, 8, NV]), ALU.add).then_inc(s["gate_step"], 1)
            v.tensor_scalar(k.half_norm_w[:], k.half_norm_w[:], 0.5, None, ALU.mult)
            dve.wait_ge(s["gate_step"], 2)
            v.tensor_scalar(soft[:], pre[:], -1.0, None, ALU.mult).then_inc(s["gate_step"], 1)
            dve.wait_ge(s["gate_step"], 3)
            v.tensor_tensor(soft[:], soft[:], pre[:], ALU.min).then_inc(s["pre_ready"], 1)
            dve.wait_ge(s["gate_log"], 1)
            v.tensor_scalar(pre[:], pre[:], 0.0, None, ALU.max).then_inc(s["gate_step"], 1)
            v.tensor_scalar(neg_a[:], neg_a[:], -1.0, None, ALU.mult).then_inc(s["gate_step"], 1)
            dve.wait_ge(s["gate_step"], 5)
            v.tensor_tensor(soft[:], soft[:], pre[:], ALU.add).then_inc(s["gate_step"], 1)
            dve.wait_ge(s["gate_step"], 6)
            v.tensor_tensor(g[:], soft[:], neg_a[:].unsqueeze(1).broadcast_to([P, NC, NV]), ALU.mult).then_inc(s["gates_done"], 1)
            dve.wait_ge(s["summed"], 1)
            v.tensor_copy(flat(g_sum[:]), ps[4][:]).then_inc(s["sums_out"], 1)
            v.tensor_copy(flat(g_last[:]), ps[5][:]).then_inc(s["sums_out"], 1)
            dve.wait_ge(s["sums_out"], 2)
            dve.wait_ge(s["gate_exp"], 2)
            for src, dst in ((g_sum, g_hc), (g_last, last_hc), (beta, beta_hc)):
                for u in range(2):
                    mm = v.tensor_copy(dst[:, u], src[:].rearrange("p c (j u) -> p u j c", u=2)[:, u])
                mm.then_inc(s["hc_done"], 1)
            dve.wait_ge(s["row_turned"], 1)
            for i in range(4):
                v.tensor_copy(gT[:, :, i * 4 * C:(i + 1) * 4 * C].rearrange("h b (c i) -> h c b i", i=C),
                              ps[i][0:NV].rearrange("h (c b i) -> h c b i", c=4, b=B)).then_inc(s["rows_copied"], 1)
            dve.wait_ge(s["cols_in"], 16 * 12)
            to = lambda t: t[:, 0:NSTEPS].rearrange("p s b -> p b s")
            v.tensor_scalar(to(k.half_beta), beta_col[:], 0.5, None, ALU.mult)
            v.tensor_scalar(to(k.minus_beta), beta_col[:], -1.0, None, ALU.mult).then_inc(s["col_step"], 1)
            v.tensor_copy(to(k.g_col), g_col[:])
            v.tensor_tensor(last_col[:], last_col[:], g_col[:], ALU.subtract).then_inc(s["col_step"], 1)
            dve.wait_ge(s["col_step"], 2)
            dve.wait_ge(s["col_exp"], 1)
            v.tensor_tensor(to(k.minus_beta_eg), to(k.minus_beta), eg_col[:], ALU.mult)

        @block.scalar
        def _(act):
            a = nc.scalar
            ln.scalar(act, xn)
            for c in range(NC):
                act.wait_ge(s["turned"], c + 1)
                a.copy(k.xT[:, :, c], ps[c % 2][:, 0:KT * P].rearrange("p (k b i) -> p k b i", k=KT, b=B)).then_inc(s["x_copied"], 1)
            act.wait_ge(s["weights_in"], 64)
            a.activation(neg_a[:], a_row[:], ACT.Exp)
            act.wait_ge(s["pre_ready"], 1)
            a.activation(g[:], soft[:], ACT.Exp).then_inc(s["gate_exp"], 1)
            act.wait_ge(s["gate_exp"], 1)
            a.activation(soft[:], g[:], ACT.Ln, bias=k.ones_col[:]).then_inc(s["gate_log"], 1)
            for i in range(2):
                a8 = slice(i * 8, (i + 1) * 8)
                last = a.activation(beta[:, a8], ps[2 + i][:].rearrange("p (c h) -> p c h", c=8)[:, :, 0:NV], ACT.Sigmoid)
            last.then_inc(s["gate_exp"], 1)
            act.wait_ge(s["rows_copied"], 4)
            a.activation(eT[:], gT[:], ACT.Exp).then_inc(s["rows_exp"], 1)
            act.wait_ge(s["cols_in"], 16 * 12)
            a.activation(eg_col[:], g_col[:], ACT.Exp).then_inc(s["col_exp"], 1)
            act.wait_ge(s["col_step"], 2)
            a.activation(k.tail_col[:, 0:NSTEPS].rearrange("p s b -> p b s"), last_col[:], ACT.Exp).then_inc(s["cols_done"], 1)

        @block.tensor
        def _(pe):
            pe.wait_ge(s["masks_ready"], 1)
            for c in range(NC):
                if c >= 2:
                    pe.wait_ge(s["x_copied"], c - 1)
                pe.wait_ge(ln.sem("done"), c // GC + 1)
                for kt in range(KT):
                    mm = nc.tensor.transpose(ps[c % 2][:, kt * P:(kt + 1) * P], xn[:, c, kt * P:(kt + 1) * P], k.ident[:])
                mm.then_inc(s["turned"], 1)
            pe.wait_ge(s["x_copied"], NC)
            pe.wait_ge(s["weights_in"], 64)
            for c in range(NC):
                for kt in range(KT):
                    mm = nc.tensor.matmul(ps[2 + c // 8][:, (c % 8) * 2 * NV:(c % 8 + 1) * 2 * NV], k.xT[:, kt, c].rearrange("p b i -> p (b i)"),
                                          w_ba[:, kt], start=(kt == 0), stop=(kt == KT - 1))
            mm.then_inc(s["ba_done"], 1)
            pe.wait_ge(s["gates_done"], 1)
            nc.tensor.matmul(ps[4][:], tri[:], flat(g[:]), start=True, stop=True)
            nc.tensor.matmul(ps[5][:], halves[:], flat(g[:]), start=True, stop=True).then_inc(s["summed"], 1)
            pe.wait_ge(s["sums_out"], 2)
            pe.wait_ge(s["gate_exp"], 2)
            for c in range(NC):
                mm = nc.tensor.transpose(ps[c // 4][0:NV, (c % 4) * P:(c % 4 + 1) * P], g_sum[:, c], k.ident[:])
            mm.then_inc(s["row_turned"], 1)


def delta_rule(nc, io, k, pairs):
    with ExitStack() as ctx:
        def sb(name, shape, dt=F32):
            return ctx.enter_context(nc.sbuf_tensor(name, shape, dt))

        bank = [ctx.enter_context(nc.psum_tensor(f"bank{i}", [P, 512], F32)) for i in range(8)]
        w_proj = sb("w_proj", [P, KT, Z_, P])
        w_z = sb("w_z", [P, KT, NT - Z_, P])
        w_out = sb("w_out", [P, 2, H])
        conv_w = sb("conv_w", [P, 4, TAPS])
        raw = sb("raw", [P, 4, B, TAPS - 1 + BLK])
        conv = sb("conv", [P, 4, B, BLK])
        th = sb("th", [P, 4, B, BLK])
        vs = sb("vs", [P, B, 2, 2, C])
        thz = sb("thz", [P, 2, B, BLK])
        zs = sb("zs", [P, 2, 2, B, BLK])
        sq = sb("sq", [P, 2, 2 * B, 2, C])
        g_blk = sb("g_blk", [P, B, BLK])
        e_blk = sb("e_blk", [P, 2, B, BLK])
        g_diff = sb("g_diff", [P, 2, B, C])
        dec_arg = sb("dec_arg", [P, 2, 2, B, C])
        dec = sb("dec", [P, 2, 2, B, C])
        ssq = sb("ssq", [P, 2, 2, B])
        rn = sb("rn", [P, 2, 2, B])
        rn2 = sb("rn2", [P, 2, B])
        l_scale = sb("l_scale", [P, 2, B])
        v_scale = sb("v_scale", [P, 2, B])
        k_tail = sb("k_tail", [P, 2, B])
        UL = sb("UL", [P, 2, 2 * B, 2, C])
        prod = sb("prod", [P, 2, 2 * B, C])
        kkq = sb("kkq", [P, 2, B, 2, 3, C])
        qg = sb("qg", [P, 4, B, 2, C])
        s_dec = sb("s_dec", [P, 4, B, 2])
        ks_scale = sb("ks_scale", [P, 4, B])
        q_scale = sb("q_scale", [P, 4, B])
        q_scale2 = sb("q_scale2", [P, 4, B])
        attnT = sb("attnT", [P, 4, B, C])
        vb = sb("vb", [P, 4, B, D])
        kdec = sb("kdec", [P, 4, B, D])
        inv = sb("inv", [P, 4, B, C])
        r = sb("r", [P, B, D])
        vt = sb("vt", [P, B, D])
        state = sb("state", [P, B, 2, D])
        state_d = sb("state_d", [P, B, 2, D])
        squares = sb("squares", [P, B, D])
        core_ss, core_ms, core_var, core_rs, core_f = (sb(n, [P, B]) for n in ("core_ss", "core_ms", "core_var", "core_rs", "core_f"))
        core_n = sb("core_n", [P, B, D])
        gated = sb("gated", [P, 2, B, C])
        credits = sb("credits", [P, 6])

        s = sems(ctx, nc, """w_in w_z_in conv_w_in w_out_in g_in e_in started
            projected_kq projected_v projected_z ssq_summed grammed turned u_turned squared powered
            ks_done vt_done core_done grown_0 grown_1 core_turned y_projected
            raw_in tap_in conv_tanhed z_tanhed decayed vb_out u_out ul_out vt_out squares_out core_out
            conv_steps kqv_ready z_ready ssq_out l_ready attn_ready p_out r_ready s_updated gated_out y_added
            hist_done kq_squared rn_ready diffed dec_args qg_ready cols_ready q_steps p1_ready
            s_decayed f_steps f_ready""")

        def per_pair(eng, body):
            with eng.Fori(0, pairs) as pair:
                with eng.Fori(0, NB // 2 - 1) as r2:
                    for odd in range(2):
                        body(pair, 2 * r2 + odd, pair * NB + 2 * r2 + odd, odd, False, False)
                body(pair, NB - 2, pair * NB + NB - 2, 0, True, False)
                body(pair, NB - 1, pair * NB + NB - 1, 1, True, True)

        block = ctx.enter_context(nc.Block())

        @block.sync
        def _(sp):
            def load_projection(pair):
                src = io["w_proj"][bass.ds(pair, 1)].rearrange("o p k t c -> (o p) k t c")
                sp.dma_start(w_proj[:], src[:, :, 0:Z_]).then_inc(s["w_in"], 16)
                sp.dma_start(conv_w[:], io["conv_w"][bass.ds(pair, 1)].rearrange("o p t w -> (o p) t w")).then_inc(s["conv_w_in"], 16)

            def load_w_z(pair):
                src = io["w_proj"][bass.ds(pair, 1)].rearrange("o p k t c -> (o p) k t c")
                sp.dma_start(w_z[:], src[:, :, Z_:]).then_inc(s["w_z_in"], 16)

            def load_w_out(pair):
                sp.dma_start(w_out[:], io["w_out"][bass.ds(pair, 1)].rearrange("o p u h -> (o p) u h")).then_inc(s["w_out_in"], 16)

            def load_g(pair, rr):
                for u in range(2):
                    src = k.g_rows[bass.ds(pair, 1), u, bass.ds(rr, 1)].rearrange("o q b t -> (o q) (b t)")
                    sp.dma_start(g_blk[u_half(u)], src.broadcast_to([C, B * BLK])).then_inc(s["g_in"], 16)

            def load_e(pair, rr):
                for u in range(2):
                    src = k.e_rows[bass.ds(pair, 1), u, bass.ds(rr, 1)].rearrange("o q b t -> (o q) (b t)")
                    sp.dma_start(e_blk[:, u], src.broadcast_to([P, B * BLK])).then_inc(s["e_in"], 16)

            load_projection(0)
            load_w_z(0)
            load_g(0, 0)
            load_e(0, 0)
            load_w_out(0)
            for m in range(2):
                sp.wait_ge(s["diffed"], m + 1)
                load_g(0, m + 1)
            sp.wait_ge(s["qg_ready"], 1)
            load_e(0, 1)

            def body(pair, rr, n):
                ahead = lambda by: (pair, rr + by) if rr_is_low(rr, by) else (pair + 1, rr + by - NB)
                if isinstance(rr, int) and rr == NB - 2:
                    sp.wait_ge(s["projected_v"], n + 2)
                    sp.wait_ge(s["conv_steps"], 12 * n + 24)
                    load_projection(pair + 1)
                if isinstance(rr, int) and rr == NB - 1:
                    sp.wait_ge(s["projected_z"], n + 1)
                    load_w_z(pair + 1)
                sp.wait_ge(s["qg_ready"], n + 2)
                load_e(*ahead(2))
                sp.wait_ge(s["diffed"], n + 3)
                load_g(*ahead(3))
                if isinstance(rr, int) and rr == NB - 1:
                    sp.wait_ge(s["y_projected"], 2 * n + 2)
                    load_w_out(pair + 1)

            rr_is_low = lambda rr, by: not isinstance(rr, int) or rr + by < NB
            with sp.Fori(0, pairs) as pair:
                with sp.Fori(0, NB - 3) as rr:
                    body(pair, rr, pair * NB + rr)
                for rr in range(NB - 3, NB):
                    body(pair, rr, pair * NB + rr)
            for name in ("w_in", "w_z_in", "conv_w_in", "w_out_in"):
                sp.wait_ge(s[name], 16 * (pairs + 1))
            sp.wait_ge(s["g_in"], 32 * (pairs * NB + 3))
            sp.wait_ge(s["e_in"], 32 * (pairs * NB + 2))

        @block.tensor
        def _(pe):
            te = nc.tensor

            def project(rr, tile, bk, place, done=None):
                for kt in range(KT):
                    w = w_z[:, kt, tile - Z_] if tile >= Z_ else w_proj[:, kt, tile]
                    mm = te.matmul(bank[bk][:, place * 2 * BLK:(place + 1) * 2 * BLK], w,
                                   k.xT[:, kt, bass.ds(rr * 2, 2)].rearrange("p c b i -> p b c i"), start=(kt == 0), stop=(kt == KT - 1))
                if done:
                    mm.then_inc(s[done], 1)

            def sum_squares(m):
                pe.wait_ge(s["kq_squared"], m + 1)
                pe.wait_ge(s["raw_in"], 2 * m + 2)
                for kq in range(2):
                    for p in range(2):
                        for b in range(B):
                            i = (kq * 2 + p) * B + b
                            mm = te.matmul(bank[1][:, i:i + 1], sq[:, kq, b * 2 + p].rearrange("p u i -> p (u i)"), k.ones_col[:],
                                           start=True, stop=True)
                mm.then_inc(s["ssq_summed"], 1)

            def gram(m, q):
                pe.wait_ge(s["kqv_ready"], 2 * m + 1)
                for p in range(2):
                    for b in range(B):
                        i = p * B + b
                        mm = te.matmul(bank[3][:, i * P:(i + 1) * P], kkq[:, q, b, p, 0:2].rearrange("p u i -> p (u i)"),
                                       kkq[:, q, b, p, 1:3], start=True, stop=True)
                mm.then_inc(s["grammed"], 1)

            def turn(m, q, p):
                pe.wait_ge(s["kqv_ready"], 2 * m + 2)
                for b in range(B):
                    te.transpose(bank[2][:, b * P:(b + 1) * P], kkq[:, q, b, p, 0:2].rearrange("p u i -> p (u i)"), k.ident[:])
                    mm = te.transpose(bank[2][:, (2 + b) * P:(3 + b) * P], vs[:, b, p].rearrange("p u i -> p (u i)"), k.ident[:])
                mm.then_inc(s["turned"], 1)

            def tiles(count, fn):
                for i in range(count):
                    for u in range(2):
                        mm = fn(i, u_half(u))
                return mm

            def ready():
                pe.wait_ge(s["started"], 1)

            def turn_u(m):
                rounds, this = in_register(pe, 5 * m + 1), in_register(pe, m + 1)
                ready()
                pe.wait_ge(s["ul_out"], rounds)
                pe.wait_ge(s["l_ready"], this)
                tiles(2 * B, lambda i, h: te.matmul(bank[4][h, i * P:i * P + C], UL[h, 0, i, 1], k.ident[h, h],
                                                    start=True, stop=True)).then_inc(s["u_turned"], 1)

            def square(m, i):
                w = (i - 1) % 2
                rounds = in_register(pe, m + 1 if i == 1 else 5 * m + i)
                ready()
                if i == 1:
                    pe.wait_ge(s["u_out"], rounds)
                else:
                    pe.wait_ge(s["ul_out"], rounds)
                if i < 5:
                    tiles(2 * B, lambda j, h: te.matmul(bank[4][h, j * P:j * P + C], UL[h, w, j, 1], UL[h, w, j, 0],
                                                        start=True, stop=True))
                tiles(2 * B, lambda j, h: te.matmul(bank[4][h, j * P + C:(j + 1) * P], UL[h, w, j, 0], UL[h, w, j, 1],
                                                    start=True, stop=True)).then_inc(s["squared"], 1)

            def power(m, i):
                w = (i - 1) % 2
                this, rounds, powers = (in_register(pe, x) for x in (m + 1, 5 * m + i, 5 * m + i - 1))
                ready()
                pe.wait_ge(s["ul_out"], rounds)
                if i == 2:
                    pe.wait_ge(s["p1_ready"], this)
                pe.wait_ge(s["p_out"], powers)
                tiles(2 * B, lambda j, h: te.matmul(bank[5][h, j * C:(j + 1) * C], UL[h, w, j, 1], prod[h, i % 2, j],
                                                    start=True, stop=True)).then_inc(s["powered"], 1)

            def keys_state(st, slot):
                pe.wait_ge(s["s_updated"], st + 1)
                for b in range(B):
                    for u in range(2):
                        mm = te.matmul(bank[6][u_half(u), b * D:(b + 1) * D], kkq[:, slot // 2, b, slot % 2, 0], state[:, b, u], start=True, stop=True)
                mm.then_inc(s["ks_done"], 1)

            def values(st, n, slot):
                this, powers, cores = in_register(pe, st + 1), in_register(pe, 5 * n + 6), in_register(pe, st + 1)
                ready()
                pe.wait_ge(s["r_ready"], this)
                pe.wait_ge(s["p_out"], powers)
                pe.wait_ge(s["core_out"], cores)
                tiles(B, lambda b, h: te.matmul(bank[7][h, b * D:(b + 1) * D], inv[h, slot, b], r[h, b],
                                                start=True, stop=True)).then_inc(s["vt_done"], 1)

            def core(st, n, slot):
                pe.wait_ge(s["vt_out"], st + 1)
                pe.wait_ge(s["qg_ready"], n + 1)
                pe.wait_ge(s["attn_ready"], n + 1)
                for b in range(B):
                    for u in range(2):
                        h = u_half(u)
                        te.matmul(bank[7][h, b * D:(b + 1) * D], qg[:, slot, b, u], state[:, b, u],
                                  start=True, stop=False, skip_group_check=True)
                        mm = te.matmul(bank[7][h, b * D:(b + 1) * D], attnT[h, slot, b], vt[h, b],
                                       start=False, stop=True, skip_group_check=True)
                mm.then_inc(s["core_done"], 1)

            def grow(st, slot):
                pe.wait_ge(s["vb_out"], 2 * st + 2)
                pe.wait_ge(s["r_ready"], st + 1)
                for u, bk in ((0, 3), (1, 6)):
                    for b in range(B):
                        mm = te.matmul(bank[bk][:, b * D:(b + 1) * D], kdec[u_half(u), slot, b], vt[u_half(u), b], start=True, stop=True)
                    mm.then_inc(s[f"grown_{u}"], 1)

            def turn_core(st, m):
                pe.wait_ge(s["core_out"], st + 2)
                pe.wait_ge(s["vb_out"], 4 * m + 4)
                pe.wait_ge(s["y_added"], st + 1)
                for b in range(B):
                    o = bank[2][:, 0:2 * P].rearrange("p (u b i) -> p u b i", u=2, b=B)[:, :, b]
                    mm = te.transpose(o, core_n[:, b], k.ident[:])
                mm.then_inc(s["core_turned"], 1)

            def project_out(st, pair):
                pe.wait_ge(s["w_out_in"], 16 * (pair + 1))
                pe.wait_ge(s["gated_out"], st + 1)
                for u in range(2):
                    mm = te.matmul(bank[2][:, 0:H], gated[:, u].rearrange("p b i -> p (b i)"), w_out[:, u],
                                   start=(u == 0), stop=(u == 1))
                mm.then_inc(s["y_projected"], 1)

            pe.wait_ge(s["started"], 1)
            pe.wait_ge(s["w_in"], 16)
            project(0, K_, 0, 0)
            project(0, Q_, 0, 1, "projected_kq")
            project(0, V_, 1, 0)
            project(0, V_ + 1, 1, 1, "projected_v")
            pe.wait_ge(s["raw_in"], 1)
            pe.wait_ge(s["w_z_in"], 16)
            project(0, Z_, 0, 0)
            project(0, Z_ + 1, 0, 1, "projected_z")
            sum_squares(0)
            gram(0, 0)
            turn(0, 0, 0)
            turn_u(0)
            pe.wait_ge(s["z_ready"], 1)
            project(1, K_, 0, 0)
            project(1, Q_, 0, 1, "projected_kq")
            square(0, 1)
            pe.wait_ge(s["vb_out"], 2)
            turn(0, 0, 1)
            pe.wait_ge(s["ssq_out"], 1)
            project(1, V_, 1, 0)
            project(1, V_ + 1, 1, 1, "projected_v")
            for i in range(2, 7):
                if i <= 5:
                    square(0, i)
                power(0, i)
            sum_squares(1)

            def body(pair, rr, n, odd, crossing, last):
                m, q, st, slot = n + 1, 1 - odd, 2 * n, 2 * odd
                rr2 = rr + 2 - NB if crossing else rr + 2
                rr1 = 0 if last else rr + 1
                pe.wait_ge(s["s_updated"], st + 1)
                gram(m, q)
                keys_state(st, slot)
                pe.wait_ge(s["y_added"], st + 1)
                turn(m, q, 0)
                if crossing and not last:
                    pe.wait_ge(s["w_in"], 16 * (pair + 2))
                pe.wait_ge(s["z_ready"], n + 1)
                project(rr2, K_, 0, 0)
                turn_u(m)
                values(st, n, slot)
                project(rr2, Q_, 0, 1, "projected_kq")
                square(m, 1)
                core(st, n, slot)
                pe.wait_ge(s["vb_out"], 4 * m + 2)
                turn(m, q, 1)
                square(m, 2)
                power(m, 2)
                pe.wait_ge(s["attn_ready"], m + 1)
                grow(st, slot)
                pe.wait_ge(s["ssq_out"], n + 2)
                project(rr2, V_, 1, 0)
                square(m, 3)
                power(m, 3)
                keys_state(st + 1, slot + 1)
                project(rr2, V_ + 1, 1, 1, "projected_v")
                square(m, 4)
                power(m, 4)
                values(st + 1, n, slot + 1)
                turn_core(st, m)
                if last:
                    pe.wait_ge(s["w_z_in"], 16 * (pair + 2))
                pe.wait_ge(s["raw_in"], 2 * n + 5)
                project(rr1, Z_, 0, 0)
                square(m, 5)
                power(m, 5)
                core(st + 1, n, slot + 1)
                project_out(st, pair)
                grow(st + 1, slot + 1)
                project(rr1, Z_ + 1, 0, 1, "projected_z")
                power(m, 6)
                sum_squares(n + 2)
                turn_core(st + 1, m)
                project_out(st + 1, pair)

            per_pair(pe, body)

        @block.scalar
        def _(act):
            a = nc.scalar

            def take_raw(m, i):
                pe_done = ("projected_kq", "projected_v")[i]
                act.wait_ge(s[pe_done], m + 1)
                act.wait_ge(s["hist_done"], m + 1)
                a.copy(raw[:, 2 * i:2 * i + 2, :, TAPS - 1:],
                       bank[i][:].rearrange("p (t b x) -> p t b x", t=2, b=B)).then_inc(s["raw_in"], 1)
                act.wait_ge(s["raw_in"], 2 * m + i + 1)
                for t in (2 * i, 2 * i + 1):
                    a.activation(conv[:, t], raw[:, t, :, 0:BLK], ACT.Copy, scale=conv_w[:, t, 0:1]).then_inc(s["tap_in"], 1)

            def tanh_conv(m, i):
                act.wait_ge(s["conv_steps"], 12 * m + 6 * i + 6)
                a.activation(th[:, 2 * i:2 * i + 2], conv[:, 2 * i:2 * i + 2], ACT.Tanh, scale=0.5).then_inc(s["conv_tanhed"], 1)

            def square_kq(m, q):
                act.wait_ge(s["kqv_ready"], 2 * m + 1)
                if not at_start(m):
                    act.wait_ge(s["ssq_summed"], m)
                for w in range(2):
                    x = kkq[:, q].rearrange("p b s w i -> p (b s) w i")[:, :, 1 + w].unsqueeze(2).broadcast_to([P, 2 * B, 2, C])
                    mm = a.activation(sq[:, w], x, ACT.Square)
                mm.then_inc(s["kq_squared"], 1)

            def tanh_z(m):
                act.wait_ge(s["projected_z"], m + 1)
                a.activation(thz[:], bank[0][:], ACT.Tanh, scale=0.5).then_inc(s["z_tanhed"], 1)

            def decays(m):
                act.wait_ge(s["dec_args"], m + 1)
                if not at_start(m):
                    act.wait_ge(s["attn_ready"], m)
                a.activation(dec[:], dec_arg[:], ACT.Exp).then_inc(s["decayed"], 1)

            def token_major(m, q, p):
                act.wait_ge(s["turned"], 2 * m + p + 1)
                act.wait_ge(s["cols_ready"], m + 1)
                for b in range(B):
                    mm = a.activation(vb[:, 2 * q + p, b], bank[2][:, (2 + b) * P:(3 + b) * P], ACT.Copy, scale=v_scale[:, p, b:b + 1])
                mm.then_inc(s["vb_out"], 1)
                for b in range(B):
                    mm = a.activation(kdec[:, 2 * q + p, b], bank[2][:, b * P:(b + 1) * P], ACT.Copy, scale=k_tail[:, p, b:b + 1])
                mm.then_inc(s["vb_out"], 1)

            def take_u(m):
                act.wait_ge(s["u_turned"], m + 1)
                a.copy(UL[:, 0, :, 0], bank[4][:].rearrange("p (b x) -> p b x", b=2 * B)[:, :, 0:C]).then_inc(s["u_out"], 1)

            def take_ul(m, i):
                act.wait_ge(s["squared"], 5 * m + i)
                if i == 2:
                    act.wait_ge(s["p1_ready"], m + 1)
                both = bank[4][:].rearrange("p (b w x) -> p b w x", b=2 * B, w=2)
                if i < 5:
                    mm = a.copy(UL[:, i % 2], both)
                else:
                    mm = a.copy(UL[:, 1, :, 1], both[:, :, 1])
                mm.then_inc(s["ul_out"], 1)

            def take_values(st):
                act.wait_ge(s["vt_done"], st + 1)
                a.copy(vt[:].rearrange("p b d -> p (b d)"), bank[7][:, 0:B * D]).then_inc(s["vt_out"], 1)

            def core_squares(st):
                act.wait_ge(s["core_done"], st + 1)
                for b in range(B):
                    mm = a.activation(squares[:, b], bank[7][:, b * D:(b + 1) * D], ACT.Square, accum_out=core_ss[:, b:b + 1])
                    mm.then_inc(s["squares_out"], 1)

            def core_scaled(st):
                act.wait_ge(s["f_ready"], st + 2)
                for b in range(B):
                    mm = a.activation(core_n[:, b], bank[7][:, b * D:(b + 1) * D], ACT.Copy, scale=core_f[:, b:b + 1])
                mm.then_inc(s["core_out"], 1)

            act.wait_ge(s["conv_w_in"], 16)
            take_raw(0, 0)
            take_raw(0, 1)
            tanh_conv(0, 0)
            square_kq(0, 0)
            tanh_conv(0, 1)
            tanh_z(0)
            decays(0)
            take_u(0)
            token_major(0, 0, 0)
            take_raw(1, 0)
            take_ul(0, 1)
            token_major(0, 0, 1)
            take_raw(1, 1)
            for i in range(2, 6):
                take_ul(0, i)
            tanh_conv(1, 0)
            square_kq(1, 1)
            tanh_conv(1, 1)
            decays(1)

            def body(pair, rr, n, odd, crossing, last):
                m, q, st = n + 1, 1 - odd, 2 * n
                token_major(m, q, 0)
                take_u(m)
                take_values(st)
                take_ul(m, 1)
                core_squares(st)
                if crossing and not last:
                    act.wait_ge(s["conv_w_in"], 16 * (pair + 2))
                take_raw(n + 2, 0)
                take_ul(m, 2)
                token_major(m, q, 1)
                core_scaled(st)
                take_ul(m, 3)
                tanh_conv(n + 2, 0)
                take_ul(m, 4)
                take_raw(n + 2, 1)
                take_values(st + 1)
                take_ul(m, 5)
                square_kq(n + 2, odd)
                core_squares(st + 1)
                core_scaled(st + 1)
                tanh_conv(n + 2, 1)
                tanh_z(n + 1)
                decays(n + 2)

            per_pair(act, body)

        @block.vector
        def _(dve):
            v = nc.vector

            def convolve(m, t):
                dve.wait_ge(s["tap_in"], 4 * m + t + 1)
                for w in range(1, TAPS):
                    if w > 1:
                        dve.wait_ge(s["conv_steps"], 12 * m + 3 * t + w - 1)
                    v.scalar_tensor_tensor(out=conv[:, t], in0=raw[:, t, :, w:w + BLK], scalar=conv_w[:, t, w:w + 1],
                                           in1=conv[:, t], op0=ALU.mult, op1=ALU.add).then_inc(s["conv_steps"], 1)

            def silu(m, i, q):
                dve.wait_ge(s["conv_tanhed"], 2 * m + i + 1)
                by_step = lambda t: t.rearrange("p b (s i) -> p (b s) i", s=2)
                if i == 0:
                    if not isinstance(m, int):
                        dve.wait_ge(s["ks_done"], 2 * m - 2)
                    for w, t in ((0, K_), (1, K_), (2, Q_)):
                        mm = v.scalar_tensor_tensor(out=kkq[:, q].rearrange("p b s w i -> p (b s) w i")[:, :, w], in0=by_step(th[:, t]), scalar=1.0,
                                                    in1=by_step(conv[:, t]), op0=ALU.add, op1=ALU.mult)
                else:
                    if not at_start(m):
                        dve.wait_ge(s["turned"], 2 * m)
                    for u in range(2):
                        mm = v.scalar_tensor_tensor(out=vs[:].rearrange("p b s u i -> p (b s) u i")[:, :, u], in0=by_step(th[:, V_ + u]), scalar=1.0,
                                                    in1=by_step(conv[:, V_ + u]), op0=ALU.add, op1=ALU.mult)
                mm.then_inc(s["kqv_ready"], 1)

            def silu_z(m, q):
                dve.wait_ge(s["z_tanhed"], m + 1)
                v.scalar_tensor_tensor(out=zs[:, q].rearrange("p u b x -> p (u b x)"), in0=thz[:].rearrange("p u b x -> p (u b x)"),
                                       scalar=1.0, in1=bank[0][:], op0=ALU.add, op1=ALU.mult).then_inc(s["z_ready"], 1)

            def take_ssq(m):
                dve.wait_ge(s["ssq_summed"], m + 1)
                v.tensor_scalar(ssq[:].rearrange("p k s b -> p (k s b)"), bank[1][:, 0:4 * B], 4e-24, None,
                                ALU.max).then_inc(s["ssq_out"], 1)

            def make_l(m, q):
                dve.wait_ge(s["grammed"], m + 1)
                dve.wait_ge(s["cols_ready"], m + 1)
                dve.wait_ge(s["decayed"], m + 1)
                for p in range(2):
                    for b in range(B):
                        i = p * B + b
                        mm = v.scalar_tensor_tensor(out=UL[:, 0, i, 1], in0=bank[3][:, i * P:i * P + C], scalar=l_scale[:, p, b:b + 1],
                                                    in1=dec[:, 0, p, b], op0=ALU.mult, op1=ALU.mult)
                mm.then_inc(s["l_ready"], 1)
                v.tensor_tensor(attnT[:, 2 * q:2 * q + 2].rearrange("p s b x -> p (s b) x"),
                                bank[3][:].rearrange("p (b x) -> p b x", b=2 * B)[:, :, C:],
                                dec[:, 1].rearrange("p s b x -> p (s b) x"), ALU.mult).then_inc(s["attn_ready"], 1)

            def take_p(m, i, q):
                dve.wait_ge(s["powered"], 5 * m + i - 1)
                out = inv[:, 2 * q:2 * q + 2].rearrange("p s b x -> p (s b) x") if i == 6 else prod[:, (i + 1) % 2]
                v.tensor_tensor(out, bank[5][:, 0:2 * B * C].rearrange("p (b x) -> p b x", b=2 * B), prod[:, i % 2],
                                ALU.add).then_inc(s["p_out"], 1)

            def make_r(st, slot):
                dve.wait_ge(s["ks_done"], st + 1)
                dve.wait_ge(s["vb_out"], 2 * st + 1)
                for b in range(B):
                    mm = v.scalar_tensor_tensor(out=r[:, b], in0=bank[6][:, b * D:(b + 1) * D], scalar=ks_scale[:, slot, b:b + 1],
                                                in1=vb[:, slot, b], op0=ALU.mult, op1=ALU.add)
                mm.then_inc(s["r_ready"], 1)

            def update(st, reset):
                dve.wait_ge(s["s_decayed"], st + 1)
                if reset:
                    for u in range(2):
                        dve.wait_ge(s[f"grown_{u}"], st + 1)
                    v.memset(state[:], 0.0).then_inc(s["s_updated"], 1)
                    return
                for u, bk in ((0, 3), (1, 6)):
                    dve.wait_ge(s[f"grown_{u}"], st + 1)
                    mm = v.tensor_tensor(state[:, :, u], bank[bk][:, 0:B * D].rearrange("p (b d) -> p b d", b=B),
                                         state_d[:, :, u], ALU.add)
                mm.then_inc(s["s_updated"], 1)

            def gate(st, odd, p):
                dve.wait_ge(s["core_turned"], st + 1)
                v.scalar_tensor_tensor(out=gated[:].rearrange("p u b i -> p (u b) i"),
                                       in0=bank[2][:, 0:2 * P].rearrange("p (q i) -> p q i", i=C), scalar=k.half_norm_w[:],
                                       in1=zs[:, odd, :, :, p * C:(p + 1) * C].rearrange("p u b i -> p (u b) i"),
                                       op0=ALU.mult, op1=ALU.mult).then_inc(s["gated_out"], 1)

            def add_y(st, chunk):
                dve.wait_ge(s["y_projected"], st + 1)
                y = k.y_sum[:, bass.ds(chunk, 1)].rearrange("p o h -> p (o h)")
                v.tensor_tensor(y, bank[2][:, 0:H], y, ALU.add).then_inc(s["y_added"], 1)

            v.memset(k.y_sum[:], 0.0)
            v.memset(state[:], 0.0).then_inc(s["s_updated"], 1)
            v.memset(credits[:, 4:5], 0.0).then_inc(s["y_added"], 1)
            v.memset(credits[:, 5:6], 0.0).then_inc(s["p_out"], 1)
            dve.wait_ge(s["conv_w_in"], 16)
            for t in range(4):
                convolve(0, t)
            silu(0, 0, 0)
            silu(0, 1, 0)
            silu_z(0, 0)
            take_ssq(0)
            make_l(0, 0)
            for t in range(4):
                convolve(1, t)
            for i in range(2, 7):
                take_p(0, i, 0)
            silu(1, 0, 1)
            silu(1, 1, 1)
            take_ssq(1)

            def body(pair, rr, n, odd, crossing, last):
                m, q, st, slot = n + 1, 1 - odd, 2 * n, 2 * odd
                make_r(st, slot)
                make_l(m, q)
                take_p(m, 2, q)
                convolve(n + 2, 0)
                convolve(n + 2, 1)
                update(st, False)
                take_p(m, 3, q)
                make_r(st + 1, slot + 1)
                silu(n + 2, 0, odd)
                take_p(m, 4, q)
                gate(st, odd, 0)
                convolve(n + 2, 2)
                take_p(m, 5, q)
                convolve(n + 2, 3)
                add_y(st, 2 * rr)
                update(st + 1, last)
                silu(n + 2, 1, odd)
                take_p(m, 6, q)
                take_ssq(n + 2)
                gate(st + 1, odd, 1)
                silu_z(n + 1, q)
                add_y(st + 1, 2 * rr + 1)

            per_pair(dve, body)

        @block.gpsimd
        def _(pool):
            g = nc.gpsimd

            def ready():
                pool.wait_ge(s["started"], 1)

            def history(m, reset):
                if not at_start(m):
                    taps = in_register(pool, 12 * m)
                    ready()
                    pool.wait_ge(s["conv_steps"], taps)
                if reset:
                    mm = g.memset(raw[:, :, :, 0:TAPS - 1], 0.0)
                else:
                    mm = g.tensor_copy(raw[:, :, :, 0:TAPS - 1], raw[:, :, :, BLK:])
                mm.then_inc(s["hist_done"], 1)

            def gate_differences(m):
                pool.wait_ge(s["g_in"], 32 * m + 32)
                for p in range(2):
                    col = k.g_col[:, bass.ds(2 * m + p, 1)].rearrange("p o b -> p (o b)")
                    mm = g.tensor_tensor(g_diff[:, p], g_blk[:, :, p * C:(p + 1) * C],
                                         col.unsqueeze(2).broadcast_to([P, B, C]), ALU.subtract)
                mm.then_inc(s["diffed"], 1)
                pool.wait_ge(s["diffed"], m + 1)
                if not at_start(m):
                    pool.wait_ge(s["decayed"], m)
                rows = g_diff[:].rearrange("p s b x -> p (s b) x")
                wide = [P, 2 * B, C]
                g.tensor_tensor(dec_arg[:, 0].rearrange("p s b x -> p (s b) x"), k.mask_l[:].unsqueeze(1).broadcast_to(wide), rows,
                                ALU.subtract)
                g.tensor_tensor(dec_arg[:, 1].rearrange("p s b x -> p (s b) x"), k.mask_u[:].unsqueeze(1).broadcast_to(wide), rows,
                                ALU.add).then_inc(s["dec_args"], 1)

            def norms(m):
                pool.wait_ge(s["ssq_out"], m + 1)
                g.tensor_tensor(rn[:].rearrange("p k s b -> p (k s b)"), ssq[:].rearrange("p k s b -> p (k s b)"),
                                k.pow_half[:], ALU.pow).then_inc(s["rn_ready"], 1)
                pool.wait_ge(s["rn_ready"], 2 * m + 1)
                g.tensor_tensor(rn2[:], rn[:, 0], rn[:, 0], ALU.mult).then_inc(s["rn_ready"], 1)

            def scales(m, q):
                pool.wait_ge(s["rn_ready"], 2 * m + 2)
                if not isinstance(m, int):
                    pool.wait_ge(s["f_ready"], 2 * m - 1)
                    pool.wait_ge(s["r_ready"], 2 * m - 2)
                if not at_start(m):
                    pool.wait_ge(s["vb_out"], 4 * m)
                    pool.wait_ge(s["l_ready"], m)
                two = slice(2 * q, 2 * q + 2)
                col = lambda t: t[:, bass.ds(2 * m, 2)]
                g.tensor_tensor(l_scale[:], rn2[:], col(k.minus_beta), ALU.mult)
                g.tensor_tensor(ks_scale[:, two], rn2[:], col(k.minus_beta_eg), ALU.mult)
                g.tensor_tensor(v_scale[:], rn[:, 0], col(k.half_beta), ALU.mult)
                g.tensor_copy(k_tail[:], col(k.tail_col))
                g.tensor_scalar(q_scale[:, two], rn[:, 1], D ** -0.5, None, ALU.mult).then_inc(s["q_steps"], 1)
                scaled, loaded = in_register(pool, m + 1), in_register(pool, 32 * m + 32)
                ready()
                pool.wait_ge(s["q_steps"], scaled)
                pool.wait_ge(s["e_in"], loaded)
                for p in range(2):
                    g.tensor_copy(s_dec[:, 2 * q + p], e_blk[:, :, :, p * C + C - 1].rearrange("p u b -> p b u"))
                g.tensor_tensor(q_scale2[:, two], q_scale[:, two], q_scale[:, two], ALU.mult).then_inc(s["cols_ready"], 1)

            def decay_queries(m, q):
                pool.wait_ge(s["e_in"], 32 * m + 32)
                if not isinstance(m, int):
                    pool.wait_ge(s["core_done"], 2 * m - 2)
                for p in range(2):
                    for b in range(B):
                        mm = g.tensor_tensor(qg[:, 2 * q + p, b], twice(kkq[:, q, b, p, 2]),
                                             e_blk[:, :, b, p * C:(p + 1) * C], ALU.mult)
                mm.then_inc(s["qg_ready"], 1)

            def first_product(m):
                pool.wait_ge(s["p_out"], 5 * m + 1)
                pool.wait_ge(s["u_out"], m + 1)
                mm = g.tensor_tensor(prod[:, 0], UL[:, 0, :, 0], k.ident_half[:].unsqueeze(1).broadcast_to([P, 2 * B, C]), ALU.add)
                mm.then_inc(s["p1_ready"], 1)

            def decay_state(st, n, slot):
                pool.wait_ge(s["s_updated"], st + 1)
                pool.wait_ge(s["cols_ready"], n + 1)
                f = lambda t: t[:].rearrange("p b u d -> p (b u) d")
                g.tensor_tensor(f(state_d), f(state), s_dec[:, slot].rearrange("p b u -> p (b u)").unsqueeze(2).broadcast_to([P, 2 * B, D]),
                                ALU.mult).then_inc(s["s_decayed"], 1)

            def rms_factor(st, slot):
                pool.wait_ge(s["squares_out"], 2 * st + 2)
                g.tensor_tensor(core_ms[:], core_ss[:], q_scale2[:, slot], ALU.mult).then_inc(s["f_steps"], 1)
                first = in_register(pool, 3 * st + 1)
                ready()
                pool.wait_ge(s["f_steps"], first)
                g.tensor_scalar(core_var[:], core_ms[:], 1.0 / D, EPS_RMS, ALU.mult, ALU.add).then_inc(s["f_steps"], 1)
                pool.wait_ge(s["f_steps"], 3 * st + 2)
                g.tensor_tensor(core_rs[:], core_var[:], k.pow_half[:, 0:B], ALU.pow).then_inc(s["f_steps"], 1)
                pool.wait_ge(s["f_steps"], 3 * st + 3)
                g.tensor_tensor(core_f[:], core_rs[:], q_scale[:, slot], ALU.mult).then_inc(s["f_ready"], 1)

            g.memset(credits[:, 0:1], 0.0).then_inc(s["f_ready"], 1)
            g.memset(credits[:, 1:2], 0.0).then_inc(s["ul_out"], 1)
            g.memset(credits[:, 2:3], 0.0).then_inc(s["core_out"], 1)
            g.memset(credits[:, 3:4], 0.0).then_inc(s["started"], 1)
            history(0, True)
            gate_differences(0)
            norms(0)
            scales(0, 0)
            decay_queries(0, 0)
            history(1, False)
            first_product(0)
            gate_differences(1)
            norms(1)
            scales(1, 1)

            def body(pair, rr, n, odd, crossing, last):
                m, q, st, slot = n + 1, 1 - odd, 2 * n, 2 * odd
                decay_state(st, n, slot)
                decay_queries(m, q)
                history(n + 2, crossing and not last)
                first_product(m)
                gate_differences(n + 2)
                rms_factor(st, slot)
                decay_state(st + 1, n, slot + 1)
                rms_factor(st + 1, slot + 1)
                norms(n + 2)
                scales(n + 2, odd)

            per_pair(pool, body)


class Kept:

    def __init__(self, ctx, nc):
        def sb(name, shape):
            return ctx.enter_context(nc.sbuf_tensor(name, shape, F32))

        self.x_tok = sb("x_tok", [P, NC, H])
        self.y_sum = sb("y_sum", [P, NC, H])
        self.xT = sb("xT", [P, KT, NC, B, C])
        self.ident = sb("ident", [P, P])
        self.ident_half = sb("ident_half", [P, C])
        self.ones_col = sb("ones_col", [P, 1])
        self.pow_half = sb("pow_half", [P, 4 * B])
        self.mask_l = sb("mask_l", [P, C])
        self.mask_u = sb("mask_u", [P, C])
        self.half_norm_w = sb("half_norm_w", [P, 1])
        self.g_col = sb("g_col", [P, NSTEPS + 4, B])
        self.tail_col = sb("tail_col", [P, NSTEPS + 4, B])
        self.half_beta = sb("half_beta", [P, NSTEPS + 4, B])
        self.minus_beta = sb("minus_beta", [P, NSTEPS + 4, B])
        self.minus_beta_eg = sb("minus_beta_eg", [P, NSTEPS + 4, B])
        self.token_rows = nc.dram_tensor("token_rows", (TOKENS, H + E), F32, kind="Internal").ap()
        self.tables = [nc.dram_tensor(f"table{t}", (TOKENS + CAP, H), F32, kind="Internal").ap() for t in range(NTAB)]
        self.slots = ctx.enter_context(nc.sbuf_tensor("slots", [CAP, E, 2], U32))
        self.g_rows = nc.dram_tensor("g_rows", (NK + 1, 2, NB, B, BLK), F32, kind="Internal").ap()
        self.e_rows = nc.dram_tensor("e_rows", (NK + 1, 2, NB, B, BLK), F32, kind="Internal").ap()


def by_token(rows):
    return rows[0:TOKENS].rearrange("(b c i) h -> b i c h", b=B, i=C)


def route(nc, io, k):
    with ExitStack() as ctx:
        def sb(name, shape, dt=F32):
            return ctx.enter_context(nc.sbuf_tensor(name, shape, dt))

        ps = [ctx.enter_context(nc.psum_tensor(f"route_bank{i}", [P, 512], F32)) for i in range(8)]
        rows = sb("rows", [P, NC, H + E])
        hn, weights = rows[:, :, 0:H], rows[:, :, H:]
        gate_w = sb("gate_w", [P, KT, E])
        bias = sb("bias", [P, E])
        per_expert = [P, NC, E]
        scores, biased, a_, b_, c_, sel, pos = (sb(n, per_expert) for n in ("scores", "biased", "work_a", "work_b", "work_c", "sel", "pos"))
        sel16 = sb("sel16", per_expert, F16)
        per_group = [P, NC, EG]
        m1, m2, cnt, gscore, rank = (sb(n, per_group) for n in ("m1", "m2", "cnt", "gscore", "rank"))
        before = sb("before", [P, EG, EG])
        resets = sb("resets", per_expert)
        top8 = sb("top8", [P, NC, 8])
        above, wsum, winv = sb("above", [P, NC]), sb("wsum", [P, NC]), sb("winv", [P, NC])
        earlier = sb("earlier", [P, NC + 1, E])
        tri16, halves16, cross16 = (sb(n, [P, P], F16) for n in ("tri16", "halves16", "cross16"))
        slot_no = sb("slot_no", [P, CAP])
        onehot = sb("onehot", [P, 2, E, CAP], F16)
        token_no = sb("token_no", [P, NC])
        token16 = sb("token16", [P, NC], F16)
        found_row = sb("found_row", [1, E * CAP])
        found = sb("found", [CAP, E])
        empty, spare = sb("empty", [CAP, E]), sb("spare", [CAP, 1])
        ln1, ln2 = LayerNorm(ctx, nc, "ln_attn"), LayerNorm(ctx, nc, "ln_mid")
        s = sems(ctx, nc, """loaded added consts consts_ready turned copied logits scored step top_done sel_ready counted 
            ranks_ready onehot_ready matched row_out spread rows_ready rows_out """)
        rows_of = lambda ap: ap.rearrange("p c e -> p (c e)")
        by_group = lambda ap: ap.rearrange("p c (g e) -> p (c g) e", g=EG)
        wide = [P, NC * EG, E // EG]

        block = ctx.enter_context(nc.Block())

        @block.sync
        def _(sp):
            sp.dma_start(gate_w[:], io["gate_w"]).then_inc(s["loaded"], 16)
            sp.dma_start(bias[:], io["bias"].partition_broadcast(P)).then_inc(s["loaded"], 16)
            sp.wait_ge(s["rows_ready"], 1)
            sp.wait_ge(ln2.sem("done"), GROUPS)
            for b in range(B):
                sp.dma_start(by_token(k.token_rows)[b], rows[u_half(b)]).then_inc(s["rows_out"], 16)
            sp.wait_ge(s["rows_out"], 32)

        @block.gpsimd
        def _(pool):
            g = nc.gpsimd
            done = [0]

            def one(ins):
                ins.then_inc(s["consts"], 1)
                done[0] += 1
                pool.wait_ge(s["consts"], done[0])

            one(g.memset(tri16[:], 1.0))
            one(g.affine_select(out=tri16[:], in_=tri16[:], compare_op=ALU.is_gt, fill=0.0, base=0, pattern=[[1, P]],
                                channel_multiplier=-1))
            one(g.memset(tri16[0:C, C:P], 0.0))
            one(g.memset(halves16[:], 0.0))
            one(g.memset(halves16[0:C, 0:C], 1.0))
            one(g.memset(halves16[C:P, C:P], 1.0))
            one(g.memset(cross16[:], 0.0))
            one(g.memset(cross16[0:C, C:P], 1.0))
            one(g.memset(before[:], 1.0))
            one(g.affine_select(out=before[:], in_=before[:], compare_op=ALU.is_gt, fill=0.0, base=0, pattern=[[1, EG], [-1, EG]],
                                channel_multiplier=0))
            one(g.memset(resets[:], 1.0))
            one(g.memset(resets[:, :, 0:1], 0.0))
            one(g.iota(slot_no[:], pattern=[[1, CAP]], base=0, channel_multiplier=0, allow_small_or_imprecise_dtypes=True))
            for b in range(B):
                one(g.iota(token_no[u_half(b)], pattern=[[C, NC]], base=1 + b * S, channel_multiplier=1,
                           allow_small_or_imprecise_dtypes=True))
            one(g.tensor_copy(token16[:], token_no[:]))
            one(g.iota(spare[:], pattern=[[0, 1]], base=TOKENS, channel_multiplier=1, allow_small_or_imprecise_dtypes=True))
            g.memset(earlier[:, 0:1], 0.0).then_inc(s["consts_ready"], 1)
            ln1.gpsimd(pool)
            ln2.gpsimd(pool)

        @block.scalar
        def _(act):
            a = nc.scalar
            ln1.scalar(act, hn)
            ln2.scalar(act, hn)
            for c in range(NC):
                act.wait_ge(s["turned"], c + 1)
                a.copy(k.xT[:, :, c], ps[c % 2][:, 0:KT * P].rearrange("p (k b i) -> p k b i", k=KT, b=B)).then_inc(s["copied"], 1)
            act.wait_ge(s["logits"], 1)
            for i in range(2):
                mm = a.activation(scores[:, i * 8:(i + 1) * 8], ps[2 + i][:].rearrange("p (c e) -> p c e", e=E), ACT.Sigmoid)
            mm.then_inc(s["scored"], 1)

        @block.tensor
        def _(pe):
            te = nc.tensor
            for c in range(NC):
                if c >= 2:
                    pe.wait_ge(s["copied"], c - 1)
                pe.wait_ge(ln2.sem("done"), c // GC + 1)
                for kt in range(KT):
                    mm = te.transpose(ps[c % 2][:, kt * P:(kt + 1) * P], hn[:, c, kt * P:(kt + 1) * P], k.ident[:])
                mm.then_inc(s["turned"], 1)
            pe.wait_ge(s["copied"], NC)
            pe.wait_ge(s["loaded"], 32)
            for c in range(NC):
                for kt in range(KT):
                    mm = te.matmul(ps[2 + c // 8][:, (c % 8) * E:(c % 8 + 1) * E], k.xT[:, kt, c].rearrange("p b i -> p (b i)"),
                                   gate_w[:, kt], start=(kt == 0), stop=(kt == KT - 1))
            mm.then_inc(s["logits"], 1)
            pe.wait_ge(s["sel_ready"], 1)
            pe.wait_ge(s["consts_ready"], 1)
            for i in range(2):
                r16 = rows_of(sel16[:])[:, i * 512:(i + 1) * 512]
                te.matmul(ps[4 + i][:], tri16[:], r16, start=True, stop=True)
                te.matmul(ps[6 + i][:], halves16[:], r16, start=True, stop=True)
            for c in range(NC):
                mm = te.matmul(ps[0][:, 0:E], cross16[:], sel16[:, c], start=(c == 0), stop=(c == NC - 1))
            mm.then_inc(s["counted"], 1)
            pe.wait_ge(s["ranks_ready"], 1)
            for c in range(NC):
                pe.wait_ge(s["onehot_ready"], c + 1)
                flat = onehot[:, c % 2].rearrange("p e s -> p (e s)")
                for q in range(6):
                    mm = te.matmul(ps[q][0:1, :], token16[:, c:c + 1], flat[:, q * 512:(q + 1) * 512], start=(c == 0), stop=(c == NC - 1))
                mm.then_inc(s["matched"], 1)
            pe.wait_ge(s["row_out"], 6)
            for e in range(E):
                mm = te.matmul(ps[6][0:CAP, e:e + 1], found_row[:, e * CAP:(e + 1) * CAP], k.ones_col[0:1], start=True, stop=True)
            mm.then_inc(s["spread"], 1)

        @block.vector
        def _(dve):
            v = nc.vector
            done = [0]

            def one(ins):
                ins.then_inc(s["step"], 1)
                done[0] += 1
                dve.wait_ge(s["step"], done[0])

            ln1.vector(dve, k.y_sum, hn)
            for g in range(GROUPS):
                a = slice(g * GC, (g + 1) * GC)
                dve.wait_ge(ln1.sem("done"), g + 1)
                v.tensor_tensor(k.x_tok[:, a], k.x_tok[:, a], hn[:, a], ALU.add).then_inc(s["added"], 1)
            ln2.vector(dve, k.x_tok, hn, lambda g: dve.wait_ge(s["added"], g + 1))
            dve.wait_ge(s["loaded"], 32)
            dve.wait_ge(s["scored"], 1)
            dve.wait_ge(s["consts_ready"], 1)
            one(v.tensor_tensor(biased[:], scores[:], bias[:].unsqueeze(1).broadcast_to(per_expert), ALU.add))
            gflat = lambda ap: ap.rearrange("p c g -> p (c g)")
            over = lambda ap: gflat(ap).unsqueeze(2).broadcast_to(wide)
            one(v.tensor_reduce(gflat(m1[:]), by_group(biased[:]), AX.X, ALU.max))
            one(v.tensor_tensor(by_group(a_[:]), by_group(biased[:]), over(m1[:]), ALU.is_equal))
            one(v.tensor_reduce(gflat(cnt[:]), by_group(a_[:]), AX.X, ALU.add))
            one(v.scalar_tensor_tensor(out=rows_of(b_[:]), in0=rows_of(a_[:]), scalar=NEG, in1=rows_of(biased[:]), op0=ALU.mult, op1=ALU.add))
            one(v.tensor_reduce(gflat(m2[:]), by_group(b_[:]), AX.X, ALU.max))
            one(v.tensor_scalar(cnt[:], cnt[:], 2.0, -2.0 * NEG, ALU.is_ge, ALU.mult))
            one(v.tensor_scalar(cnt[:], cnt[:], NEG, None, ALU.add))
            one(v.tensor_tensor(cnt[:], cnt[:], m1[:], ALU.min))
            one(v.tensor_tensor(m2[:], m2[:], cnt[:], ALU.max))
            one(v.tensor_tensor(gscore[:], m1[:], m2[:], ALU.add))
            pairs = [P, NC, EG, EG]
            as_pairs = lambda ap: ap.rearrange("p c (g h) -> p c g h", g=EG)
            other, own = gscore[:].unsqueeze(2).broadcast_to(pairs), gscore[:].unsqueeze(3).broadcast_to(pairs)
            one(v.tensor_tensor(as_pairs(a_[:]), other, own, ALU.is_gt))
            one(v.tensor_tensor(as_pairs(b_[:]), other, own, ALU.is_equal))
            one(v.tensor_tensor(b_[:], b_[:], before[:].rearrange("p g h -> p (g h)").unsqueeze(1).broadcast_to(per_expert), ALU.mult))
            one(v.tensor_tensor(a_[:], a_[:], b_[:], ALU.add))
            one(v.tensor_reduce(gflat(rank[:]), a_[:].rearrange("p c (g h) -> p (c g) h", g=EG), AX.X, ALU.add))
            one(v.tensor_scalar(rank[:], rank[:], float(KG), NEG, ALU.is_ge, ALU.mult))
            one(v.tensor_tensor(by_group(c_[:]), by_group(biased[:]), over(rank[:]), ALU.add))
            for c in range(NC):
                v.max(out=top8[:, c], in_=c_[:, c]).then_inc(s["top_done"], 1)
            dve.wait_ge(s["top_done"], NC)
            least = top8[:, :, TOP - 1:TOP].broadcast_to(per_expert)
            one(v.tensor_tensor(a_[:], c_[:], least, ALU.is_gt))
            one(v.tensor_tensor(b_[:], c_[:], least, ALU.is_equal))
            one(v.tensor_reduce(above[:], a_[:], AX.X, ALU.add))
            one(v.tensor_tensor_scan(rows_of(c_[:]), rows_of(resets[:]), rows_of(b_[:]), 0.0, ALU.mult, ALU.add))
            one(v.tensor_tensor(c_[:], c_[:], above[:].unsqueeze(2).broadcast_to(per_expert), ALU.add))
            one(v.scalar_tensor_tensor(out=rows_of(b_[:]), in0=rows_of(c_[:]), scalar=float(TOP), in1=rows_of(b_[:]), op0=ALU.is_le, op1=ALU.mult))
            one(v.tensor_tensor(sel[:], a_[:], b_[:], ALU.add))
            v.tensor_copy(sel16[:], sel[:]).then_inc(s["sel_ready"], 1)
            one(v.tensor_tensor(c_[:], scores[:], sel[:], ALU.mult))
            one(v.tensor_reduce(wsum[:], c_[:], AX.X, ALU.add))
            one(v.reciprocal(winv[:], wsum[:]))
            one(v.tensor_tensor(c_[:], c_[:], winv[:].unsqueeze(2).broadcast_to(per_expert), ALU.mult))
            v.tensor_scalar(weights, c_[:], ROUTE_SCALE, None, ALU.mult).then_inc(s["rows_ready"], 1)
            dve.wait_ge(s["counted"], 1)
            one(v.tensor_copy(earlier[:, 0], ps[0][:, 0:E]))
            for c in range(NC):
                one(v.tensor_tensor(earlier[:, c + 1], ps[6 + c // 8][:, (c % 8) * E:(c % 8 + 1) * E], earlier[:, c], ALU.add))
            for i in range(2):
                a8 = slice(i * 8, (i + 1) * 8)
                mm = v.tensor_tensor(pos[:, a8], ps[4 + i][:].rearrange("p (c e) -> p c e", e=E), earlier[:, a8], ALU.add)
                one(mm)
            one(v.tensor_scalar(b_[:], sel[:], -2.0 * CAP, 2.0 * CAP, ALU.mult, ALU.add))
            v.tensor_tensor(a_[:], pos[:], b_[:], ALU.add).then_inc(s["ranks_ready"], 1)
            dve.wait_ge(s["ranks_ready"], 1)
            for c in range(NC):
                if c >= 2:
                    dve.wait_ge(s["matched"], c - 1)
                v.tensor_tensor(onehot[:, c % 2], a_[:, c].unsqueeze(2).broadcast_to([P, E, CAP]),
                                slot_no[:].unsqueeze(1).broadcast_to([P, E, CAP]), ALU.is_equal).then_inc(s["onehot_ready"], 1)
            dve.wait_ge(s["matched"], NC)
            for q in range(6):
                v.tensor_copy(found_row[:, q * 512:(q + 1) * 512], ps[q][0:1, :]).then_inc(s["row_out"], 1)
            dve.wait_ge(s["spread"], 1)
            one(v.tensor_copy(found[:], ps[6][0:CAP, 0:E]))
            one(v.tensor_scalar(k.slots[:, :, 0], found[:], -1.0, 0.0, ALU.add, ALU.max))
            one(v.tensor_scalar(spare[:], spare[:], 1.0, None, ALU.add))
            one(v.tensor_scalar(empty[:], found[:], 0.0, spare[:], ALU.is_equal, ALU.mult))
            one(v.scalar_tensor_tensor(out=k.slots[:, :, 1], in0=found[:], scalar=-1.0, in1=empty[:], op0=ALU.add, op1=ALU.add))


def experts(nc, io, k):
    with ExitStack() as ctx:
        def sb(name, shape, dt=F32):
            return ctx.enter_context(nc.sbuf_tensor(name, shape, dt))

        ps = [ctx.enter_context(nc.psum_tensor(f"moe_bank{i}", [P, 512], F32)) for i in range(8)]
        wsg, wsu, wsd = sb("wsg", [P, KT, F]), sb("wsu", [P, KT, F]), sb("wsd", [F, H])
        w_in = sb("w_gate_up", [P, NTAB, 2, KT, F])
        w_down = sb("w_down", [F, NTAB, H])
        at = sb("slot_rows", [CAP, NTAB, 2], U32)
        xg = sb("gathered", [CAP, NTAB, H + E])
        xgT = sb("gatheredT", [P, 2, KT, CAP])
        act_g = sb("act_g", [F, 2, CAP])
        hidden = sb("hidden", [F, 2, CAP])
        scaled = sb("scaled", [CAP, NTAB, H])
        credit = sb("credit", [1, 1])
        sh_g = sb("sh_g", [F, 2, 512])
        sh_h = sb("sh_h", [F, 2, 512])
        s = sems(ctx, nc, "sh_in pool_started sh_up sh_silu sh_hidden sh_down sh_out located " +
                 "turned turn_out upped silued multiplied downed weighted " +
                 " ".join(f"w_in_{t} gathered_{t} added_{t}" for t in range(NTAB)))
        NSH = 4

        block = ctx.enter_context(nc.Block())

        @block.sync
        def _(sp):
            for dst, src in ((wsg, "ws_gate"), (wsu, "ws_up"), (wsd, "ws_down")):
                sp.dma_start(dst[:], io[src]).then_inc(s["sh_in"], 16)

            def load(e, t):
                sp.dma_start(w_in[:, t], io["w_gate_up"][bass.ds(e, 1)].rearrange("o p g k f -> (o p) g k f")).then_inc(s[f"w_in_{t}"], 16)
                sp.dma_start(w_down[:, t], io["w_down"][bass.ds(e, 1)].rearrange("o f h -> (o f) h")).then_inc(s[f"w_in_{t}"], 16)

            for t in range(NTAB):
                load(t, t)
            with sp.Fori(0, E // NTAB - 1) as r:
                for t in range(NTAB):
                    sp.wait_ge(s["downed"], r * NTAB + t + 1)
                    load(r * NTAB + NTAB + t, t)
            for t in range(NTAB):
                sp.wait_ge(s[f"w_in_{t}"], 32 * (E // NTAB))

        @block.gpsimd
        def _(pool):
            g = nc.gpsimd

            def gather(e, r, t):
                g.tensor_copy(at[:, t], k.slots[:, bass.ds(e, 1)].rearrange("p o w -> p (o w)")).then_inc(s["located"], 1)
                made = in_register(pool, e + 1)
                pool.wait_ge(s["pool_started"], 1)
                pool.wait_ge(s["located"], made)
                g.indirect_dma_start(xg[:, t], None, k.token_rows, bass.IndirectOffsetOnAxis(ap=at[:, t, 0:1], axis=0),
                                     bounds_check=TOKENS - 1, oob_is_err=True).then_inc(s[f"gathered_{t}"], 16)

            def add(e, r, t):
                done = in_register(pool, e + 2)
                pool.wait_ge(s["pool_started"], 1)
                pool.wait_ge(s["weighted"], done)
                g.indirect_dma_start(k.tables[t], bass.IndirectOffsetOnAxis(ap=at[:, t, 1:2], axis=0), scaled[:, t], None,
                                     bounds_check=TOKENS + CAP - 1, oob_is_err=True, compute_op=ALU.add).then_inc(s[f"added_{t}"], 16)

            g.memset(credit[:], 0.0).then_inc(s["pool_started"], 1)
            for t in range(NTAB):
                gather(t, 0, t)
            with pool.Fori(0, E // NTAB - 1) as r:
                for t in range(NTAB):
                    add(r * NTAB + t, r, t)
                for t in range(NTAB):
                    landed = in_register(pool, 16 * (r + 1))
                    pool.wait_ge(s["pool_started"], 1)
                    pool.wait_ge(s[f"added_{t}"], landed)
                    gather(r * NTAB + NTAB + t, r + 1, t)
            for t in range(NTAB):
                add(E - NTAB + t, E // NTAB - 1, t)
            for t in range(NTAB):
                pool.wait_ge(s[f"added_{t}"], 16 * (E // NTAB))

        def per_expert(eng, body):
            with eng.Fori(0, E // NTAB) as r:
                for t in range(NTAB):
                    body(r * NTAB + t, r, t)

        @block.tensor
        def _(pe):
            te = nc.tensor
            pe.wait_ge(s["sh_in"], 48)
            for q in range(NSH):
                if q >= 2:
                    pe.wait_ge(s["sh_hidden"], q - 1)
                for g, w in enumerate((wsg, wsu)):
                    for kt in range(KT):
                        mm = te.matmul(ps[2 * (q % 2) + g][0:F, :], w[:, kt], k.xT[:, kt, 4 * q:4 * q + 4].rearrange("p c b i -> p (c b i)"),
                                       start=(kt == 0), stop=(kt == KT - 1))
                mm.then_inc(s["sh_up"], 1)
                pe.wait_ge(s["sh_hidden"], q + 1)
                for c in range(4):
                    n = 4 * q + c
                    if n >= 2:
                        pe.wait_ge(s["sh_out"], n - 1)
                    te.matmul(ps[4 + n % 2][:, 0:H], sh_h[:, q % 2, c * P:(c + 1) * P], wsd[:], start=True, stop=True).then_inc(s["sh_down"], 1)
            pe.wait_ge(s["sh_out"], NC)

            def body(e, r, t):
                w = t % 2
                landed, before = in_register(pe, 16 * (r + 1)), in_register(pe, e)
                pe.wait_ge(s["sh_in"], 48)
                pe.wait_ge(s[f"gathered_{t}"], landed)
                pe.wait_ge(s["weighted"], before)
                for kt in range(KT):
                    mm = te.transpose(ps[w][:, kt * CAP:(kt + 1) * CAP], xg[:, t, kt * P:(kt + 1) * P], k.ident[0:CAP, 0:CAP])
                mm.then_inc(s["turned"], 1)
                pe.wait_ge(s[f"w_in_{t}"], 32 * (r + 1))
                pe.wait_ge(s["turn_out"], e + 1)
                for g in range(2):
                    for kt in range(KT):
                        mm = te.matmul(ps[2 + w][0:F, g * CAP:(g + 1) * CAP], w_in[:, t, g, kt], xgT[:, w, kt],
                                       start=(kt == 0), stop=(kt == KT - 1))
                mm.then_inc(s["upped"], 1)
                pe.wait_ge(s["multiplied"], e + 1)
                te.matmul(ps[4 + w][0:CAP, 0:H], hidden[:, w], w_down[:, t], start=True, stop=True).then_inc(s["downed"], 1)

            per_expert(pe, body)

        @block.scalar
        def _(act):
            a = nc.scalar
            for q in range(NSH):
                act.wait_ge(s["sh_up"], q + 1)
                if q >= 2:
                    act.wait_ge(s["sh_hidden"], q - 1)
                a.activation(sh_g[:, q % 2], ps[2 * (q % 2)][0:F, :], ACT.Silu).then_inc(s["sh_silu"], 1)
                for c in range(4):
                    n = 4 * q + c
                    act.wait_ge(s["sh_down"], n + 1)
                    a.copy(k.y_sum[:, n], ps[4 + n % 2][:, 0:H]).then_inc(s["sh_out"], 1)

            def body(e, r, t):
                w = t % 2
                act.wait_ge(s["turned"], e + 1)
                a.copy(xgT[:, w].rearrange("p k s -> p (k s)"), ps[w][:, 0:KT * CAP]).then_inc(s["turn_out"], 1)
                act.wait_ge(s["upped"], e + 1)
                a.activation(act_g[:, w], ps[2 + w][0:F, 0:CAP], ACT.Silu).then_inc(s["silued"], 1)

            per_expert(act, body)

        @block.vector
        def _(dve):
            v = nc.vector
            for q in range(NSH):
                dve.wait_ge(s["sh_silu"], q + 1)
                if q >= 2:
                    dve.wait_ge(s["sh_down"], 4 * (q - 1))
                v.tensor_tensor(sh_h[:, q % 2], ps[2 * (q % 2) + 1][0:F, :], sh_g[:, q % 2], ALU.mult).then_inc(s["sh_hidden"], 1)
            v.memset(sh_g[0:1, 0, 0:1], 0.0).then_inc(s["weighted"], 1)

            def body(e, r, t):
                w = t % 2
                dve.wait_ge(s["silued"], e + 1)
                v.tensor_tensor(hidden[:, w], ps[2 + w][0:F, CAP:2 * CAP], act_g[:, w], ALU.mult).then_inc(s["multiplied"], 1)
                dve.wait_ge(s["downed"], e + 1)
                v.tensor_scalar(scaled[:, t], ps[4 + w][0:CAP, 0:H], xg[:, t, bass.ds(H + e, 1)], None, ALU.mult).then_inc(s["weighted"], 1)

            per_expert(dve, body)


def combine(nc, io, k, out):
    with ExitStack() as ctx:
        def sb(name, shape, dt=F32):
            return ctx.enter_context(nc.sbuf_tensor(name, shape, dt))

        part = [sb(f"part{t}", [P, NC, H]) for t in range(NTAB)]
        ln = LayerNorm(ctx, nc, "ln_out")
        s = sems(ctx, nc, "paired sums out_ready stored " + " ".join(f"parts_in_{g}" for g in range(GROUPS)))
        block = ctx.enter_context(nc.Block())
        groups = [slice(g * GC, (g + 1) * GC) for g in range(GROUPS)]

        @block.sync
        def _(sp):
            for g, a in enumerate(groups):
                for t in range(NTAB):
                    for b in range(B):
                        sp.dma_start(part[t][u_half(b), a], by_token(k.tables[t])[b][:, a]).then_inc(s[f"parts_in_{g}"], 16)
            for g, a in enumerate(groups):
                sp.wait_ge(s["out_ready"], g + 1)
                for b in range(B):
                    sp.dma_start(out[b].rearrange("(c i) h -> i c h", i=C)[:, a], part[0][u_half(b), a]).then_inc(s["stored"], 16)
            sp.wait_ge(s["stored"], 16 * B * GROUPS)

        @block.gpsimd
        def _(pool):
            for g, a in enumerate(groups):
                pool.wait_ge(s[f"parts_in_{g}"], 16 * B * NTAB)
                nc.gpsimd.tensor_tensor(part[2][:, a], part[2][:, a], part[3][:, a], ALU.add).then_inc(s["paired"], 1)
            ln.gpsimd(pool)

        @block.scalar
        def _(act):
            ln.scalar(act, part[0])

        @block.vector
        def _(dve):
            v = nc.vector

            def add_parts(g):
                a = groups[g]
                dve.wait_ge(s[f"parts_in_{g}"], 16 * B * NTAB)
                v.tensor_tensor(part[1][:, a], part[1][:, a], part[0][:, a], ALU.add).then_inc(s["sums"], 1)
                dve.wait_ge(s["paired"], g + 1)
                v.tensor_tensor(k.y_sum[:, a], k.y_sum[:, a], part[2][:, a], ALU.add).then_inc(s["sums"], 1)
                dve.wait_ge(s["sums"], 3 * g + 2)
                v.tensor_tensor(k.y_sum[:, a], k.y_sum[:, a], part[1][:, a], ALU.add).then_inc(s["sums"], 1)
                dve.wait_ge(s["sums"], 3 * g + 3)

            ln.vector(dve, k.y_sum, part[0], add_parts)
            for g, a in enumerate(groups):
                dve.wait_ge(ln.sem("done"), g + 1)
                v.tensor_tensor(part[0][:, a], part[0][:, a], k.x_tok[:, a], ALU.add).then_inc(s["out_ready"], 1)


def build(nc, io, out):
    with ExitStack() as ctx:
        k = Kept(ctx, nc)
        setup(nc, io, k)
        delta_rule(nc, io, k, NK)
        route(nc, io, k)
        experts(nc, io, k)
        combine(nc, io, k, out)


def laid_out(v):
    import numpy as np

    qkv, z = v["L0_attn_W_qkv"], v["L0_attn_W_z"]
    key_dim = NK * D

    def tiles_of(pair):
        rows = [qkv, qkv] + [qkv] * 2 + [z] * 2
        first = [key_dim + pair * D, pair * D] + [2 * key_dim + (2 * pair + u) * D for u in range(2)] + [(2 * pair + u) * D for u in range(2)]
        return rows, first

    w_proj, conv_w, w_out = [], [], []
    for pair in [*range(NK), NK - 1]:
        rows, first = tiles_of(pair)
        w_proj.append(np.stack([w[a:a + D] for w, a in zip(rows, first)]).reshape(NT, D, KT, P).transpose(3, 2, 0, 1))
        conv_w.append(np.stack([v["L0_attn_conv_w"][a:a + D] for a in first[:4]], axis=1))
        w_out.append(v["L0_attn_W_out"][:, 2 * pair * D:(2 * pair + 2) * D].reshape(H, 2, D).transpose(2, 1, 0))
    kfirst = lambda w: w.reshape(KT, P, w.shape[-1]).transpose(1, 0, 2)
    gate_up = np.stack([v["L0_ffn_w_gate"], v["L0_ffn_w_up"]], axis=1)
    return {
        "x": v["L0_attn_x"], "w_proj": np.stack(w_proj), "conv_w": np.stack(conv_w), "w_out": np.stack(w_out),
        "w_ba": np.concatenate([v["L0_attn_W_b"], v["L0_attn_W_a"]]).reshape(2 * NV, KT, P).transpose(2, 1, 0),
        "dt_bias": v["L0_attn_dt_bias"], "A_log": v["L0_attn_A_log"], "norm_w": v["L0_attn_norm_w"].reshape(D, 1),
        "gate_w": kfirst(v["L0_ffn_gate_w"]), "bias": v["L0_ffn_bias"],
        "w_gate_up": gate_up.reshape(E, 2, KT, P, F).transpose(0, 3, 1, 2, 4), "w_down": v["L0_ffn_w_down"],
        "ws_gate": kfirst(v["L0_ffn_ws_gate"]), "ws_up": kfirst(v["L0_ffn_ws_up"]), "ws_down": v["L0_ffn_ws_down"],
    }


def kernel(**inputs):
    import numpy as np
    import concourse.bacc as bacc
    from concourse.bass_utils import run_bass_kernel_spmd

    nc = bacc.Bacc("TRN2", target_bir_lowering=False, num_devices=1)
    arrays, io = {}, {}
    for name, a in laid_out({n: np.asarray(a) for n, a in inputs.items()}).items():
        arrays[f"in_{name}"] = np.ascontiguousarray(a)
        io[name] = nc.dram_tensor(f"in_{name}", a.shape, mybir.dt.from_np(a.dtype), kind="ExternalInput").ap()
    out = nc.dram_tensor("out", (B, S, H), F32, kind="ExternalOutput").ap()
    build(nc, io, out)
    got = run_bass_kernel_spmd(nc, [arrays], core_ids=[0])
    return got.results[0]["out"]
```

```python
from contextlib import ExitStack

import concourse.bass as bass
from concourse import mybir

ALU = mybir.AluOpType
ACT = mybir.ActivationFunctionType
AX = mybir.AxisListType
F32 = mybir.dt.float32
F16 = mybir.dt.float16
U32 = mybir.dt.uint32

P = 128
B, S, H = 2, 1024, 256
KT = H // P
D = 128
NK = 16
NV = 2 * NK
C = 64
NC = S // C
BLK = 2 * C
NB = S // BLK
NSTEPS = NK * NC
TAPS = 4
K_, Q_, V_, Z_ = 0, 1, 2, 4
NT = 6
NEG = -1e30
EPS_LN, EPS_RMS = 1e-5, 1e-6
E = 64
TOP = 6
EG, KG = 8, 4
F = 96
CAP = 48
ROUTE_SCALE = 2.5
NTAB = 4
TOKENS = B * S
GROUPS = 4
GC = NC // GROUPS
ZPARTS = 8
ZCOLS = (TOKENS + CAP) // 16 * H // ZPARTS


def twice(ap):
    return ap.unsqueeze(1).broadcast_to([ap.shape[0], 2, ap.shape[1]])


def sems(ctx, nc, names):
    return {n: ctx.enter_context(nc.semaphore(n)) for n in names.split()}


def at_start(count):
    return isinstance(count, int) and count == 0


def in_register(eng, count):
    if not isinstance(count, int):
        eng.compute_val(count)
    return count


def u_half(u):
    return slice(u * C, (u + 1) * C)


class LayerNorm:

    def __init__(self, ctx, nc, name):
        self.nc = nc
        self.total = ctx.enter_context(nc.sbuf_tensor(name + "_total", [P, NC], F32))
        self.mean = ctx.enter_context(nc.sbuf_tensor(name + "_mean", [P, NC], F32))
        self.sumsq = ctx.enter_context(nc.sbuf_tensor(name + "_sumsq", [P, NC], F32))
        self.var = ctx.enter_context(nc.sbuf_tensor(name + "_var", [P, NC], F32))
        self.inv = ctx.enter_context(nc.sbuf_tensor(name + "_inv", [P, NC], F32))
        self.minus_half = ctx.enter_context(nc.sbuf_tensor(name + "_minus_half", [P, GC], F32))
        self.squares = ctx.enter_context(nc.sbuf_tensor(name + "_squares", [P, H], F32))
        self.s = sems(ctx, nc, " ".join(f"{name}_{x}" for x in "averaged centred squared inverted done".split()))
        self.name = name

    def sem(self, what):
        return self.s[f"{self.name}_{what}"]

    def vector(self, eng, src, dst, before_group=None, after_group=None, lag=GROUPS):
        v = self.nc.vector
        for g in range(GROUPS + lag):
            if g < GROUPS:
                a = slice(g * GC, (g + 1) * GC)
                if before_group:
                    before_group(g)
                v.tensor_reduce(self.total[:, a], src[:, a], AX.X, ALU.add).then_inc(self.sem("averaged"), 1)
                eng.wait_ge(self.sem("averaged"), 2 * g + 1)
                v.tensor_scalar(self.mean[:, a], self.total[:, a], -1.0 / H, None, ALU.mult).then_inc(self.sem("averaged"), 1)
                eng.wait_ge(self.sem("averaged"), 2 * g + 2)
                v.tensor_tensor(dst[:, a], src[:, a], self.mean[:, a].unsqueeze(2).broadcast_to([P, GC, H]),
                                ALU.add).then_inc(self.sem("centred"), 1)
            if g >= lag:
                g -= lag
                a = slice(g * GC, (g + 1) * GC)
                eng.wait_ge(self.sem("inverted"), 2 * g + 3)
                v.tensor_tensor(dst[:, a], dst[:, a], self.inv[:, a].unsqueeze(2).broadcast_to([P, GC, H]),
                                ALU.mult).then_inc(self.sem("done"), 1)
                if after_group:
                    after_group(g)

    def scalar(self, eng, dst):
        a = self.nc.scalar
        for g in range(GROUPS):
            eng.wait_ge(self.sem("centred"), g + 1)
            for c in range(g * GC, (g + 1) * GC):
                if c:
                    eng.wait_ge(self.sem("squared"), c)
                a.activation(self.squares[:], dst[:, c], ACT.Square, accum_out=self.sumsq[:, c:c + 1]).then_inc(self.sem("squared"), 1)

    def gpsimd(self, eng, before_group=None):
        p = self.nc.gpsimd
        p.memset(self.minus_half[:], -0.5).then_inc(self.sem("inverted"), 1)
        for g in range(GROUPS):
            a = slice(g * GC, (g + 1) * GC)
            if before_group:
                before_group(g)
            eng.wait_ge(self.sem("squared"), (g + 1) * GC)
            p.tensor_scalar(self.var[:, a], self.sumsq[:, a], 1.0 / H, EPS_LN, ALU.mult, ALU.add).then_inc(self.sem("inverted"), 1)
            eng.wait_ge(self.sem("inverted"), 2 * g + 2)
            p.tensor_tensor(self.inv[:, a], self.var[:, a], self.minus_half[:], ALU.pow).then_inc(self.sem("inverted"), 1)


def setup(nc, io, k):
    with ExitStack() as ctx:
        def sb(name, shape, dt=F32):
            return ctx.enter_context(nc.sbuf_tensor(name, shape, dt))

        ps = [ctx.enter_context(nc.psum_tensor(f"setup_bank{i}", [P, 512], F32)) for i in range(6)]
        xn = sb("xn", [P, NC, H])
        w_ba = sb("w_ba", [P, KT, 2 * NV])
        dt_row, a_row, neg_a = sb("dt_row", [P, NV]), sb("a_row", [P, NV]), sb("neg_a", [P, NV])
        tri, halves = sb("tri", [P, P]), sb("halves", [P, P])
        gate_shape = [P, NC, NV]
        beta, pre, soft, g, g_sum, g_last = (sb(n, gate_shape) for n in ("beta", "pre", "soft", "g", "g_sum", "g_last"))
        gT, eT = sb("gT", [NV, B, S]), sb("eT", [NV, B, S])
        zeros = sb("zeros", [2, NB * B * BLK])
        zeros_wide = sb("zeros_wide", [16, ZCOLS])
        beta_hc, g_hc, last_hc = (sb(n, [P, 2, NK, NC]) for n in ("beta_hc", "g_hc", "last_hc"))
        beta_col, g_col, last_col, eg_col = (sb(n, [P, B, NSTEPS]) for n in ("beta_col", "g_sum_col", "last_col", "eg_col"))
        ln = LayerNorm(ctx, nc, "ln_in")
        s = sems(ctx, nc, """x_in weights_in tables_zeroed masks_cleared masks_ready turned x_copied ba_done summed row_turned
            pre_ready gate_exp gate_log gate_step gates_done hc_done sums_out rows_copied rows_exp rows_out cols_in col_exp col_step
            cols_done""")
        flat = lambda ap: ap.rearrange("p c h -> p (c h)")

        block = ctx.enter_context(nc.Block())

        @block.sync
        def _(sp):
            for b in range(B):
                sp.dma_start(k.x_tok[b * C:(b + 1) * C], io["x"][b].rearrange("(c i) h -> i c h", i=C)).then_inc(s["x_in"], 16)
            for dst, src in ((w_ba[:], io["w_ba"]), (dt_row[:], io["dt_bias"].partition_broadcast(P)),
                             (a_row[:], io["A_log"].partition_broadcast(P)), (k.half_norm_w[:], io["norm_w"])):
                sp.dma_start(dst, src).then_inc(s["weights_in"], 16)
            sp.wait_ge(s["masks_cleared"], 1)
            for t in range(NTAB):
                rows = k.tables[t].rearrange("(p q) h -> p (q h)", q=(TOKENS + CAP) // 16)
                for part in range(ZPARTS):
                    sp.dma_start(rows[:, part * ZCOLS:(part + 1) * ZCOLS], zeros_wide[0:16]).then_inc(s["tables_zeroed"], 16)
            sp.wait_ge(s["hc_done"], 3)
            for src, dst in ((g_hc, g_col), (beta_hc, beta_col), (last_hc, last_col)):
                for u in range(2):
                    for b in range(B):
                        sp.dma_start(dst[u_half(u), b], src[u_half(b), u].rearrange("p j c -> p (j c)")).then_inc(s["cols_in"], 16)
            sp.wait_ge(s["rows_exp"], 1)
            sp.wait_ge(s["rows_copied"], 4)
            for src, dst in ((gT, k.g_rows), (eT, k.e_rows)):
                for b in range(B):
                    sp.dma_start(dst[0:NK].rearrange("j u r b t -> (j u) r b t")[:, :, b],
                                 src[:, b].rearrange("h (r t) -> h r t", r=NB)).then_inc(s["rows_out"], 16)
                sp.dma_start(dst[NK].rearrange("u r b t -> u (r b t)"), zeros[:]).then_inc(s["rows_out"], 16)
            sp.wait_ge(s["rows_out"], 16 * 6)
            sp.wait_ge(s["tables_zeroed"], 16 * NTAB * ZPARTS)

        @block.gpsimd
        def _(pool):
            g_ = nc.gpsimd
            g_.memset(k.ident[:], 0.0)
            g_.memset(k.ident_half[:], 0.0)
            g_.memset(tri[:], 1.0)
            g_.memset(halves[:], 0.0)
            g_.memset(k.mask_l[:], 0.0)
            g_.memset(k.mask_u[:], 0.0)
            g_.memset(k.ones_col[:], 1.0)
            g_.memset(k.pow_half[:], -0.5)
            for t in (k.g_col, k.tail_col, k.half_beta, k.minus_beta, k.minus_beta_eg):
                g_.memset(t[:, NSTEPS:], 0.0)
            g_.memset(zeros_wide[:], 0.0)
            g_.memset(zeros[:], 0.0).then_inc(s["masks_cleared"], 1)
            pool.wait_ge(s["masks_cleared"], 1)
            g_.affine_select(out=k.ident[:], in_=k.ident[:], compare_op=ALU.not_equal, fill=1.0, base=0,
                             pattern=[[-1, P]], channel_multiplier=1)
            g_.affine_select(out=tri[:], in_=tri[:], compare_op=ALU.is_ge, fill=0.0, base=0,
                             pattern=[[1, P]], channel_multiplier=-1).then_inc(s["masks_cleared"], 1)
            steps = 2
            for u in range(2):
                h = u_half(u)
                for make in (lambda: g_.memset(halves[h, h], 1.0),
                             lambda: g_.affine_select(out=k.ident_half[h], in_=k.ident_half[h], compare_op=ALU.not_equal, fill=1.0,
                                                      base=0, pattern=[[-1, C]], channel_multiplier=1),
                             lambda: g_.affine_select(out=k.mask_l[h], in_=k.mask_l[h], compare_op=ALU.is_gt, fill=NEG, base=0,
                                                      pattern=[[-1, C]], channel_multiplier=1),
                             lambda: g_.affine_select(out=k.mask_u[h], in_=k.mask_u[h], compare_op=ALU.is_ge, fill=NEG, base=0,
                                                      pattern=[[1, C]], channel_multiplier=-1)):
                    pool.wait_ge(s["masks_cleared"], steps)
                    make().then_inc(s["masks_cleared"], 1)
                    steps += 1
            pool.wait_ge(s["masks_cleared"], steps)
            g_.memset(tri[0:C, C:P], 0.0).then_inc(s["masks_ready"], 1)
            pool.wait_ge(s["masks_ready"], 1)
            ln.gpsimd(pool)

        @block.vector
        def _(dve):
            v = nc.vector
            dve.wait_ge(s["x_in"], 32)
            ln.vector(dve, k.x_tok, xn)
            dve.wait_ge(s["weights_in"], 64)
            dve.wait_ge(s["ba_done"], 1)
            for i in range(2):
                a8 = slice(i * 8, (i + 1) * 8)
                v.tensor_tensor(pre[:, a8], ps[2 + i][:].rearrange("p (c h) -> p c h", c=8)[:, :, NV:],
                                dt_row[:].unsqueeze(1).broadcast_to([P, 8, NV]), ALU.add).then_inc(s["gate_step"], 1)
            v.tensor_scalar(k.half_norm_w[:], k.half_norm_w[:], 0.5, None, ALU.mult)
            dve.wait_ge(s["gate_step"], 2)
            v.tensor_scalar(soft[:], pre[:], -1.0, None, ALU.mult).then_inc(s["gate_step"], 1)
            dve.wait_ge(s["gate_step"], 3)
            v.tensor_tensor(soft[:], soft[:], pre[:], ALU.min).then_inc(s["pre_ready"], 1)
            dve.wait_ge(s["gate_log"], 1)
            v.tensor_scalar(pre[:], pre[:], 0.0, None, ALU.max).then_inc(s["gate_step"], 1)
            v.tensor_scalar(neg_a[:], neg_a[:], -1.0, None, ALU.mult).then_inc(s["gate_step"], 1)
            dve.wait_ge(s["gate_step"], 5)
            v.tensor_tensor(soft[:], soft[:], pre[:], ALU.add).then_inc(s["gate_step"], 1)
            dve.wait_ge(s["gate_step"], 6)
            v.tensor_tensor(g[:], soft[:], neg_a[:].unsqueeze(1).broadcast_to([P, NC, NV]), ALU.mult).then_inc(s["gates_done"], 1)
            dve.wait_ge(s["summed"], 1)
            v.tensor_copy(flat(g_sum[:]), ps[4][:]).then_inc(s["sums_out"], 1)
            v.tensor_copy(flat(g_last[:]), ps[5][:]).then_inc(s["sums_out"], 1)
            dve.wait_ge(s["sums_out"], 2)
            dve.wait_ge(s["gate_exp"], 2)
            for src, dst in ((g_sum, g_hc), (g_last, last_hc), (beta, beta_hc)):
                for u in range(2):
                    mm = v.tensor_copy(dst[:, u], src[:].rearrange("p c (j u) -> p u j c", u=2)[:, u])
                mm.then_inc(s["hc_done"], 1)
            dve.wait_ge(s["row_turned"], 1)
            for i in range(4):
                v.tensor_copy(gT[:, :, i * 4 * C:(i + 1) * 4 * C].rearrange("h b (c i) -> h c b i", i=C),
                              ps[i][0:NV].rearrange("h (c b i) -> h c b i", c=4, b=B)).then_inc(s["rows_copied"], 1)
            dve.wait_ge(s["cols_in"], 16 * 12)
            to = lambda t: t[:, 0:NSTEPS].rearrange("p s b -> p b s")
            v.tensor_scalar(to(k.half_beta), beta_col[:], 0.5, None, ALU.mult)
            v.tensor_scalar(to(k.minus_beta), beta_col[:], -1.0, None, ALU.mult).then_inc(s["col_step"], 1)
            v.tensor_copy(to(k.g_col), g_col[:])
            v.tensor_tensor(last_col[:], last_col[:], g_col[:], ALU.subtract).then_inc(s["col_step"], 1)
            dve.wait_ge(s["col_step"], 2)
            dve.wait_ge(s["col_exp"], 1)
            v.tensor_tensor(to(k.minus_beta_eg), to(k.minus_beta), eg_col[:], ALU.mult)

        @block.scalar
        def _(act):
            a = nc.scalar
            ln.scalar(act, xn)
            for c in range(NC):
                act.wait_ge(s["turned"], c + 1)
                a.copy(k.xT[:, :, c], ps[c % 2][:, 0:KT * P].rearrange("p (k b i) -> p k b i", k=KT, b=B)).then_inc(s["x_copied"], 1)
            act.wait_ge(s["weights_in"], 64)
            a.activation(neg_a[:], a_row[:], ACT.Exp)
            act.wait_ge(s["pre_ready"], 1)
            a.activation(g[:], soft[:], ACT.Exp).then_inc(s["gate_exp"], 1)
            act.wait_ge(s["gate_exp"], 1)
            a.activation(soft[:], g[:], ACT.Ln, bias=k.ones_col[:]).then_inc(s["gate_log"], 1)
            for i in range(2):
                a8 = slice(i * 8, (i + 1) * 8)
                last = a.activation(beta[:, a8], ps[2 + i][:].rearrange("p (c h) -> p c h", c=8)[:, :, 0:NV], ACT.Sigmoid)
            last.then_inc(s["gate_exp"], 1)
            act.wait_ge(s["rows_copied"], 4)
            a.activation(eT[:], gT[:], ACT.Exp).then_inc(s["rows_exp"], 1)
            act.wait_ge(s["cols_in"], 16 * 12)
            a.activation(eg_col[:], g_col[:], ACT.Exp).then_inc(s["col_exp"], 1)
            act.wait_ge(s["col_step"], 2)
            a.activation(k.tail_col[:, 0:NSTEPS].rearrange("p s b -> p b s"), last_col[:], ACT.Exp).then_inc(s["cols_done"], 1)

        @block.tensor
        def _(pe):
            pe.wait_ge(s["masks_ready"], 1)
            for c in range(NC):
                if c >= 2:
                    pe.wait_ge(s["x_copied"], c - 1)
                pe.wait_ge(ln.sem("done"), c // GC + 1)
                for kt in range(KT):
                    mm = nc.tensor.transpose(ps[c % 2][:, kt * P:(kt + 1) * P], xn[:, c, kt * P:(kt + 1) * P], k.ident[:])
                mm.then_inc(s["turned"], 1)
            pe.wait_ge(s["x_copied"], NC)
            pe.wait_ge(s["weights_in"], 64)
            for c in range(NC):
                for kt in range(KT):
                    mm = nc.tensor.matmul(ps[2 + c // 8][:, (c % 8) * 2 * NV:(c % 8 + 1) * 2 * NV], k.xT[:, kt, c].rearrange("p b i -> p (b i)"),
                                          w_ba[:, kt], start=(kt == 0), stop=(kt == KT - 1))
            mm.then_inc(s["ba_done"], 1)
            pe.wait_ge(s["gates_done"], 1)
            nc.tensor.matmul(ps[4][:], tri[:], flat(g[:]), start=True, stop=True)
            nc.tensor.matmul(ps[5][:], halves[:], flat(g[:]), start=True, stop=True).then_inc(s["summed"], 1)
            pe.wait_ge(s["sums_out"], 2)
            pe.wait_ge(s["gate_exp"], 2)
            for c in range(NC):
                mm = nc.tensor.transpose(ps[c // 4][0:NV, (c % 4) * P:(c % 4 + 1) * P], g_sum[:, c], k.ident[:])
            mm.then_inc(s["row_turned"], 1)


def delta_rule(nc, io, k, pairs):
    with ExitStack() as ctx:
        def sb(name, shape, dt=F32):
            return ctx.enter_context(nc.sbuf_tensor(name, shape, dt))

        bank = [ctx.enter_context(nc.psum_tensor(f"bank{i}", [P, 512], F32)) for i in range(8)]
        w_proj = sb("w_proj", [P, KT, Z_, P])
        w_z = sb("w_z", [P, KT, NT - Z_, P])
        w_out = sb("w_out", [P, 2, H])
        conv_w = sb("conv_w", [P, 4, TAPS])
        raw = sb("raw", [P, 4, B, TAPS - 1 + BLK])
        conv = sb("conv", [P, 4, B, BLK])
        th = sb("th", [P, 4, B, BLK])
        vs = sb("vs", [P, B, 2, 2, C])
        thz = sb("thz", [P, 2, B, BLK])
        zs = sb("zs", [P, 2, 2, B, BLK])
        sq = sb("sq", [P, 2 * B, 2, C])
        g_blk = sb("g_blk", [P, B, BLK])
        e_blk = sb("e_blk", [P, 2, B, BLK])
        g_diff = sb("g_diff", [P, 2, B, C])
        dec_arg = sb("dec_arg", [P, 2, 2, B, C])
        dec = sb("dec", [P, 2, 2, B, C])
        ssq = sb("ssq", [P, 2, 2, B])
        rn = sb("rn", [P, 2, 2, B])
        rn2 = sb("rn2", [P, 2, B])
        l_scale = sb("l_scale", [P, 2, B])
        v_scale = sb("v_scale", [P, 2, B])
        k_tail = sb("k_tail", [P, 2, B])
        rounds = sb("rounds", [P, 2, 2 * B, 3, C])
        L_, U_, PROD = 0, 1, 2
        kkq = sb("kkq", [P, 2, B, 2, 3, C])
        qg = sb("qg", [P, 4, B, 2, C])
        s_dec = sb("s_dec", [P, 4, B, 2])
        ks_scale = sb("ks_scale", [P, 4, B])
        q_scale = sb("q_scale", [P, 4, B])
        q_scale2 = sb("q_scale2", [P, 4, B])
        attnT = sb("attnT", [P, 4, B, C])
        vb = sb("vb", [P, 4, B, D])
        kdec = sb("kdec", [P, 4, B, D])
        inv = sb("inv", [P, 4, B, C])
        r = sb("r", [P, B, D])
        vt = sb("vt", [P, B, D])
        state = sb("state", [P, B, 2, D])
        state_d = sb("state_d", [P, B, 2, D])
        squares = sb("squares", [P, B, D])
        core_ss, core_ms, core_var, core_rs, core_f = (sb(n, [P, B]) for n in ("core_ss", "core_ms", "core_var", "core_rs", "core_f"))
        core_n = sb("core_n", [P, B, D])
        gated = sb("gated", [P, 2, B, C])
        credits = sb("credits", [P, 6])

        s = sems(ctx, nc, """w_in w_z_in conv_w_in w_out_in g_in e_in started
            projected_kq projected_v projected_z ssq_summed grammed turned u_turned squared powered
            ks_done vt_done core_done grown_0 grown_1 core_turned y_projected
            raw_in tap_in conv_tanhed z_tanhed decayed vb_out u_out ul_out vt_out squares_out core_out
            conv_steps kqv_ready z_ready ssq_out l_ready attn_ready p_out r_ready s_updated gated_out y_added
            hist_done kq_squared rn_ready diffed dec_args qg_ready cols_ready q_steps p1_ready
            s_decayed f_steps f_ready u_copied""")

        def per_pair(eng, body):
            with eng.Fori(0, pairs) as pair:
                with eng.Fori(0, NB // 2 - 1) as r2:
                    for odd in range(2):
                        body(pair, 2 * r2 + odd, pair * NB + 2 * r2 + odd, odd, False, False)
                body(pair, NB - 2, pair * NB + NB - 2, 0, True, False)
                body(pair, NB - 1, pair * NB + NB - 1, 1, True, True)

        block = ctx.enter_context(nc.Block())

        @block.sync
        def _(sp):
            def load_projection(pair):
                src = io["w_proj"][bass.ds(pair, 1)].rearrange("o p k t c -> (o p) k t c")
                sp.dma_start(w_proj[:], src[:, :, 0:Z_]).then_inc(s["w_in"], 16)
                sp.dma_start(conv_w[:], io["conv_w"][bass.ds(pair, 1)].rearrange("o p t w -> (o p) t w")).then_inc(s["conv_w_in"], 16)

            def load_w_z(pair):
                src = io["w_proj"][bass.ds(pair, 1)].rearrange("o p k t c -> (o p) k t c")
                sp.dma_start(w_z[:], src[:, :, Z_:]).then_inc(s["w_z_in"], 16)

            def load_w_out(pair):
                sp.dma_start(w_out[:], io["w_out"][bass.ds(pair, 1)].rearrange("o p u h -> (o p) u h")).then_inc(s["w_out_in"], 16)

            def load_g(pair, rr):
                for u in range(2):
                    src = k.g_rows[bass.ds(pair, 1), u, bass.ds(rr, 1)].rearrange("o q b t -> (o q) (b t)")
                    sp.dma_start(g_blk[u_half(u)], src.broadcast_to([C, B * BLK])).then_inc(s["g_in"], 16)

            def load_e(pair, rr):
                for u in range(2):
                    src = k.e_rows[bass.ds(pair, 1), u, bass.ds(rr, 1)].rearrange("o q b t -> (o q) (b t)")
                    sp.dma_start(e_blk[:, u], src.broadcast_to([P, B * BLK])).then_inc(s["e_in"], 16)

            load_projection(0)
            load_w_z(0)
            load_g(0, 0)
            load_e(0, 0)
            load_w_out(0)
            for m in range(2):
                sp.wait_ge(s["diffed"], m + 1)
                load_g(0, m + 1)
            sp.wait_ge(s["qg_ready"], 1)
            load_e(0, 1)

            def body(pair, rr, n):
                ahead = lambda by: (pair, rr + by) if rr_is_low(rr, by) else (pair + 1, rr + by - NB)
                if isinstance(rr, int) and rr == NB - 2:
                    sp.wait_ge(s["projected_v"], n + 2)
                    sp.wait_ge(s["conv_steps"], 12 * n + 24)
                    load_projection(pair + 1)
                if isinstance(rr, int) and rr == NB - 1:
                    sp.wait_ge(s["projected_z"], n + 1)
                    load_w_z(pair + 1)
                sp.wait_ge(s["qg_ready"], n + 2)
                load_e(*ahead(2))
                sp.wait_ge(s["diffed"], n + 3)
                load_g(*ahead(3))
                if isinstance(rr, int) and rr == NB - 1:
                    sp.wait_ge(s["y_projected"], 2 * n + 2)
                    load_w_out(pair + 1)

            rr_is_low = lambda rr, by: not isinstance(rr, int) or rr + by < NB
            with sp.Fori(0, pairs) as pair:
                with sp.Fori(0, NB - 3) as rr:
                    body(pair, rr, pair * NB + rr)
                for rr in range(NB - 3, NB):
                    body(pair, rr, pair * NB + rr)
            for name in ("w_in", "w_z_in", "conv_w_in", "w_out_in"):
                sp.wait_ge(s[name], 16 * (pairs + 1))
            sp.wait_ge(s["g_in"], 32 * (pairs * NB + 3))
            sp.wait_ge(s["e_in"], 32 * (pairs * NB + 2))

        @block.tensor
        def _(pe):
            te = nc.tensor

            def project(rr, tile, bk, place, done=None):
                for kt in range(KT):
                    w = w_z[:, kt, tile - Z_] if tile >= Z_ else w_proj[:, kt, tile]
                    mm = te.matmul(bank[bk][:, place * 2 * BLK:(place + 1) * 2 * BLK], w,
                                   k.xT[:, kt, bass.ds(rr * 2, 2)].rearrange("p c b i -> p b c i"), start=(kt == 0), stop=(kt == KT - 1))
                if done:
                    mm.then_inc(s[done], 1)

            def sum_squares(m):
                pe.wait_ge(s["kq_squared"], m + 1)
                pe.wait_ge(s["raw_in"], 2 * m + 2)
                for kq in range(2):
                    for p in range(2):
                        for b in range(B):
                            i = (kq * 2 + p) * B + b
                            for u in range(2):
                                mm = te.matmul(bank[1][u_half(u), i:i + 1], sq[:, b * 2 + p, kq], k.ones_col[:], start=True, stop=True)
                mm.then_inc(s["ssq_summed"], 1)

            def gram(m, q):
                pe.wait_ge(s["kqv_ready"], 2 * m + 1)
                for p in range(2):
                    for b in range(B):
                        i = p * B + b
                        mm = te.matmul(bank[3][:, i * P:(i + 1) * P], kkq[:, q, b, p, 0:2].rearrange("p u i -> p (u i)"),
                                       kkq[:, q, b, p, 1:3], start=True, stop=True)
                mm.then_inc(s["grammed"], 1)

            def turn(m, q, p):
                pe.wait_ge(s["kqv_ready"], 2 * m + 2)
                for b in range(B):
                    te.transpose(bank[2][:, b * P:(b + 1) * P], kkq[:, q, b, p, 0:2].rearrange("p u i -> p (u i)"), k.ident[:])
                    mm = te.transpose(bank[2][:, (2 + b) * P:(3 + b) * P], vs[:, b, p].rearrange("p u i -> p (u i)"), k.ident[:])
                mm.then_inc(s["turned"], 1)

            def tiles(count, fn):
                for i in range(count):
                    for u in range(2):
                        mm = fn(i, u_half(u))
                return mm

            def ready():
                pe.wait_ge(s["started"], 1)

            def turn_u(m):
                before, this = in_register(pe, 5 * m + 1), in_register(pe, m + 1)
                ready()
                pe.wait_ge(s["ul_out"], before)
                pe.wait_ge(s["p_out"], before)
                pe.wait_ge(s["l_ready"], this)
                tiles(2 * B, lambda i, h: te.matmul(bank[4][h, i * P:i * P + C], rounds[h, 0, i, L_], k.ident[h, h],
                                                    start=True, stop=True)).then_inc(s["u_turned"], 1)

            def square_l(w):
                return tiles(2 * B, lambda j, h: te.matmul(bank[5][h, j * C:(j + 1) * C], rounds[h, w, j, U_], rounds[h, w, j, L_],
                                                           start=True, stop=True))

            def first_round(m):
                this = in_register(pe, m + 1)
                ready()
                pe.wait_ge(s["u_out"], this)
                tiles(2 * B, lambda j, h: te.matmul(bank[4][h, j * P:j * P + C], rounds[h, 0, j, L_], rounds[h, 0, j, U_],
                                                    start=True, stop=True))
                square_l(0).then_inc(s["squared"], 1)

            def next_round(m, i):
                w = (i - 1) % 2
                this, before, powers = (in_register(pe, x) for x in (m + 1, 5 * m + i, 5 * m + i - 1))
                ready()
                pe.wait_ge(s["ul_out"], before)
                if i == 2:
                    pe.wait_ge(s["p1_ready"], this)
                pe.wait_ge(s["p_out"], powers)
                if i < 5:
                    mm = tiles(2 * B, lambda j, h: te.matmul(bank[4][h, j * P:(j + 1) * P], rounds[h, w, j, L_], rounds[h, w, j, U_:],
                                                             start=True, stop=True))
                else:
                    mm = tiles(2 * B, lambda j, h: te.matmul(bank[4][h, j * P + C:(j + 1) * P], rounds[h, w, j, L_],
                                                             rounds[h, w, j, PROD], start=True, stop=True))
                mm.then_inc(s["powered"], 1)
                if i < 6:
                    square_l(w).then_inc(s["squared"], 1)

            def keys_state(st, slot):
                pe.wait_ge(s["s_updated"], st + 1)
                for b in range(B):
                    for u in range(2):
                        mm = te.matmul(bank[6][u_half(u), b * D:(b + 1) * D], kkq[:, slot // 2, b, slot % 2, 0], state[:, b, u], start=True, stop=True)
                mm.then_inc(s["ks_done"], 1)

            def values(st, n, slot):
                this, powers, cores = in_register(pe, st + 1), in_register(pe, 5 * n + 6), in_register(pe, st + 1)
                ready()
                pe.wait_ge(s["r_ready"], this)
                pe.wait_ge(s["p_out"], powers)
                pe.wait_ge(s["core_out"], cores)
                tiles(B, lambda b, h: te.matmul(bank[7][h, b * D:(b + 1) * D], inv[h, slot, b], r[h, b],
                                                start=True, stop=True)).then_inc(s["vt_done"], 1)

            def core(st, n, slot):
                pe.wait_ge(s["vt_out"], st + 1)
                pe.wait_ge(s["qg_ready"], n + 1)
                pe.wait_ge(s["attn_ready"], n + 1)
                for b in range(B):
                    for u in range(2):
                        te.matmul(bank[7][u_half(u), b * D:(b + 1) * D], qg[:, slot, b, u], state[:, b, u],
                                  start=True, stop=False, skip_group_check=True)
                    for u in range(2):
                        h = u_half(u)
                        mm = te.matmul(bank[7][h, b * D:(b + 1) * D], attnT[h, slot, b], vt[h, b],
                                       start=False, stop=True, skip_group_check=True)
                mm.then_inc(s["core_done"], 1)

            def grow(st, slot):
                pe.wait_ge(s["vb_out"], 2 * st + 2)
                pe.wait_ge(s["r_ready"], st + 1)
                for b in range(B):
                    for u, bk in ((0, 3), (1, 6)):
                        mm = te.matmul(bank[bk][:, b * D:(b + 1) * D], kdec[u_half(u), slot, b], vt[u_half(u), b], start=True, stop=True)
                        if b == B - 1:
                            mm.then_inc(s[f"grown_{u}"], 1)

            def turn_core(st, m):
                pe.wait_ge(s["core_out"], st + 2)
                pe.wait_ge(s["vb_out"], 4 * m + 4)
                pe.wait_ge(s["y_added"], st + 1)
                for b in range(B):
                    o = bank[2][:, 0:2 * P].rearrange("p (u b i) -> p u b i", u=2, b=B)[:, :, b]
                    mm = te.transpose(o, core_n[:, b], k.ident[:])
                mm.then_inc(s["core_turned"], 1)

            def project_out(st, pair):
                pe.wait_ge(s["w_out_in"], 16 * (pair + 1))
                pe.wait_ge(s["gated_out"], st + 1)
                for u in range(2):
                    mm = te.matmul(bank[2][:, 0:H], gated[:, u].rearrange("p b i -> p (b i)"), w_out[:, u],
                                   start=(u == 0), stop=(u == 1))
                mm.then_inc(s["y_projected"], 1)

            pe.wait_ge(s["started"], 1)
            pe.wait_ge(s["w_in"], 16)
            project(0, K_, 0, 0)
            project(0, Q_, 0, 1, "projected_kq")
            project(0, V_, 1, 0)
            project(0, V_ + 1, 1, 1, "projected_v")
            pe.wait_ge(s["raw_in"], 1)
            pe.wait_ge(s["w_z_in"], 16)
            project(0, Z_, 0, 0)
            project(0, Z_ + 1, 0, 1, "projected_z")
            sum_squares(0)
            gram(0, 0)
            turn(0, 0, 0)
            turn_u(0)
            pe.wait_ge(s["z_ready"], 1)
            project(1, K_, 0, 0)
            project(1, Q_, 0, 1, "projected_kq")
            first_round(0)
            pe.wait_ge(s["vb_out"], 2)
            turn(0, 0, 1)
            pe.wait_ge(s["ssq_out"], 1)
            project(1, V_, 1, 0)
            project(1, V_ + 1, 1, 1, "projected_v")
            for i in range(2, 7):
                next_round(0, i)
            sum_squares(1)

            def body(pair, rr, n, odd, crossing, last):
                m, q, st, slot = n + 1, 1 - odd, 2 * n, 2 * odd
                rr2 = rr + 2 - NB if crossing else rr + 2
                rr1 = 0 if last else rr + 1
                pe.wait_ge(s["s_updated"], st + 1)
                gram(m, q)
                keys_state(st, slot)
                pe.wait_ge(s["y_added"], st + 1)
                turn(m, q, 0)
                if crossing and not last:
                    pe.wait_ge(s["w_in"], 16 * (pair + 2))
                pe.wait_ge(s["z_ready"], n + 1)
                project(rr2, K_, 0, 0)
                values(st, n, slot)
                turn_u(m)
                project(rr2, Q_, 0, 1, "projected_kq")
                first_round(m)
                core(st, n, slot)
                pe.wait_ge(s["vb_out"], 4 * m + 2)
                turn(m, q, 1)
                next_round(m, 2)
                pe.wait_ge(s["attn_ready"], m + 1)
                grow(st, slot)
                pe.wait_ge(s["ssq_out"], n + 2)
                project(rr2, V_, 1, 0)
                next_round(m, 3)
                keys_state(st + 1, slot + 1)
                project(rr2, V_ + 1, 1, 1, "projected_v")
                next_round(m, 4)
                values(st + 1, n, slot + 1)
                turn_core(st, m)
                if last:
                    pe.wait_ge(s["w_z_in"], 16 * (pair + 2))
                pe.wait_ge(s["raw_in"], 2 * n + 5)
                project(rr1, Z_, 0, 0)
                next_round(m, 5)
                core(st + 1, n, slot + 1)
                grow(st + 1, slot + 1)
                project(rr1, Z_ + 1, 0, 1, "projected_z")
                project_out(st, pair)
                sum_squares(n + 2)
                turn_core(st + 1, m)
                next_round(m, 6)
                project_out(st + 1, pair)

            per_pair(pe, body)

        @block.scalar
        def _(act):
            a = nc.scalar

            def take_raw(m, i):
                pe_done = ("projected_kq", "projected_v")[i]
                act.wait_ge(s[pe_done], m + 1)
                act.wait_ge(s["hist_done"], m + 1)
                a.copy(raw[:, 2 * i:2 * i + 2, :, TAPS - 1:],
                       bank[i][:].rearrange("p (t b x) -> p t b x", t=2, b=B)).then_inc(s["raw_in"], 1)
                act.wait_ge(s["raw_in"], 2 * m + i + 1)
                for t in (2 * i, 2 * i + 1):
                    a.activation(conv[:, t], raw[:, t, :, 0:BLK], ACT.Copy, scale=conv_w[:, t, 0:1]).then_inc(s["tap_in"], 1)

            def tanh_conv(m, i):
                act.wait_ge(s["conv_steps"], 12 * m + 6 * i + 6)
                a.activation(th[:, 2 * i:2 * i + 2], conv[:, 2 * i:2 * i + 2], ACT.Tanh, scale=0.5).then_inc(s["conv_tanhed"], 1)

            def square_kq(m, q):
                act.wait_ge(s["kqv_ready"], 2 * m + 1)
                if not at_start(m):
                    act.wait_ge(s["ssq_summed"], m)
                mm = a.activation(sq[:], kkq[:, q].rearrange("p b s w i -> p (b s) w i")[:, :, 1:3], ACT.Square)
                mm.then_inc(s["kq_squared"], 1)

            def tanh_z(m):
                act.wait_ge(s["projected_z"], m + 1)
                a.activation(thz[:], bank[0][:], ACT.Tanh, scale=0.5).then_inc(s["z_tanhed"], 1)

            def decays(m):
                act.wait_ge(s["dec_args"], m + 1)
                if not at_start(m):
                    act.wait_ge(s["attn_ready"], m)
                a.activation(dec[:], dec_arg[:], ACT.Exp).then_inc(s["decayed"], 1)

            def token_major(m, q, p):
                act.wait_ge(s["turned"], 2 * m + p + 1)
                act.wait_ge(s["cols_ready"], m + 1)
                for b in range(B):
                    mm = a.activation(vb[:, 2 * q + p, b], bank[2][:, (2 + b) * P:(3 + b) * P], ACT.Copy, scale=v_scale[:, p, b:b + 1])
                mm.then_inc(s["vb_out"], 1)
                for b in range(B):
                    mm = a.activation(kdec[:, 2 * q + p, b], bank[2][:, b * P:(b + 1) * P], ACT.Copy, scale=k_tail[:, p, b:b + 1])
                mm.then_inc(s["vb_out"], 1)

            def take_u(m):
                act.wait_ge(s["u_turned"], m + 1)
                a.copy(rounds[:, 0, :, U_], bank[4][:].rearrange("p (b x) -> p b x", b=2 * B)[:, :, 0:C]).then_inc(s["u_out"], 1)

            def take_ul(m, i):
                act.wait_ge(s["squared"], 5 * m + i)
                if i == 2:
                    act.wait_ge(s["p1_ready"], m + 1)
                if i < 5:
                    a.copy(rounds[:, i % 2, :, U_], bank[4][:].rearrange("p (b x) -> p b x", b=2 * B)[:, :, 0:C]).then_inc(s["u_copied"], 1)
                mm = a.copy(rounds[:, i % 2, :, L_], bank[5][:, 0:2 * B * C].rearrange("p (b x) -> p b x", b=2 * B))
                mm.then_inc(s["ul_out"], 1)

            def take_values(st):
                act.wait_ge(s["vt_done"], st + 1)
                a.copy(vt[:].rearrange("p b d -> p (b d)"), bank[7][:, 0:B * D]).then_inc(s["vt_out"], 1)

            def core_squares(st):
                act.wait_ge(s["core_done"], st + 1)
                for b in range(B):
                    mm = a.activation(squares[:, b], bank[7][:, b * D:(b + 1) * D], ACT.Square, accum_out=core_ss[:, b:b + 1])
                    mm.then_inc(s["squares_out"], 1)

            def core_scaled(st):
                act.wait_ge(s["f_ready"], st + 2)
                for b in range(B):
                    mm = a.activation(core_n[:, b], bank[7][:, b * D:(b + 1) * D], ACT.Copy, scale=core_f[:, b:b + 1])
                mm.then_inc(s["core_out"], 1)

            act.wait_ge(s["conv_w_in"], 16)
            take_raw(0, 0)
            take_raw(0, 1)
            tanh_conv(0, 0)
            square_kq(0, 0)
            tanh_conv(0, 1)
            tanh_z(0)
            decays(0)
            take_u(0)
            token_major(0, 0, 0)
            take_raw(1, 0)
            take_ul(0, 1)
            token_major(0, 0, 1)
            take_raw(1, 1)
            for i in range(2, 6):
                take_ul(0, i)
            tanh_conv(1, 0)
            square_kq(1, 1)
            tanh_conv(1, 1)
            decays(1)

            def body(pair, rr, n, odd, crossing, last):
                m, q, st = n + 1, 1 - odd, 2 * n
                token_major(m, q, 0)
                take_u(m)
                take_values(st)
                take_ul(m, 1)
                core_squares(st)
                if crossing and not last:
                    act.wait_ge(s["conv_w_in"], 16 * (pair + 2))
                take_raw(n + 2, 0)
                take_ul(m, 2)
                token_major(m, q, 1)
                core_scaled(st)
                take_ul(m, 3)
                tanh_conv(n + 2, 0)
                take_ul(m, 4)
                take_raw(n + 2, 1)
                take_values(st + 1)
                take_ul(m, 5)
                square_kq(n + 2, odd)
                core_squares(st + 1)
                core_scaled(st + 1)
                tanh_conv(n + 2, 1)
                tanh_z(n + 1)
                decays(n + 2)

            per_pair(act, body)

        @block.vector
        def _(dve):
            v = nc.vector

            def convolve(m, t):
                dve.wait_ge(s["tap_in"], 4 * m + t + 1)
                for w in range(1, TAPS):
                    if w > 1:
                        dve.wait_ge(s["conv_steps"], 12 * m + 3 * t + w - 1)
                    v.scalar_tensor_tensor(out=conv[:, t], in0=raw[:, t, :, w:w + BLK], scalar=conv_w[:, t, w:w + 1],
                                           in1=conv[:, t], op0=ALU.mult, op1=ALU.add).then_inc(s["conv_steps"], 1)

            def silu(m, i, q):
                dve.wait_ge(s["conv_tanhed"], 2 * m + i + 1)
                by_step = lambda t: t.rearrange("p b (s i) -> p (b s) i", s=2)
                if i == 0:
                    if not isinstance(m, int):
                        dve.wait_ge(s["ks_done"], 2 * m - 2)
                    for w, t in ((0, K_), (1, K_), (2, Q_)):
                        mm = v.scalar_tensor_tensor(out=kkq[:, q].rearrange("p b s w i -> p (b s) w i")[:, :, w], in0=by_step(th[:, t]), scalar=1.0,
                                                    in1=by_step(conv[:, t]), op0=ALU.add, op1=ALU.mult)
                else:
                    if not at_start(m):
                        dve.wait_ge(s["turned"], 2 * m)
                    for u in range(2):
                        mm = v.scalar_tensor_tensor(out=vs[:].rearrange("p b s u i -> p (b s) u i")[:, :, u], in0=by_step(th[:, V_ + u]), scalar=1.0,
                                                    in1=by_step(conv[:, V_ + u]), op0=ALU.add, op1=ALU.mult)
                mm.then_inc(s["kqv_ready"], 1)

            def silu_z(m, q):
                dve.wait_ge(s["z_tanhed"], m + 1)
                v.scalar_tensor_tensor(out=zs[:, q].rearrange("p u b x -> p (u b x)"), in0=thz[:].rearrange("p u b x -> p (u b x)"),
                                       scalar=1.0, in1=bank[0][:], op0=ALU.add, op1=ALU.mult).then_inc(s["z_ready"], 1)

            def take_ssq(m):
                dve.wait_ge(s["ssq_summed"], m + 1)
                v.tensor_scalar(ssq[:].rearrange("p k s b -> p (k s b)"), bank[1][:, 0:4 * B], 4e-24, None,
                                ALU.max).then_inc(s["ssq_out"], 1)

            def make_l(m, q):
                dve.wait_ge(s["grammed"], m + 1)
                dve.wait_ge(s["cols_ready"], m + 1)
                dve.wait_ge(s["decayed"], m + 1)
                for p in range(2):
                    for b in range(B):
                        i = p * B + b
                        mm = v.scalar_tensor_tensor(out=rounds[:, 0, i, L_], in0=bank[3][:, i * P:i * P + C], scalar=l_scale[:, p, b:b + 1],
                                                    in1=dec[:, 0, p, b], op0=ALU.mult, op1=ALU.mult)
                mm.then_inc(s["l_ready"], 1)
                v.tensor_tensor(attnT[:, 2 * q:2 * q + 2].rearrange("p s b x -> p (s b) x"),
                                bank[3][:].rearrange("p (b x) -> p b x", b=2 * B)[:, :, C:],
                                dec[:, 1].rearrange("p s b x -> p (s b) x"), ALU.mult).then_inc(s["attn_ready"], 1)

            def take_p(m, i, q):
                dve.wait_ge(s["powered"], 5 * m + i - 1)
                if i < 5:
                    dve.wait_ge(s["u_copied"], 4 * m + i)
                out = inv[:, 2 * q:2 * q + 2].rearrange("p s b x -> p (s b) x") if i == 6 else rounds[:, i % 2, :, PROD]
                v.tensor_tensor(out, bank[4][:].rearrange("p (b x) -> p b x", b=2 * B)[:, :, C:], rounds[:, (i - 1) % 2, :, PROD],
                                ALU.add).then_inc(s["p_out"], 1)

            def make_r(st, slot):
                dve.wait_ge(s["ks_done"], st + 1)
                dve.wait_ge(s["vb_out"], 2 * st + 1)
                for b in range(B):
                    mm = v.scalar_tensor_tensor(out=r[:, b], in0=bank[6][:, b * D:(b + 1) * D], scalar=ks_scale[:, slot, b:b + 1],
                                                in1=vb[:, slot, b], op0=ALU.mult, op1=ALU.add)
                mm.then_inc(s["r_ready"], 1)

            def update(st, reset):
                dve.wait_ge(s["s_decayed"], st + 1)
                if reset:
                    for u in range(2):
                        dve.wait_ge(s[f"grown_{u}"], st + 1)
                    v.memset(state[:], 0.0).then_inc(s["s_updated"], 1)
                    return
                for u, bk in ((0, 3), (1, 6)):
                    dve.wait_ge(s[f"grown_{u}"], st + 1)
                    mm = v.tensor_tensor(state[:, :, u], bank[bk][:, 0:B * D].rearrange("p (b d) -> p b d", b=B),
                                         state_d[:, :, u], ALU.add)
                mm.then_inc(s["s_updated"], 1)

            def gate(st, odd, p):
                dve.wait_ge(s["core_turned"], st + 1)
                v.scalar_tensor_tensor(out=gated[:].rearrange("p u b i -> p (u b) i"),
                                       in0=bank[2][:, 0:2 * P].rearrange("p (q i) -> p q i", i=C), scalar=k.half_norm_w[:],
                                       in1=zs[:, odd, :, :, p * C:(p + 1) * C].rearrange("p u b i -> p (u b) i"),
                                       op0=ALU.mult, op1=ALU.mult).then_inc(s["gated_out"], 1)

            def add_y(st, chunk):
                dve.wait_ge(s["y_projected"], st + 1)
                y = k.y_sum[:, bass.ds(chunk, 1)].rearrange("p o h -> p (o h)")
                v.tensor_tensor(y, bank[2][:, 0:H], y, ALU.add).then_inc(s["y_added"], 1)

            v.memset(k.y_sum[:], 0.0)
            v.memset(state[:], 0.0).then_inc(s["s_updated"], 1)
            v.memset(credits[:, 4:5], 0.0).then_inc(s["y_added"], 1)
            v.memset(credits[:, 5:6], 0.0).then_inc(s["p_out"], 1)
            dve.wait_ge(s["conv_w_in"], 16)
            for t in range(4):
                convolve(0, t)
            silu(0, 0, 0)
            silu(0, 1, 0)
            silu_z(0, 0)
            take_ssq(0)
            make_l(0, 0)
            for t in range(4):
                convolve(1, t)
            for i in range(2, 7):
                take_p(0, i, 0)
            silu(1, 0, 1)
            silu(1, 1, 1)
            take_ssq(1)

            def body(pair, rr, n, odd, crossing, last):
                m, q, st, slot = n + 1, 1 - odd, 2 * n, 2 * odd
                make_r(st, slot)
                make_l(m, q)
                take_p(m, 2, q)
                convolve(n + 2, 0)
                update(st, False)
                take_p(m, 3, q)
                make_r(st + 1, slot + 1)
                convolve(n + 2, 1)
                take_p(m, 4, q)
                silu(n + 2, 0, odd)
                gate(st, odd, 0)
                convolve(n + 2, 2)
                take_p(m, 5, q)
                convolve(n + 2, 3)
                update(st + 1, last)
                add_y(st, 2 * rr)
                take_ssq(n + 2)
                gate(st + 1, odd, 1)
                take_p(m, 6, q)
                silu(n + 2, 1, odd)
                silu_z(n + 1, q)
                add_y(st + 1, 2 * rr + 1)

            per_pair(dve, body)

        @block.gpsimd
        def _(pool):
            g = nc.gpsimd

            def ready():
                pool.wait_ge(s["started"], 1)

            def history(m, reset):
                if not at_start(m):
                    taps = in_register(pool, 12 * m)
                    ready()
                    pool.wait_ge(s["conv_steps"], taps)
                if reset:
                    mm = g.memset(raw[:, :, :, 0:TAPS - 1], 0.0)
                else:
                    mm = g.tensor_copy(raw[:, :, :, 0:TAPS - 1], raw[:, :, :, BLK:])
                mm.then_inc(s["hist_done"], 1)

            def gate_differences(m):
                pool.wait_ge(s["g_in"], 32 * m + 32)
                for p in range(2):
                    col = k.g_col[:, bass.ds(2 * m + p, 1)].rearrange("p o b -> p (o b)")
                    mm = g.tensor_tensor(g_diff[:, p], g_blk[:, :, p * C:(p + 1) * C],
                                         col.unsqueeze(2).broadcast_to([P, B, C]), ALU.subtract)
                mm.then_inc(s["diffed"], 1)
                pool.wait_ge(s["diffed"], m + 1)
                if not at_start(m):
                    pool.wait_ge(s["decayed"], m)
                rows = g_diff[:].rearrange("p s b x -> p (s b) x")
                wide = [P, 2 * B, C]
                g.tensor_tensor(dec_arg[:, 0].rearrange("p s b x -> p (s b) x"), k.mask_l[:].unsqueeze(1).broadcast_to(wide), rows,
                                ALU.subtract)
                g.tensor_tensor(dec_arg[:, 1].rearrange("p s b x -> p (s b) x"), k.mask_u[:].unsqueeze(1).broadcast_to(wide), rows,
                                ALU.add).then_inc(s["dec_args"], 1)

            def norms(m):
                pool.wait_ge(s["ssq_out"], m + 1)
                g.tensor_tensor(rn[:].rearrange("p k s b -> p (k s b)"), ssq[:].rearrange("p k s b -> p (k s b)"),
                                k.pow_half[:], ALU.pow).then_inc(s["rn_ready"], 1)
                pool.wait_ge(s["rn_ready"], 2 * m + 1)
                g.tensor_tensor(rn2[:], rn[:, 0], rn[:, 0], ALU.mult).then_inc(s["rn_ready"], 1)

            def scales(m, q):
                pool.wait_ge(s["rn_ready"], 2 * m + 2)
                if not isinstance(m, int):
                    pool.wait_ge(s["f_ready"], 2 * m - 1)
                    pool.wait_ge(s["r_ready"], 2 * m - 2)
                if not at_start(m):
                    pool.wait_ge(s["vb_out"], 4 * m)
                    pool.wait_ge(s["l_ready"], m)
                two = slice(2 * q, 2 * q + 2)
                col = lambda t: t[:, bass.ds(2 * m, 2)]
                g.tensor_tensor(l_scale[:], rn2[:], col(k.minus_beta), ALU.mult)
                g.tensor_tensor(ks_scale[:, two], rn2[:], col(k.minus_beta_eg), ALU.mult)
                g.tensor_tensor(v_scale[:], rn[:, 0], col(k.half_beta), ALU.mult)
                g.tensor_copy(k_tail[:], col(k.tail_col))
                g.tensor_scalar(q_scale[:, two], rn[:, 1], D ** -0.5, None, ALU.mult).then_inc(s["q_steps"], 1)
                scaled, loaded = in_register(pool, m + 1), in_register(pool, 32 * m + 32)
                ready()
                pool.wait_ge(s["q_steps"], scaled)
                pool.wait_ge(s["e_in"], loaded)
                for p in range(2):
                    g.tensor_copy(s_dec[:, 2 * q + p], e_blk[:, :, :, p * C + C - 1].rearrange("p u b -> p b u"))
                g.tensor_tensor(q_scale2[:, two], q_scale[:, two], q_scale[:, two], ALU.mult).then_inc(s["cols_ready"], 1)

            def decay_queries(m, q):
                pool.wait_ge(s["e_in"], 32 * m + 32)
                if not isinstance(m, int):
                    pool.wait_ge(s["core_done"], 2 * m - 2)
                for p in range(2):
                    for b in range(B):
                        mm = g.tensor_tensor(qg[:, 2 * q + p, b], twice(kkq[:, q, b, p, 2]),
                                             e_blk[:, :, b, p * C:(p + 1) * C], ALU.mult)
                mm.then_inc(s["qg_ready"], 1)

            def first_product(m):
                pool.wait_ge(s["p_out"], 5 * m + 1)
                pool.wait_ge(s["u_out"], m + 1)
                mm = g.tensor_tensor(rounds[:, 1, :, PROD], rounds[:, 0, :, U_], k.ident_half[:].unsqueeze(1).broadcast_to([P, 2 * B, C]), ALU.add)
                mm.then_inc(s["p1_ready"], 1)

            def decay_state(st, n, slot):
                pool.wait_ge(s["s_updated"], st + 1)
                pool.wait_ge(s["cols_ready"], n + 1)
                f = lambda t: t[:].rearrange("p b u d -> p (b u) d")
                g.tensor_tensor(f(state_d), f(state), s_dec[:, slot].rearrange("p b u -> p (b u)").unsqueeze(2).broadcast_to([P, 2 * B, D]),
                                ALU.mult).then_inc(s["s_decayed"], 1)

            def rms_factor(st, slot):
                pool.wait_ge(s["squares_out"], 2 * st + 2)
                g.tensor_tensor(core_ms[:], core_ss[:], q_scale2[:, slot], ALU.mult).then_inc(s["f_steps"], 1)
                first = in_register(pool, 3 * st + 1)
                ready()
                pool.wait_ge(s["f_steps"], first)
                g.tensor_scalar(core_var[:], core_ms[:], 1.0 / D, EPS_RMS, ALU.mult, ALU.add).then_inc(s["f_steps"], 1)
                pool.wait_ge(s["f_steps"], 3 * st + 2)
                g.tensor_tensor(core_rs[:], core_var[:], k.pow_half[:, 0:B], ALU.pow).then_inc(s["f_steps"], 1)
                pool.wait_ge(s["f_steps"], 3 * st + 3)
                g.tensor_tensor(core_f[:], core_rs[:], q_scale[:, slot], ALU.mult).then_inc(s["f_ready"], 1)

            g.memset(credits[:, 0:1], 0.0).then_inc(s["f_ready"], 1)
            g.memset(credits[:, 1:2], 0.0).then_inc(s["ul_out"], 1)
            g.memset(credits[:, 2:3], 0.0).then_inc(s["core_out"], 1)
            g.memset(credits[:, 3:4], 0.0).then_inc(s["started"], 1)
            history(0, True)
            gate_differences(0)
            norms(0)
            scales(0, 0)
            decay_queries(0, 0)
            history(1, False)
            first_product(0)
            gate_differences(1)
            norms(1)
            scales(1, 1)

            def body(pair, rr, n, odd, crossing, last):
                m, q, st, slot = n + 1, 1 - odd, 2 * n, 2 * odd
                decay_state(st, n, slot)
                decay_queries(m, q)
                history(n + 2, crossing and not last)
                first_product(m)
                gate_differences(n + 2)
                rms_factor(st, slot)
                decay_state(st + 1, n, slot + 1)
                rms_factor(st + 1, slot + 1)
                norms(n + 2)
                scales(n + 2, odd)

            per_pair(pool, body)


class Kept:

    def __init__(self, ctx, nc):
        def sb(name, shape):
            return ctx.enter_context(nc.sbuf_tensor(name, shape, F32))

        self.x_tok = sb("x_tok", [P, NC, H])
        self.y_sum = sb("y_sum", [P, NC, H])
        self.xT = sb("xT", [P, KT, NC, B, C])
        self.ident = sb("ident", [P, P])
        self.ident_half = sb("ident_half", [P, C])
        self.ones_col = sb("ones_col", [P, 1])
        self.pow_half = sb("pow_half", [P, 4 * B])
        self.mask_l = sb("mask_l", [P, C])
        self.mask_u = sb("mask_u", [P, C])
        self.half_norm_w = sb("half_norm_w", [P, 1])
        self.g_col = sb("g_col", [P, NSTEPS + 4, B])
        self.tail_col = sb("tail_col", [P, NSTEPS + 4, B])
        self.half_beta = sb("half_beta", [P, NSTEPS + 4, B])
        self.minus_beta = sb("minus_beta", [P, NSTEPS + 4, B])
        self.minus_beta_eg = sb("minus_beta_eg", [P, NSTEPS + 4, B])
        self.token_rows = nc.dram_tensor("token_rows", (TOKENS, H + E), F32, kind="Internal").ap()
        self.tables = [nc.dram_tensor(f"table{t}", (TOKENS + CAP, H), F32, kind="Internal").ap() for t in range(NTAB)]
        self.slots = ctx.enter_context(nc.sbuf_tensor("slots", [CAP, E, 2], U32))
        self.g_rows = nc.dram_tensor("g_rows", (NK + 1, 2, NB, B, BLK), F32, kind="Internal").ap()
        self.e_rows = nc.dram_tensor("e_rows", (NK + 1, 2, NB, B, BLK), F32, kind="Internal").ap()


def by_token(rows):
    return rows[0:TOKENS].rearrange("(b c i) h -> b i c h", b=B, i=C)


def route(nc, io, k):
    with ExitStack() as ctx:
        def sb(name, shape, dt=F32):
            return ctx.enter_context(nc.sbuf_tensor(name, shape, dt))

        ps = [ctx.enter_context(nc.psum_tensor(f"route_bank{i}", [P, 512], F32)) for i in range(8)]
        rows = sb("rows", [P, NC, H + E])
        hn, weights = rows[:, :, 0:H], rows[:, :, H:]
        gate_w = sb("gate_w", [P, KT, E])
        bias = sb("bias", [P, E])
        per_expert = [P, NC, E]
        scores, biased, a_, b_, c_, sel, pos = (sb(n, per_expert) for n in ("scores", "biased", "work_a", "work_b", "work_c", "sel", "pos"))
        sel16 = sb("sel16", per_expert, F16)
        per_group = [P, NC, EG]
        m1, m2, cnt, gscore, rank = (sb(n, per_group) for n in ("m1", "m2", "cnt", "gscore", "rank"))
        before = sb("before", [P, EG, EG])
        resets = sb("resets", per_expert)
        top8 = sb("top8", [P, NC, 8])
        above, wsum, winv = sb("above", [P, NC]), sb("wsum", [P, NC]), sb("winv", [P, NC])
        earlier = sb("earlier", [P, NC + 1, E])
        tri16, halves16, cross16 = (sb(n, [P, P], F16) for n in ("tri16", "halves16", "cross16"))
        slot_no = sb("slot_no", [P, CAP, E], F16)
        place16 = sb("place16", per_expert, F16)
        onehot = sb("onehot", [P, 2, CAP, E], F16)
        token_no = sb("token_no", [P, NC])
        token16 = sb("token16", [P, NC], F16)
        found_row = sb("found_row", [1, CAP * E])
        found = sb("found", [CAP, E])
        empty, spare = sb("empty", [CAP, E]), sb("spare", [CAP, 1])
        wsg, wsu, wsd = sb("wsg", [P, KT, F]), sb("wsu", [P, KT, F]), sb("wsd", [F, H])
        sh_g = sb("sh_g", [F, 512])
        sh_h = sb("sh_h", [F, 2, 512])
        NSH = 4
        ln1, ln2 = LayerNorm(ctx, nc, "ln_attn"), LayerNorm(ctx, nc, "ln_mid")
        s = sems(ctx, nc, """loaded added consts consts_ready turned copied logits scored step top_done sel_ready counted 
            ranks_ready onehot_ready matched row_out spread rows_ready rows_out sh_up sh_silu sh_hidden sh_down sh_out """)
        rows_of = lambda ap: ap.rearrange("p c e -> p (c e)")
        by_group = lambda ap: ap.rearrange("p c (g e) -> p (c g) e", g=EG)
        wide = [P, NC * EG, E // EG]

        block = ctx.enter_context(nc.Block())

        @block.sync
        def _(sp):
            sp.dma_start(gate_w[:], io["gate_w"]).then_inc(s["loaded"], 16)
            sp.dma_start(bias[:], io["bias"].partition_broadcast(P)).then_inc(s["loaded"], 16)
            for dst, src in ((wsg, "ws_gate"), (wsu, "ws_up"), (wsd, "ws_down")):
                sp.dma_start(dst[:], io[src]).then_inc(s["loaded"], 16)
            sp.wait_ge(s["rows_ready"], 1)
            sp.wait_ge(ln2.sem("done"), GROUPS)
            for b in range(B):
                sp.dma_start(by_token(k.token_rows)[b], rows[u_half(b)]).then_inc(s["rows_out"], 16)
            sp.wait_ge(s["row_out"], 6)
            sp.dma_start(found[:], found_row[:].rearrange("o (s e) -> o s e", e=E)).then_inc(s["spread"], 16)
            sp.wait_ge(s["rows_out"], 32)

        @block.gpsimd
        def _(pool):
            g = nc.gpsimd
            done = [0]

            def one(ins):
                ins.then_inc(s["consts"], 1)
                done[0] += 1
                pool.wait_ge(s["consts"], done[0])

            one(g.memset(tri16[:], 1.0))
            one(g.affine_select(out=tri16[:], in_=tri16[:], compare_op=ALU.is_gt, fill=0.0, base=0, pattern=[[1, P]],
                                channel_multiplier=-1))
            one(g.memset(tri16[0:C, C:P], 0.0))
            one(g.memset(halves16[:], 0.0))
            one(g.memset(halves16[0:C, 0:C], 1.0))
            one(g.memset(halves16[C:P, C:P], 1.0))
            one(g.memset(cross16[:], 0.0))
            one(g.memset(cross16[0:C, C:P], 1.0))
            one(g.memset(before[:], 1.0))
            one(g.affine_select(out=before[:], in_=before[:], compare_op=ALU.is_gt, fill=0.0, base=0, pattern=[[1, EG], [-1, EG]],
                                channel_multiplier=0))
            one(g.memset(resets[:], 1.0))
            one(g.memset(resets[:, :, 0:1], 0.0))
            one(g.iota(slot_no[:], pattern=[[1, CAP], [0, E]], base=0, channel_multiplier=0, allow_small_or_imprecise_dtypes=True))
            for b in range(B):
                one(g.iota(token_no[u_half(b)], pattern=[[C, NC]], base=1 + b * S, channel_multiplier=1,
                           allow_small_or_imprecise_dtypes=True))
            one(g.tensor_copy(token16[:], token_no[:]))
            one(g.iota(spare[:], pattern=[[0, 1]], base=TOKENS, channel_multiplier=1, allow_small_or_imprecise_dtypes=True))
            g.memset(earlier[:, 0:1], 0.0).then_inc(s["consts_ready"], 1)
            ln1.gpsimd(pool)
            ln2.gpsimd(pool)

        @block.scalar
        def _(act):
            a = nc.scalar
            ln1.scalar(act, hn)
            ln2.scalar(act, hn)
            for c in range(NC):
                act.wait_ge(s["turned"], c + 1)
                a.copy(k.xT[:, :, c], ps[c % 2][:, 0:KT * P].rearrange("p (k b i) -> p k b i", k=KT, b=B)).then_inc(s["copied"], 1)
            act.wait_ge(s["logits"], 1)
            for i in range(2):
                mm = a.activation(scores[:, i * 8:(i + 1) * 8], ps[2 + i][:].rearrange("p (c e) -> p c e", e=E), ACT.Sigmoid)
            mm.then_inc(s["scored"], 1)
            for q in range(NSH):
                act.wait_ge(s["sh_up"], q + 1)
                if q >= 1:
                    act.wait_ge(s["sh_hidden"], q)
                a.activation(sh_g[:], ps[4 + 2 * (q % 2)][0:F, :], ACT.Silu).then_inc(s["sh_silu"], 1)
                for c in range(4):
                    n = 4 * q + c
                    act.wait_ge(s["sh_down"], n + 1)
                    a.copy(k.y_sum[:, n], ps[n % 2][:, 0:H]).then_inc(s["sh_out"], 1)

        @block.tensor
        def _(pe):
            te = nc.tensor
            for c in range(NC):
                if c >= 2:
                    pe.wait_ge(s["copied"], c - 1)
                pe.wait_ge(ln2.sem("done"), c // GC + 1)
                for kt in range(KT):
                    mm = te.transpose(ps[c % 2][:, kt * P:(kt + 1) * P], hn[:, c, kt * P:(kt + 1) * P], k.ident[:])
                mm.then_inc(s["turned"], 1)
            pe.wait_ge(s["copied"], NC)
            pe.wait_ge(s["loaded"], 16 * 5)
            for c in range(NC):
                for kt in range(KT):
                    mm = te.matmul(ps[2 + c // 8][:, (c % 8) * E:(c % 8 + 1) * E], k.xT[:, kt, c].rearrange("p b i -> p (b i)"),
                                   gate_w[:, kt], start=(kt == 0), stop=(kt == KT - 1))
            mm.then_inc(s["logits"], 1)
            for q in range(NSH):
                if q >= 2:
                    pe.wait_ge(s["sh_hidden"], q - 1)
                for g, w in enumerate((wsg, wsu)):
                    for kt in range(KT):
                        mm = te.matmul(ps[4 + 2 * (q % 2) + g][0:F, :], w[:, kt], k.xT[:, kt, 4 * q:4 * q + 4].rearrange("p c b i -> p (c b i)"),
                                       start=(kt == 0), stop=(kt == KT - 1))
                mm.then_inc(s["sh_up"], 1)
                pe.wait_ge(s["sh_hidden"], q + 1)
                for c in range(4):
                    n = 4 * q + c
                    if n >= 2:
                        pe.wait_ge(s["sh_out"], n - 1)
                    te.matmul(ps[n % 2][:, 0:H], sh_h[:, q % 2, c * P:(c + 1) * P], wsd[:], start=True, stop=True).then_inc(s["sh_down"], 1)
            pe.wait_ge(s["sh_out"], NC)
            pe.wait_ge(s["sel_ready"], 1)
            pe.wait_ge(s["consts_ready"], 1)
            for i in range(2):
                r16 = rows_of(sel16[:])[:, i * 512:(i + 1) * 512]
                te.matmul(ps[4 + i][:], tri16[:], r16, start=True, stop=True)
                te.matmul(ps[6 + i][:], halves16[:], r16, start=True, stop=True)
            for c in range(NC):
                mm = te.matmul(ps[0][:, 0:E], cross16[:], sel16[:, c], start=(c == 0), stop=(c == NC - 1))
            mm.then_inc(s["counted"], 1)
            pe.wait_ge(s["ranks_ready"], 1)
            for c in range(NC):
                pe.wait_ge(s["onehot_ready"], c + 1)
                flat = onehot[:, c % 2].rearrange("p s e -> p (s e)")
                for q in range(6):
                    mm = te.matmul(ps[q][0:1, :], token16[:, c:c + 1], flat[:, q * 512:(q + 1) * 512], start=(c == 0), stop=(c == NC - 1))
                mm.then_inc(s["matched"], 1)

        @block.vector
        def _(dve):
            v = nc.vector
            done = [0]

            def one(ins):
                ins.then_inc(s["step"], 1)
                done[0] += 1
                dve.wait_ge(s["step"], done[0])

            def shared_hidden(q):
                dve.wait_ge(s["sh_silu"], q + 1)
                if q >= 2:
                    dve.wait_ge(s["sh_down"], 4 * (q - 1))
                v.tensor_tensor(sh_h[:, q % 2], ps[4 + 2 * (q % 2) + 1][0:F, :], sh_g[:], ALU.mult).then_inc(s["sh_hidden"], 1)

            ln1.vector(dve, k.y_sum, hn)
            for g in range(GROUPS):
                a = slice(g * GC, (g + 1) * GC)
                dve.wait_ge(ln1.sem("done"), g + 1)
                v.tensor_tensor(k.x_tok[:, a], k.x_tok[:, a], hn[:, a], ALU.add).then_inc(s["added"], 1)
            ln2.vector(dve, k.x_tok, hn, lambda g: dve.wait_ge(s["added"], g + 1))
            dve.wait_ge(s["loaded"], 16 * 5)
            dve.wait_ge(s["scored"], 1)
            dve.wait_ge(s["consts_ready"], 1)
            one(v.tensor_tensor(biased[:], scores[:], bias[:].unsqueeze(1).broadcast_to(per_expert), ALU.add))
            gflat = lambda ap: ap.rearrange("p c g -> p (c g)")
            over = lambda ap: gflat(ap).unsqueeze(2).broadcast_to(wide)
            one(v.tensor_reduce(gflat(m1[:]), by_group(biased[:]), AX.X, ALU.max))
            one(v.tensor_tensor(by_group(a_[:]), by_group(biased[:]), over(m1[:]), ALU.is_equal))
            one(v.tensor_reduce(gflat(cnt[:]), by_group(a_[:]), AX.X, ALU.add))
            one(v.scalar_tensor_tensor(out=rows_of(b_[:]), in0=rows_of(a_[:]), scalar=NEG, in1=rows_of(biased[:]), op0=ALU.mult, op1=ALU.add))
            one(v.tensor_reduce(gflat(m2[:]), by_group(b_[:]), AX.X, ALU.max))
            one(v.tensor_scalar(cnt[:], cnt[:], 2.0, -2.0 * NEG, ALU.is_ge, ALU.mult))
            one(v.tensor_scalar(cnt[:], cnt[:], NEG, None, ALU.add))
            one(v.tensor_tensor(cnt[:], cnt[:], m1[:], ALU.min))
            one(v.tensor_tensor(m2[:], m2[:], cnt[:], ALU.max))
            one(v.tensor_tensor(gscore[:], m1[:], m2[:], ALU.add))
            shared_hidden(0)
            pairs = [P, NC, EG, EG]
            as_pairs = lambda ap: ap.rearrange("p c (g h) -> p c g h", g=EG)
            other, own = gscore[:].unsqueeze(2).broadcast_to(pairs), gscore[:].unsqueeze(3).broadcast_to(pairs)
            one(v.tensor_tensor(as_pairs(a_[:]), other, own, ALU.is_gt))
            one(v.tensor_tensor(as_pairs(b_[:]), other, own, ALU.is_equal))
            one(v.tensor_tensor(b_[:], b_[:], before[:].rearrange("p g h -> p (g h)").unsqueeze(1).broadcast_to(per_expert), ALU.mult))
            one(v.tensor_tensor(a_[:], a_[:], b_[:], ALU.add))
            one(v.tensor_reduce(gflat(rank[:]), a_[:].rearrange("p c (g h) -> p (c g) h", g=EG), AX.X, ALU.add))
            one(v.tensor_scalar(rank[:], rank[:], float(KG), NEG, ALU.is_ge, ALU.mult))
            shared_hidden(1)
            one(v.tensor_tensor(by_group(c_[:]), by_group(biased[:]), over(rank[:]), ALU.add))
            for c in range(NC):
                v.max(out=top8[:, c], in_=c_[:, c]).then_inc(s["top_done"], 1)
            dve.wait_ge(s["top_done"], NC)
            shared_hidden(2)
            least = top8[:, :, TOP - 1:TOP].broadcast_to(per_expert)
            one(v.tensor_tensor(a_[:], c_[:], least, ALU.is_gt))
            one(v.tensor_tensor(b_[:], c_[:], least, ALU.is_equal))
            one(v.tensor_reduce(above[:], a_[:], AX.X, ALU.add))
            one(v.tensor_tensor_scan(rows_of(c_[:]), rows_of(resets[:]), rows_of(b_[:]), 0.0, ALU.mult, ALU.add))
            one(v.tensor_tensor(c_[:], c_[:], above[:].unsqueeze(2).broadcast_to(per_expert), ALU.add))
            one(v.scalar_tensor_tensor(out=rows_of(b_[:]), in0=rows_of(c_[:]), scalar=float(TOP), in1=rows_of(b_[:]), op0=ALU.is_le, op1=ALU.mult))
            one(v.tensor_tensor(sel[:], a_[:], b_[:], ALU.add))
            v.tensor_copy(sel16[:], sel[:]).then_inc(s["sel_ready"], 1)
            one(v.tensor_tensor(c_[:], scores[:], sel[:], ALU.mult))
            shared_hidden(3)
            one(v.tensor_reduce(wsum[:], c_[:], AX.X, ALU.add))
            one(v.reciprocal(winv[:], wsum[:]))
            one(v.tensor_tensor(c_[:], c_[:], winv[:].unsqueeze(2).broadcast_to(per_expert), ALU.mult))
            v.tensor_scalar(weights, c_[:], ROUTE_SCALE, None, ALU.mult).then_inc(s["rows_ready"], 1)
            dve.wait_ge(s["counted"], 1)
            one(v.tensor_copy(earlier[:, 0], ps[0][:, 0:E]))
            for c in range(NC):
                one(v.tensor_tensor(earlier[:, c + 1], ps[6 + c // 8][:, (c % 8) * E:(c % 8 + 1) * E], earlier[:, c], ALU.add))
            for i in range(2):
                a8 = slice(i * 8, (i + 1) * 8)
                mm = v.tensor_tensor(pos[:, a8], ps[4 + i][:].rearrange("p (c e) -> p c e", e=E), earlier[:, a8], ALU.add)
                one(mm)
            one(v.tensor_scalar(b_[:], sel[:], -2.0 * CAP, 2.0 * CAP, ALU.mult, ALU.add))
            v.tensor_tensor(place16[:], pos[:], b_[:], ALU.add).then_inc(s["ranks_ready"], 1)
            dve.wait_ge(s["ranks_ready"], 1)
            for c in range(NC):
                if c >= 2:
                    dve.wait_ge(s["matched"], c - 1)
                v.tensor_tensor(onehot[:, c % 2], place16[:, c].unsqueeze(1).broadcast_to([P, CAP, E]), slot_no[:], ALU.is_equal).then_inc(s["onehot_ready"], 1)
            dve.wait_ge(s["matched"], NC)
            for q in range(6):
                v.tensor_copy(found_row[:, q * 512:(q + 1) * 512], ps[q][0:1, :]).then_inc(s["row_out"], 1)
            dve.wait_ge(s["spread"], 16)
            one(v.tensor_scalar(k.slots[:, :, 0], found[:], -1.0, 0.0, ALU.add, ALU.max))
            one(v.tensor_scalar(spare[:], spare[:], 1.0, None, ALU.add))
            one(v.tensor_scalar(empty[:], found[:], 0.0, spare[:], ALU.is_equal, ALU.mult))
            one(v.scalar_tensor_tensor(out=k.slots[:, :, 1], in0=found[:], scalar=-1.0, in1=empty[:], op0=ALU.add, op1=ALU.add))


def experts(nc, io, k):
    with ExitStack() as ctx:
        def sb(name, shape, dt=F32):
            return ctx.enter_context(nc.sbuf_tensor(name, shape, dt))

        ps = [ctx.enter_context(nc.psum_tensor(f"moe_bank{i}", [P, 512], F32)) for i in range(8)]
        w_in = sb("w_gate_up", [P, 2, NTAB, 2, KT, F])
        w_down = sb("w_down", [F, 2, NTAB, H])
        at = sb("slot_rows", [CAP, 4, NTAB, 2], U32)
        xg = sb("gathered", [CAP, 4, NTAB, H + E])
        xgT = sb("gatheredT", [P, 2, NTAB, KT, CAP])
        act_g = sb("act_g", [F, NTAB * CAP])
        hidden = sb("hidden", [F, 2, NTAB * CAP])
        scaled = sb("scaled", [CAP, 4, NTAB, H])
        credit = sb("credit", [1, 1])
        s = sems(ctx, nc, "pool_started located " +
                 "turned turn_out upped silued multiplied downed weighted w_in_0 w_in_1 gathered_0 gathered_1 gathered_2 gathered_3 " +
                 " ".join(f"added_{t}" for t in range(NTAB)))
        FOURS = E // NTAB

        block = ctx.enter_context(nc.Block())

        @block.sync
        def _(sp):
            def load(q, h):
                four = bass.ds(q * NTAB, NTAB)
                for t in range(NTAB):
                    sp.dma_start(w_in[:, h, t], io["w_gate_up"][bass.ds(q * NTAB + t, 1)].rearrange("o p g k f -> (o p) g k f")).then_inc(s[f"w_in_{h}"], 16)
                sp.dma_start(w_down[:, h], io["w_down"][four].rearrange("e f h -> f e h")).then_inc(s[f"w_in_{h}"], 16)

            for h in range(2):
                load(h, h)
            with sp.Fori(0, FOURS // 2 - 1) as r:
                for h in range(2):
                    sp.wait_ge(s["downed"], 2 * r + h + 1)
                    load(2 * r + 2 + h, h)
            for h in range(2):
                sp.wait_ge(s[f"w_in_{h}"], 16 * (NTAB + 1) * (FOURS // 2))

        @block.gpsimd
        def _(pool):
            g = nc.gpsimd

            def gather(q, w):
                if not (isinstance(q, int) and q < 4):
                    used = in_register(pool, q - 3)
                    pool.wait_ge(s["pool_started"], 1)
                    pool.wait_ge(s["weighted"], used)
                g.tensor_copy(at[:, w], k.slots[:, bass.ds(q * NTAB, NTAB)]).then_inc(s["located"], 1)
                made = in_register(pool, q + 1)
                pool.wait_ge(s["pool_started"], 1)
                pool.wait_ge(s["located"], made)
                for t in range(NTAB):
                    g.indirect_dma_start(xg[:, w, t], None, k.token_rows, bass.IndirectOffsetOnAxis(ap=at[:, w, t, 0:1], axis=0),
                                         bounds_check=TOKENS - 1, oob_is_err=True).then_inc(s[f"gathered_{w}"], 16)

            def add(q, w):
                done = in_register(pool, q + 1)
                if not (isinstance(q, int) and q == 0):
                    landed = in_register(pool, 16 * q)
                    pool.wait_ge(s["pool_started"], 1)
                    for t in range(NTAB):
                        pool.wait_ge(s[f"added_{t}"], landed)
                else:
                    pool.wait_ge(s["pool_started"], 1)
                pool.wait_ge(s["weighted"], done)
                for t in range(NTAB):
                    g.indirect_dma_start(k.tables[t], bass.IndirectOffsetOnAxis(ap=at[:, w, t, 1:2], axis=0), scaled[:, w, t], None,
                                         bounds_check=TOKENS + CAP - 1, oob_is_err=True, compute_op=ALU.add).then_inc(s[f"added_{t}"], 16)

            g.memset(credit[:], 0.0).then_inc(s["pool_started"], 1)
            for q in range(3):
                gather(q, q)
            gather(3, 3)
            add(0, 0)
            with pool.Fori(1, FOURS // 4) as r:
                for w in range(4):
                    add(4 * r + w - 3, (w + 1) % 4)
                    gather(4 * r + w, w)
            for q in range(FOURS - 3, FOURS):
                add(q, q % 4)
            for t in range(NTAB):
                pool.wait_ge(s[f"added_{t}"], 16 * FOURS)

        def per_four(eng, body):
            with eng.Fori(0, FOURS // 2) as r:
                for h in range(2):
                    body(2 * r + h, r, h)

        @block.tensor
        def _(pe):
            te = nc.tensor

            def turn(r, w):
                h = w % 2
                landed = in_register(pe, 16 * NTAB * (r + 1))
                pe.wait_ge(s["pool_started"], 1)
                pe.wait_ge(s[f"gathered_{w}"], landed)
                for t in range(NTAB):
                    for kt in range(KT):
                        i = (t * KT + kt) * CAP
                        mm = te.transpose(ps[h][:, i:i + CAP], xg[:, w, t, kt * P:(kt + 1) * P], k.ident[0:CAP, 0:CAP])
                mm.then_inc(s["turned"], 1)

            def body(q, r, w, last=False):
                h, r2 = w % 2, 2 * r + w // 2
                pe.wait_ge(s[f"w_in_{h}"], 16 * (NTAB + 1) * (r2 + 1))
                pe.wait_ge(s["turn_out"], q + 1)
                for g in range(2):
                    for t in range(NTAB):
                        i = (g * NTAB + t) * CAP
                        for kt in range(KT):
                            mm = te.matmul(ps[2 + h][0:F, i:i + CAP], w_in[:, h, t, g, kt], xgT[:, h, t, kt],
                                           start=(kt == 0), stop=(kt == KT - 1))
                mm.then_inc(s["upped"], 1)
                if not last:
                    turn(r + w // 3, (w + 1) % 4)
                pe.wait_ge(s["multiplied"], q + 1)
                for t in range(NTAB):
                    mm = te.matmul(ps[4 + 2 * h + t // 2][0:CAP, (t % 2) * H:(t % 2 + 1) * H], hidden[:, h, t * CAP:(t + 1) * CAP],
                                   w_down[:, h, t], start=True, stop=True)
                mm.then_inc(s["downed"], 1)

            turn(0, 0)
            with pe.Fori(0, FOURS // 4 - 1) as r:
                for w in range(4):
                    body(4 * r + w, r, w)
            for w in range(4):
                body(FOURS - 4 + w, FOURS // 4 - 1, w, w == 3)

        @block.scalar
        def _(act):
            a = nc.scalar

            def body(q, r, h):
                act.wait_ge(s["turned"], q + 1)
                a.copy(xgT[:, h].rearrange("p t k s -> p (t k s)"), ps[h][:, 0:NTAB * KT * CAP]).then_inc(s["turn_out"], 1)
                act.wait_ge(s["upped"], q + 1)
                a.activation(act_g[:], ps[2 + h][0:F, 0:NTAB * CAP], ACT.Silu).then_inc(s["silued"], 1)

            per_four(act, body)

        @block.vector
        def _(dve):
            v = nc.vector

            def body(q, w):
                h = w % 2
                dve.wait_ge(s["silued"], q + 1)
                v.tensor_tensor(hidden[:, h], ps[2 + h][0:F, NTAB * CAP:2 * NTAB * CAP], act_g[:], ALU.mult).then_inc(s["multiplied"], 1)
                dve.wait_ge(s["downed"], q + 1)
                for t in range(NTAB):
                    mm = v.tensor_scalar(scaled[:, w, t], ps[4 + 2 * h + t // 2][0:CAP, (t % 2) * H:(t % 2 + 1) * H],
                                         xg[:, w, t, bass.ds(H + q * NTAB + t, 1)], None, ALU.mult)
                mm.then_inc(s["weighted"], 1)

            with dve.Fori(0, FOURS // 4) as r:
                for w in range(4):
                    body(4 * r + w, w)


def combine(nc, io, k, out):
    with ExitStack() as ctx:
        def sb(name, shape, dt=F32):
            return ctx.enter_context(nc.sbuf_tensor(name, shape, dt))

        part = [sb(f"part{t}", [P, NC, H]) for t in range(NTAB)]
        ln = LayerNorm(ctx, nc, "ln_out")
        s = sems(ctx, nc, "paired sums out_ready stored " + " ".join(f"parts_in_{g}" for g in range(GROUPS)))
        block = ctx.enter_context(nc.Block())
        groups = [slice(g * GC, (g + 1) * GC) for g in range(GROUPS)]

        @block.sync
        def _(sp):
            for g, a in enumerate(groups):
                for t in range(NTAB):
                    for b in range(B):
                        sp.dma_start(part[t][u_half(b), a], by_token(k.tables[t])[b][:, a]).then_inc(s[f"parts_in_{g}"], 16)
            for g, a in enumerate(groups):
                sp.wait_ge(s["out_ready"], g + 1)
                for b in range(B):
                    sp.dma_start(out[b].rearrange("(c i) h -> i c h", i=C)[:, a], part[0][u_half(b), a]).then_inc(s["stored"], 16)
            sp.wait_ge(s["stored"], 16 * B * GROUPS)

        @block.gpsimd
        def _(pool):
            def add_pair(g):
                a = groups[g]
                pool.wait_ge(s[f"parts_in_{g}"], 16 * B * NTAB)
                nc.gpsimd.tensor_tensor(part[2][:, a], part[2][:, a], part[3][:, a], ALU.add).then_inc(s["paired"], 1)

            add_pair(0)
            add_pair(1)
            ln.gpsimd(pool, lambda g: add_pair(g + 2) if g + 2 < GROUPS else None)

        @block.scalar
        def _(act):
            ln.scalar(act, part[0])

        @block.vector
        def _(dve):
            v = nc.vector

            def add_parts(g):
                a = groups[g]
                dve.wait_ge(s[f"parts_in_{g}"], 16 * B * NTAB)
                v.tensor_tensor(part[1][:, a], part[1][:, a], part[0][:, a], ALU.add).then_inc(s["sums"], 1)
                dve.wait_ge(s["paired"], g + 1)
                v.tensor_tensor(k.y_sum[:, a], k.y_sum[:, a], part[2][:, a], ALU.add).then_inc(s["sums"], 1)
                dve.wait_ge(s["sums"], 3 * g + 2)
                v.tensor_tensor(k.y_sum[:, a], k.y_sum[:, a], part[1][:, a], ALU.add).then_inc(s["sums"], 1)
                dve.wait_ge(s["sums"], 3 * g + 3)

            def add_input(g):
                a = groups[g]
                dve.wait_ge(ln.sem("done"), g + 1)
                v.tensor_tensor(part[0][:, a], part[0][:, a], k.x_tok[:, a], ALU.add).then_inc(s["out_ready"], 1)

            ln.vector(dve, k.y_sum, part[0], add_parts, add_input, lag=2)


def build(nc, io, out):
    with ExitStack() as ctx:
        k = Kept(ctx, nc)
        setup(nc, io, k)
        delta_rule(nc, io, k, NK)
        route(nc, io, k)
        experts(nc, io, k)
        combine(nc, io, k, out)


def laid_out(v):
    import numpy as np

    qkv, z = v["L0_attn_W_qkv"], v["L0_attn_W_z"]
    key_dim = NK * D

    def tiles_of(pair):
        rows = [qkv, qkv] + [qkv] * 2 + [z] * 2
        first = [key_dim + pair * D, pair * D] + [2 * key_dim + (2 * pair + u) * D for u in range(2)] + [(2 * pair + u) * D for u in range(2)]
        return rows, first

    w_proj, conv_w, w_out = [], [], []
    for pair in [*range(NK), NK - 1]:
        rows, first = tiles_of(pair)
        w_proj.append(np.stack([w[a:a + D] for w, a in zip(rows, first)]).reshape(NT, D, KT, P).transpose(3, 2, 0, 1))
        conv_w.append(np.stack([v["L0_attn_conv_w"][a:a + D] for a in first[:4]], axis=1))
        w_out.append(v["L0_attn_W_out"][:, 2 * pair * D:(2 * pair + 2) * D].reshape(H, 2, D).transpose(2, 1, 0))
    kfirst = lambda w: w.reshape(KT, P, w.shape[-1]).transpose(1, 0, 2)
    gate_up = np.stack([v["L0_ffn_w_gate"], v["L0_ffn_w_up"]], axis=1)
    return {
        "x": v["L0_attn_x"], "w_proj": np.stack(w_proj), "conv_w": np.stack(conv_w), "w_out": np.stack(w_out),
        "w_ba": np.concatenate([v["L0_attn_W_b"], v["L0_attn_W_a"]]).reshape(2 * NV, KT, P).transpose(2, 1, 0),
        "dt_bias": v["L0_attn_dt_bias"], "A_log": v["L0_attn_A_log"], "norm_w": v["L0_attn_norm_w"].reshape(D, 1),
        "gate_w": kfirst(v["L0_ffn_gate_w"]), "bias": v["L0_ffn_bias"],
        "w_gate_up": gate_up.reshape(E, 2, KT, P, F).transpose(0, 3, 1, 2, 4), "w_down": v["L0_ffn_w_down"],
        "ws_gate": kfirst(v["L0_ffn_ws_gate"]), "ws_up": kfirst(v["L0_ffn_ws_up"]), "ws_down": v["L0_ffn_ws_down"],
    }


def kernel(**inputs):
    import numpy as np
    import concourse.bacc as bacc
    from concourse.bass_utils import run_bass_kernel_spmd

    nc = bacc.Bacc("TRN2", target_bir_lowering=False, num_devices=1)
    arrays, io = {}, {}
    for name, a in laid_out({n: np.asarray(a) for n, a in inputs.items()}).items():
        arrays[f"in_{name}"] = np.ascontiguousarray(a)
        io[name] = nc.dram_tensor(f"in_{name}", a.shape, mybir.dt.from_np(a.dtype), kind="ExternalInput").ap()
    out = nc.dram_tensor("out", (B, S, H), F32, kind="ExternalOutput").ap()
    build(nc, io, out)
    got = run_bass_kernel_spmd(nc, [arrays], core_ids=[0])
    return got.results[0]["out"]
```
